# Optimizing a Trainium2 kernel written in Bass

```python
import numpy as np
import jax
import jax.numpy as jnp

def _softmax(x, axis=-1):
    return jax.nn.softmax(x, axis=axis)

def _gelu(x):
    return jax.nn.gelu(x, approximate=True)

def _silu(x):
    return jax.nn.silu(x)

def _sigmoid(x):
    return jax.nn.sigmoid(x)

def _layernorm(x, axis=-1, eps=1e-05):
    m = jnp.mean(x, axis=axis, keepdims=True)
    v = jnp.var(x, axis=axis, keepdims=True)
    return (x - m) / jnp.sqrt(v + eps)

def _scatter_add(tgt, idx, src, axis=0):
    return tgt.at[idx].add(src)

def _segment_sum(src, seg, n):
    return jax.ops.segment_sum(src, seg, n)
kernel_name = 'mk_xattn_ffn_d4_seqx_r8_b66512'

def setup_inputs(seed: int=0):
    np.random.seed(seed)
    _w = jnp.asarray

    def _rec_inputs():
        import jax
        import jax.numpy as jnp
        _rk = jax.random.key(seed)
        x = -0.0002928 + 1 * jax.random.normal(jax.random.fold_in(_rk, 1), (8, 256, 128), jnp.float32)
        _lenS = 256 - jax.random.randint(jax.random.fold_in(_rk, 7), (8,), 0, max(1, 256 // 4) + 1, jnp.int32)
        _lenS2 = 64 - jax.random.randint(jax.random.fold_in(_rk, 8), (8,), 0, max(1, 64 // 4) + 1, jnp.int32)
        _ctx_1024P = jax.random.normal(jax.random.fold_in(_rk, 11), (8, 16, 128), jnp.float32)
        _ctx_1024c = jax.random.dirichlet(jax.random.fold_in(_rk, 511), 0.3 * jnp.ones((16,), jnp.float32), (8, 64))
        _ctx_1024t = jnp.einsum('bsk,bkd->bsd', _ctx_1024c, _ctx_1024P)
        _ctx_1024t = _ctx_1024t * jax.lax.rsqrt(jnp.mean(jnp.square(_ctx_1024t)) + 1e-12) * 0.953939
        ctx_1024 = -1.39393e-06 + 0.999914 * (_ctx_1024t + 0.3 * jax.random.normal(jax.random.fold_in(_rk, 611), (8, 64, 128), jnp.float32))
        _validS = jnp.arange(256)[None, :] < _lenS[:, None]
        _validS2 = jnp.arange(64)[None, :] < _lenS2[:, None]
        _causal = jnp.tril(jnp.ones((256, 256), dtype=bool))
        mask_BxS2_bk0 = jnp.logical_not(jnp.broadcast_to(_validS2[:, :], (8, 64)))
        return (x, ctx_1024, mask_BxS2_bk0)
    x, ctx_1024, mask_BxS2_bk0 = _rec_inputs()

    def _L0_xattn_setup():
        import jax, jax.numpy as jnp
        import numpy as np
        DIM = 128
        NUM_HEADS = 16
        HEAD_DIM = DIM // NUM_HEADS
        SCALE = HEAD_DIM ** (-0.5)
        key = jax.random.key(seed)
        ks = jax.random.split(key, 8)
        B, Nq, Nkv, C = (2, 256, 256, DIM)
        s = 0.02
        return {'query': jax.random.normal(ks[0], (B, Nq, C), jnp.float32), 'key': jax.random.normal(ks[1], (B, Nkv, C), jnp.float32), 'value': jax.random.normal(ks[2], (B, Nkv, C), jnp.float32), 'Wq': jax.random.normal(ks[3], (C, C), jnp.float32) * s, 'bq': jnp.zeros((C,), jnp.float32), 'Wk': jax.random.normal(ks[4], (C, C), jnp.float32) * s, 'bk': jnp.zeros((C,), jnp.float32), 'Wv': jax.random.normal(ks[5], (C, C), jnp.float32) * s, 'bv': jnp.zeros((C,), jnp.float32), 'Wo': jax.random.normal(ks[6], (C, C), jnp.float32) * s, 'bo': jnp.zeros((C,), jnp.float32)}
    _L0_xattn_all = _L0_xattn_setup()
    _L0_xattn_in = {k: v for k, v in _L0_xattn_all.items() if k in ('Wq', 'bq', 'Wk', 'bk', 'Wv', 'bv', 'Wo', 'bo')}
    del _L0_xattn_all

    def _L0_ffn_setup():
        import jax, jax.numpy as jnp
        import numpy as np
        N_EXP = 8
        TOP_K = 2
        CAPACITY_FACTOR = 1.25
        key = jax.random.key(seed)
        ks = jax.random.split(key, 5)
        B, T, D = (4, 128, 128)
        H = 4 * D
        E = N_EXP
        x = jax.random.normal(ks[0], (B, T, D), jnp.float32)
        gate_w = jax.random.normal(ks[1], (D, E), jnp.float32) * 0.02
        c_fc = jax.random.normal(ks[2], (E, D, H), jnp.float32) * 0.02
        fc_bias = jnp.zeros((E, 1, H), jnp.float32)
        c_proj = jax.random.normal(ks[3], (E, H, D), jnp.float32) * 0.02
        proj_bias = jnp.zeros((E, 1, D), jnp.float32)
        return dict(x=x, gate_w=gate_w, c_fc=c_fc, fc_bias=fc_bias, c_proj=c_proj, proj_bias=proj_bias)
    _L0_ffn_all = _L0_ffn_setup()
    _L0_ffn_in = {k: v for k, v in _L0_ffn_all.items() if k in ('gate_w', 'c_fc', 'fc_bias', 'c_proj', 'proj_bias')}
    del _L0_ffn_all

    def _L1_xattn_setup():
        import jax, jax.numpy as jnp
        import numpy as np
        import math
        D_MODEL = 128
        D_K = 64
        D_V = 64
        N_HEADS = 16
        key = jax.random.key(seed)
        ks = jax.random.split(key, 12)
        bz, sq = (4, 256)
        std = math.sqrt(1.0 / D_MODEL)
        inp = {'q': jax.random.normal(ks[0], (bz, sq, D_MODEL), jnp.float32), 'k': jax.random.normal(ks[1], (bz, sq, D_MODEL), jnp.float32), 'v': jax.random.normal(ks[2], (bz, sq, D_MODEL), jnp.float32), 'att_mask': jax.random.randint(ks[3], (bz, sq), 0, 2).astype(bool), 'Wq': std * jax.random.normal(ks[4], (D_K * N_HEADS, D_MODEL), jnp.float32), 'bq': jnp.zeros((D_K * N_HEADS,), jnp.float32), 'Wk': std * jax.random.normal(ks[5], (D_K * N_HEADS, D_MODEL), jnp.float32), 'bk': jnp.zeros((D_K * N_HEADS,), jnp.float32), 'Wv': std * jax.random.normal(ks[6], (D_V * N_HEADS, D_MODEL), jnp.float32), 'bv': jnp.zeros((D_V * N_HEADS,), jnp.float32), 'Wo': std * jax.random.normal(ks[7], (D_MODEL, D_V * N_HEADS), jnp.float32), 'bo': jnp.zeros((D_MODEL,), jnp.float32)}
        return inp
    _L1_xattn_all = _L1_xattn_setup()
    _L1_xattn_in = {k: v for k, v in _L1_xattn_all.items() if k in ('Wq', 'bq', 'Wk', 'bk', 'Wv', 'bv', 'Wo', 'bo')}
    del _L1_xattn_all

    def _L1_ffn_setup():
        import jax, jax.numpy as jnp
        import numpy as np
        B, S, D, H, F, E = (2, 128, 128, 16, 512, 8)
        HD = D // H
        EPS = 1e-06

        def _layernorm(x, g, b):
            m = jnp.mean(x, axis=-1, keepdims=True)
            v = jnp.var(x, axis=-1, keepdims=True)
            return (x - m) / jnp.sqrt(v + EPS) * g + b
        key = jax.random.key(seed)
        ks = jax.random.split(key, 10)
        sc = 0.02
        x = jax.random.normal(ks[0], (B, S, D), jnp.float32)
        Wq = jax.random.normal(ks[1], (D, D), jnp.float32) * sc
        Wk = jax.random.normal(ks[2], (D, D), jnp.float32) * sc
        Wv = jax.random.normal(ks[3], (D, D), jnp.float32) * sc
        Wo = jax.random.normal(ks[4], (D, D), jnp.float32) * sc
        bo = jnp.zeros((D,), jnp.float32)
        Wr = jax.random.normal(ks[5], (D, E), jnp.float32) * sc
        We1 = jax.random.normal(ks[6], (E, D, F), jnp.float32) * sc
        be1 = jnp.zeros((E, F), jnp.float32)
        We2 = jax.random.normal(ks[7], (E, F, D), jnp.float32) * sc
        be2 = jnp.zeros((E, D), jnp.float32)
        ln1_g = jnp.ones((D,), jnp.float32)
        ln1_b = jnp.zeros((D,), jnp.float32)
        ln2_g = jnp.ones((D,), jnp.float32)
        ln2_b = jnp.zeros((D,), jnp.float32)
        return {'x': x, 'Wq': Wq, 'Wk': Wk, 'Wv': Wv, 'Wo': Wo, 'bo': bo, 'Wr': Wr, 'We1': We1, 'be1': be1, 'We2': We2, 'be2': be2, 'ln1_g': ln1_g, 'ln1_b': ln1_b, 'ln2_g': ln2_g, 'ln2_b': ln2_b}
    _L1_ffn_all = _L1_ffn_setup()
    _L1_ffn_in = {k: v for k, v in _L1_ffn_all.items() if k in ('Wq', 'Wk', 'Wv', 'Wo', 'bo', 'Wr', 'We1', 'be1', 'We2', 'be2', 'ln1_g', 'ln1_b', 'ln2_g', 'ln2_b')}
    del _L1_ffn_all

    def _L2_xattn_setup():
        import jax, jax.numpy as jnp
        import numpy as np
        MODEL_DIM = 128
        NUM_HEADS = 16
        HEAD_DIM = MODEL_DIM // NUM_HEADS
        SCALE = HEAD_DIM ** (-0.5)
        key = jax.random.key(seed)
        ks = jax.random.split(key, 8)
        B, LQ, LC = (2, 256, 256)
        std = MODEL_DIM ** (-0.5)
        return {'query': jax.random.normal(ks[0], (B, LQ, MODEL_DIM), jnp.float32), 'context': jax.random.normal(ks[1], (B, LC, MODEL_DIM), jnp.float32), 'Wq': jax.random.normal(ks[2], (MODEL_DIM, MODEL_DIM), jnp.float32) * std, 'bq': jnp.zeros((MODEL_DIM,), jnp.float32), 'Wkv': jax.random.normal(ks[3], (MODEL_DIM, 2 * MODEL_DIM), jnp.float32) * std, 'bkv': jnp.zeros((2 * MODEL_DIM,), jnp.float32), 'Wout': jax.random.normal(ks[4], (MODEL_DIM, MODEL_DIM), jnp.float32) * std, 'bout': jnp.zeros((MODEL_DIM,), jnp.float32)}
    _L2_xattn_all = _L2_xattn_setup()
    _L2_xattn_in = {k: v for k, v in _L2_xattn_all.items() if k in ('Wq', 'bq', 'Wkv', 'bkv', 'Wout', 'bout')}
    del _L2_xattn_all

    def _L2_ffn_setup():
        import jax, jax.numpy as jnp
        import numpy as np
        B, S, D = (4, 512, 128)
        DD = 4 * D
        N_EXPERTS = 8
        CAPACITY = 1.0
        LN_EPS = 1e-05
        key = jax.random.key(seed)
        ks = jax.random.split(key, 8)
        s1 = 1.0 / np.sqrt(D)
        s2 = 1.0 / np.sqrt(DD)
        return {'x': jax.random.normal(ks[0], (B, S, D), jnp.float32), 'gate_w': jax.random.normal(ks[1], (N_EXPERTS, D), jnp.float32) * 0.02, 'ln_w': jnp.ones((D,), jnp.float32), 'ln_b': jnp.zeros((D,), jnp.float32), 'fc1s': jax.random.normal(ks[2], (N_EXPERTS, DD, D), jnp.float32) * s1, 'b1s': jax.random.normal(ks[3], (N_EXPERTS, DD), jnp.float32) * s1, 'fc2s': jax.random.normal(ks[4], (N_EXPERTS, D, DD), jnp.float32) * s2, 'b2s': jax.random.normal(ks[5], (N_EXPERTS, D), jnp.float32) * s2}
    _L2_ffn_all = _L2_ffn_setup()
    _L2_ffn_in = {k: v for k, v in _L2_ffn_all.items() if k in ('gate_w', 'ln_w', 'ln_b', 'fc1s', 'b1s', 'fc2s', 'b2s')}
    del _L2_ffn_all

    def _L3_xattn_setup():
        import jax, jax.numpy as jnp
        import numpy as np
        EMBED = 128
        HEADS = 16
        HEAD_DIM = EMBED // HEADS
        EXP_DIM = 2 * HEAD_DIM

        def _feature_map(x, fm_w, fm_b):
            z = jnp.einsum('nshd,ed->nshe', x, fm_w) + fm_b
            return jnp.concatenate([jnp.exp(z), jnp.exp(-z)], axis=-1)
        key = jax.random.key(seed)
        ks = jax.random.split(key, 7)
        N, S = (4, 256)
        values = jax.random.normal(ks[0], (N, S, EMBED), dtype=jnp.float32)
        keys_ = jax.random.normal(ks[1], (N, S, EMBED), dtype=jnp.float32)
        query = jax.random.normal(ks[2], (N, S, EMBED), dtype=jnp.float32)
        fm_w = jnp.eye(HEAD_DIM, dtype=jnp.float32) + 0.02 * jax.random.normal(ks[3], (HEAD_DIM, HEAD_DIM), dtype=jnp.float32)
        fm_b = 0.02 * jax.random.normal(ks[4], (HEAD_DIM,), dtype=jnp.float32)
        fc_w = jax.random.normal(ks[5], (EMBED, HEADS * EXP_DIM), dtype=jnp.float32) * (1.0 / np.sqrt(HEADS * EXP_DIM))
        fc_b = jnp.zeros((EMBED,), dtype=jnp.float32)
        return {'values': values, 'keys': keys_, 'query': query, 'fm_w': fm_w, 'fm_b': fm_b, 'fc_w': fc_w, 'fc_b': fc_b}
    _L3_xattn_all = _L3_xattn_setup()
    _L3_xattn_in = {k: v for k, v in _L3_xattn_all.items() if k in ('fm_w', 'fm_b', 'fc_w', 'fc_b')}
    del _L3_xattn_all

    def _L3_ffn_setup():
        import jax, jax.numpy as jnp
        import numpy as np
        THRESH_FACTOR = 0.7

        def ternary_quantize(w):
            delta = THRESH_FACTOR * jnp.mean(jnp.abs(w))
            return jnp.where(w > delta, 1.0, jnp.where(w < -delta, -1.0, 0.0)).astype(w.dtype)
        key = jax.random.key(seed)
        k1, k2, k3 = jax.random.split(key, 3)
        B, S, D_IN, D_OUT = (8, 512, 128, 128)
        inp = {'input': jax.random.normal(k1, (B, S, D_IN), dtype=jnp.float32), 'weight': jax.random.normal(k2, (D_OUT, D_IN), dtype=jnp.float32) * (1.0 / np.sqrt(D_IN)), 'alpha': jnp.ones((1,), dtype=jnp.float32), 'bias': jax.random.normal(k3, (D_OUT,), dtype=jnp.float32) * (1.0 / np.sqrt(D_IN))}
        return inp
    _L3_ffn_all = _L3_ffn_setup()
    _L3_ffn_in = {k: v for k, v in _L3_ffn_all.items() if k in ('weight', 'alpha', 'bias')}
    del _L3_ffn_all
    return {'x': x, 'ctx_1024': ctx_1024, 'mask_BxS2_bk0': mask_BxS2_bk0, 'L0_xattn_Wq': _L0_xattn_in['Wq'], 'L0_xattn_bq': _L0_xattn_in['bq'], 'L0_xattn_Wk': _L0_xattn_in['Wk'], 'L0_xattn_bk': _L0_xattn_in['bk'], 'L0_xattn_Wv': _L0_xattn_in['Wv'], 'L0_xattn_bv': _L0_xattn_in['bv'], 'L0_xattn_Wo': _L0_xattn_in['Wo'], 'L0_xattn_bo': _L0_xattn_in['bo'], 'L0_ffn_gate_w': _L0_ffn_in['gate_w'], 'L0_ffn_c_fc': _L0_ffn_in['c_fc'], 'L0_ffn_fc_bias': _L0_ffn_in['fc_bias'], 'L0_ffn_c_proj': _L0_ffn_in['c_proj'], 'L0_ffn_proj_bias': _L0_ffn_in['proj_bias'], 'L1_xattn_Wq': _L1_xattn_in['Wq'], 'L1_xattn_bq': _L1_xattn_in['bq'], 'L1_xattn_Wk': _L1_xattn_in['Wk'], 'L1_xattn_bk': _L1_xattn_in['bk'], 'L1_xattn_Wv': _L1_xattn_in['Wv'], 'L1_xattn_bv': _L1_xattn_in['bv'], 'L1_xattn_Wo': _L1_xattn_in['Wo'], 'L1_xattn_bo': _L1_xattn_in['bo'], 'L1_ffn_Wq': _L1_ffn_in['Wq'], 'L1_ffn_Wk': _L1_ffn_in['Wk'], 'L1_ffn_Wv': _L1_ffn_in['Wv'], 'L1_ffn_Wo': _L1_ffn_in['Wo'], 'L1_ffn_bo': _L1_ffn_in['bo'], 'L1_ffn_Wr': _L1_ffn_in['Wr'], 'L1_ffn_We1': _L1_ffn_in['We1'], 'L1_ffn_be1': _L1_ffn_in['be1'], 'L1_ffn_We2': _L1_ffn_in['We2'], 'L1_ffn_be2': _L1_ffn_in['be2'], 'L1_ffn_ln1_g': _L1_ffn_in['ln1_g'], 'L1_ffn_ln1_b': _L1_ffn_in['ln1_b'], 'L1_ffn_ln2_g': _L1_ffn_in['ln2_g'], 'L1_ffn_ln2_b': _L1_ffn_in['ln2_b'], 'L2_xattn_Wq': _L2_xattn_in['Wq'], 'L2_xattn_bq': _L2_xattn_in['bq'], 'L2_xattn_Wkv': _L2_xattn_in['Wkv'], 'L2_xattn_bkv': _L2_xattn_in['bkv'], 'L2_xattn_Wout': _L2_xattn_in['Wout'], 'L2_xattn_bout': _L2_xattn_in['bout'], 'L2_ffn_gate_w': _L2_ffn_in['gate_w'], 'L2_ffn_ln_w': _L2_ffn_in['ln_w'], 'L2_ffn_ln_b': _L2_ffn_in['ln_b'], 'L2_ffn_fc1s': _L2_ffn_in['fc1s'], 'L2_ffn_b1s': _L2_ffn_in['b1s'], 'L2_ffn_fc2s': _L2_ffn_in['fc2s'], 'L2_ffn_b2s': _L2_ffn_in['b2s'], 'L3_xattn_fm_w': _L3_xattn_in['fm_w'], 'L3_xattn_fm_b': _L3_xattn_in['fm_b'], 'L3_xattn_fc_w': _L3_xattn_in['fc_w'], 'L3_xattn_fc_b': _L3_xattn_in['fc_b'], 'L3_ffn_weight': _L3_ffn_in['weight'], 'L3_ffn_alpha': _L3_ffn_in['alpha'], 'L3_ffn_bias': _L3_ffn_in['bias']}

def reference(x, ctx_1024, mask_BxS2_bk0, L0_xattn_Wq, L0_xattn_bq, L0_xattn_Wk, L0_xattn_bk, L0_xattn_Wv, L0_xattn_bv, L0_xattn_Wo, L0_xattn_bo, L0_ffn_gate_w, L0_ffn_c_fc, L0_ffn_fc_bias, L0_ffn_c_proj, L0_ffn_proj_bias, L1_xattn_Wq, L1_xattn_bq, L1_xattn_Wk, L1_xattn_bk, L1_xattn_Wv, L1_xattn_bv, L1_xattn_Wo, L1_xattn_bo, L1_ffn_Wq, L1_ffn_Wk, L1_ffn_Wv, L1_ffn_Wo, L1_ffn_bo, L1_ffn_Wr, L1_ffn_We1, L1_ffn_be1, L1_ffn_We2, L1_ffn_be2, L1_ffn_ln1_g, L1_ffn_ln1_b, L1_ffn_ln2_g, L1_ffn_ln2_b, L2_xattn_Wq, L2_xattn_bq, L2_xattn_Wkv, L2_xattn_bkv, L2_xattn_Wout, L2_xattn_bout, L2_ffn_gate_w, L2_ffn_ln_w, L2_ffn_ln_b, L2_ffn_fc1s, L2_ffn_b1s, L2_ffn_fc2s, L2_ffn_b2s, L3_xattn_fm_w, L3_xattn_fm_b, L3_xattn_fc_w, L3_xattn_fc_b, L3_ffn_weight, L3_ffn_alpha, L3_ffn_bias):
    import jax
    import jax.numpy as jnp

    def _L0_xattn_ref(query, key, value, Wq, bq, Wk, bk, Wv, bv, Wo, bo):
        import jax, jax.numpy as jnp
        import numpy as np
        DIM = 128
        NUM_HEADS = 16
        HEAD_DIM = DIM // NUM_HEADS
        SCALE = HEAD_DIM ** (-0.5)
        B, Nq, C = query.shape
        H, D = (NUM_HEADS, HEAD_DIM)
        q = (query @ Wq.T + bq).reshape(B, Nq, H, D).transpose(0, 2, 1, 3)
        k = (key @ Wk.T + bk).reshape(B, -1, H, D).transpose(0, 2, 1, 3)
        v = (value @ Wv.T + bv).reshape(B, -1, H, D).transpose(0, 2, 1, 3)
        attn = jnp.einsum('bhqd,bhkd->bhqk', q, k) * SCALE
        attn = jax.nn.softmax(attn, axis=-1)
        out = jnp.einsum('bhqk,bhkd->bhqd', attn, v)
        out = out.transpose(0, 2, 1, 3).reshape(B, Nq, C)
        return out @ Wo.T + bo

    def _L0_ffn_ref(x, gate_w, c_fc, fc_bias, c_proj, proj_bias):
        import jax, jax.numpy as jnp
        import numpy as np
        N_EXP = 8
        TOP_K = 2
        CAPACITY_FACTOR = 1.25
        B, T, D = x.shape
        n = B * T
        E, k = (N_EXP, TOP_K)
        cap = int(CAPACITY_FACTOR * n * k / E)
        xt = x.reshape(n, D)
        logits = xt @ gate_w
        top_logits, top_idx = jax.lax.top_k(logits, k)
        masked = jnp.full_like(logits, -jnp.inf)
        masked = masked.at[jnp.arange(n)[:, None], top_idx].set(top_logits)
        router_probs = jax.nn.softmax(masked, axis=-1)
        exp_mask = jax.nn.one_hot(top_idx, E, dtype=jnp.int32)
        exp_mask = jnp.transpose(exp_mask, (1, 0, 2))
        exp_rank = jnp.cumsum(exp_mask.reshape(k * n, E), axis=0) - 1
        exp_rank = exp_rank.reshape(k, n, E)
        exp_mask = exp_mask * (exp_rank < cap).astype(jnp.int32)
        used_capacity = jnp.sum(exp_mask, axis=(0, 1))
        exp_rank = jnp.sum(exp_mask * exp_rank, axis=-1)
        exp_weights = exp_mask.astype(x.dtype) * router_probs[None]
        rank_oh = jax.nn.one_hot(exp_rank, cap, dtype=x.dtype)
        cb_weight = jnp.einsum('kne,knc->nec', exp_weights, rank_oh)
        sec_mask = (cb_weight != 0).astype(x.dtype)
        exp_batches = jnp.einsum('nec,nd->ecd', sec_mask, xt)
        h = jnp.einsum('ecd,edh->ech', exp_batches, c_fc) + fc_bias
        h = jax.nn.gelu(h, approximate=False)
        exp_out = jnp.einsum('ech,ehd->ecd', h, c_proj) + proj_bias
        out = jnp.einsum('nec,ecd->nd', cb_weight, exp_out)
        return out.reshape(B, T, D)

    def _L1_xattn_ref(q, k, v, att_mask, Wq, bq, Wk, bk, Wv, bv, Wo, bo):
        import jax, jax.numpy as jnp
        import numpy as np
        import math
        D_MODEL = 128
        D_K = 64
        D_V = 64
        N_HEADS = 16
        bz, len_q, _ = q.shape
        len_k = k.shape[1]
        q_h = (q @ Wq.T + bq).reshape(bz, len_q, N_HEADS, D_K).transpose(0, 2, 1, 3)
        k_h = (k @ Wk.T + bk).reshape(bz, len_k, N_HEADS, D_K).transpose(0, 2, 1, 3)
        v_h = (v @ Wv.T + bv).reshape(bz, len_k, N_HEADS, D_V).transpose(0, 2, 1, 3)
        scores = jnp.einsum('bhqd,bhkd->bhqk', q_h, k_h) / jnp.sqrt(jnp.float32(D_K))
        scores = jnp.where(att_mask[:, None, None, :], jnp.float32(-1000000000.0), scores)
        attn = jax.nn.softmax(scores, axis=-1)
        out = jnp.einsum('bhqk,bhkd->bhqd', attn, v_h)
        out = out.transpose(0, 2, 1, 3).reshape(bz, len_q, N_HEADS * D_V)
        return out @ Wo.T + bo

    def _L1_ffn_ref(x, Wq, Wk, Wv, Wo, bo, Wr, We1, be1, We2, be2, ln1_g, ln1_b, ln2_g, ln2_b):
        import jax, jax.numpy as jnp
        import numpy as np
        B, S, D, H, F, E = (2, 128, 128, 16, 512, 8)
        HD = D // H
        EPS = 1e-06

        def _layernorm(x, g, b):
            m = jnp.mean(x, axis=-1, keepdims=True)
            v = jnp.var(x, axis=-1, keepdims=True)
            return (x - m) / jnp.sqrt(v + EPS) * g + b
        b, s, d = x.shape

        def split_heads(t):
            return t.reshape(b, s, H, HD).transpose(0, 2, 1, 3)
        q = split_heads(x @ Wq)
        k = split_heads(x @ Wk)
        v = split_heads(x @ Wv)
        scores = jnp.einsum('bhqd,bhkd->bhqk', q, k) / jnp.sqrt(jnp.float32(HD))
        attn_w = jax.nn.softmax(scores, axis=-1)
        ctx = jnp.einsum('bhqk,bhkd->bhqd', attn_w, v)
        ctx = ctx.transpose(0, 2, 1, 3).reshape(b, s, d)
        attn_out = ctx @ Wo + bo
        out1 = _layernorm(x + attn_out, ln1_g, ln1_b)
        router_probs = jax.nn.softmax(out1 @ Wr, axis=-1)
        top_g, top_i = jax.lax.top_k(router_probs, 2)
        top_g = jax.nn.softmax(top_g, axis=-1)
        acc = jnp.zeros_like(out1)
        for e in range(E):
            sel = top_i == e
            msk = jnp.any(sel, axis=-1)[..., None].astype(out1.dtype)
            h = jax.nn.gelu(out1 * msk @ We1[e] + be1[e], approximate=False)
            o = h @ We2[e] + be2[e]
            gate = jnp.sum(top_g * sel.astype(top_g.dtype), axis=-1, keepdims=True)
            acc = acc + o * gate
        return _layernorm(out1 + acc, ln2_g, ln2_b)

    def _L2_xattn_ref(query, context, Wq, bq, Wkv, bkv, Wout, bout):
        import jax, jax.numpy as jnp
        import numpy as np
        MODEL_DIM = 128
        NUM_HEADS = 16
        HEAD_DIM = MODEL_DIM // NUM_HEADS
        SCALE = HEAD_DIM ** (-0.5)
        B, LQ, _ = query.shape
        LC = context.shape[1]
        H, D = (NUM_HEADS, HEAD_DIM)
        q = query @ Wq + bq
        kv = context @ Wkv + bkv
        kv = kv.reshape(B, LC, H, D, 2)
        k = jnp.transpose(kv[..., 0], (0, 2, 1, 3))
        v = jnp.transpose(kv[..., 1], (0, 2, 1, 3))
        q = jnp.transpose(q.reshape(B, LQ, H, D), (0, 2, 1, 3))
        scores = jnp.einsum('bhid,bhjd->bhij', q, k) * SCALE
        attn = jax.nn.softmax(scores, axis=-1)
        out = jnp.einsum('bhij,bhjd->bhid', attn, v)
        out = jnp.transpose(out, (0, 2, 1, 3)).reshape(B, LQ, H * D)
        return out @ Wout + bout

    def _L2_ffn_ref(x, gate_w, ln_w, ln_b, fc1s, b1s, fc2s, b2s):
        import jax, jax.numpy as jnp
        import numpy as np
        B, S, D = (4, 512, 128)
        DD = 4 * D
        N_EXPERTS = 8
        CAPACITY = 1.0
        LN_EPS = 1e-05
        og_shape = x.shape
        d = og_shape[-1]
        xf = x.reshape(-1, d)
        bs = xf.shape[0]
        n = gate_w.shape[0]
        k = int(bs * CAPACITY) // n
        scores = jax.nn.softmax(xf @ gate_w.T, axis=-1)
        vals, idx = jax.lax.top_k(scores.T, k)
        kept_w = vals.T
        kept_idx = idx.T
        flat_idx = kept_idx.reshape(-1)
        y = xf[flat_idx].reshape(k, n, d)
        mu = y.mean(-1, keepdims=True)
        var = ((y - mu) ** 2).mean(-1, keepdims=True)
        y = (y - mu) * jax.lax.rsqrt(var + LN_EPS) * ln_w + ln_b
        h = jnp.einsum('knd,nfd->knf', y, fc1s) + b1s
        h = jax.nn.gelu(h, approximate=True)
        out = jnp.einsum('knf,ndf->knd', h, fc2s) + b2s
        out = out * kept_w[..., None]
        xf = xf.at[flat_idx].add(out.reshape(k * n, d))
        return xf.reshape(og_shape)

    def _L3_xattn_ref(values, keys, query, fm_w, fm_b, fc_w, fc_b):
        import jax, jax.numpy as jnp
        import numpy as np
        EMBED = 128
        HEADS = 16
        HEAD_DIM = EMBED // HEADS
        EXP_DIM = 2 * HEAD_DIM

        def _feature_map(x, fm_w, fm_b):
            z = jnp.einsum('nshd,ed->nshe', x, fm_w) + fm_b
            return jnp.concatenate([jnp.exp(z), jnp.exp(-z)], axis=-1)
        N, S, _ = query.shape
        v = values.reshape(N, -1, HEADS, HEAD_DIM)
        k = keys.reshape(N, -1, HEADS, HEAD_DIM)
        q = query.reshape(N, -1, HEADS, HEAD_DIM)
        v, k, q = (_feature_map(x, fm_w, fm_b) for x in (v, k, q))
        scores = jnp.einsum('nqhd,nkhd->nhqk', q, k) / jnp.sqrt(jnp.float32(EMBED))
        attn = jax.nn.softmax(scores, axis=-1)
        out = jnp.einsum('nhql,nlhd->nqhd', attn, v)
        out = out.reshape(N, S, HEADS * EXP_DIM)
        return out @ fc_w.T + fc_b

    def _L3_ffn_ref(input, weight, alpha, bias):
        import jax, jax.numpy as jnp
        import numpy as np
        THRESH_FACTOR = 0.7

        def ternary_quantize(w):
            delta = THRESH_FACTOR * jnp.mean(jnp.abs(w))
            return jnp.where(w > delta, 1.0, jnp.where(w < -delta, -1.0, 0.0)).astype(w.dtype)
        w_ternary = ternary_quantize(weight)
        w_eff = w_ternary * alpha
        out = jnp.einsum('bsd,od->bso', input, w_eff) + bias
        return out
    x = x + _L0_xattn_ref(_layernorm(x, axis=-1), ctx_1024, ctx_1024, L0_xattn_Wq, L0_xattn_bq, L0_xattn_Wk, L0_xattn_bk, L0_xattn_Wv, L0_xattn_bv, L0_xattn_Wo, L0_xattn_bo)
    x = x + _L0_ffn_ref(_layernorm(x, axis=-1), L0_ffn_gate_w, L0_ffn_c_fc, L0_ffn_fc_bias, L0_ffn_c_proj, L0_ffn_proj_bias)
    x = x + _L1_xattn_ref(_layernorm(x, axis=-1), ctx_1024, ctx_1024, mask_BxS2_bk0, L1_xattn_Wq, L1_xattn_bq, L1_xattn_Wk, L1_xattn_bk, L1_xattn_Wv, L1_xattn_bv, L1_xattn_Wo, L1_xattn_bo)
    x = x + _L1_ffn_ref(_layernorm(x, axis=-1), L1_ffn_Wq, L1_ffn_Wk, L1_ffn_Wv, L1_ffn_Wo, L1_ffn_bo, L1_ffn_Wr, L1_ffn_We1, L1_ffn_be1, L1_ffn_We2, L1_ffn_be2, L1_ffn_ln1_g, L1_ffn_ln1_b, L1_ffn_ln2_g, L1_ffn_ln2_b)
    x = x + _L2_xattn_ref(_layernorm(x, axis=-1), ctx_1024, L2_xattn_Wq, L2_xattn_bq, L2_xattn_Wkv, L2_xattn_bkv, L2_xattn_Wout, L2_xattn_bout)
    x = x + _L2_ffn_ref(_layernorm(x, axis=-1), L2_ffn_gate_w, L2_ffn_ln_w, L2_ffn_ln_b, L2_ffn_fc1s, L2_ffn_b1s, L2_ffn_fc2s, L2_ffn_b2s)
    x = x + _L3_xattn_ref(ctx_1024, ctx_1024, _layernorm(x, axis=-1), L3_xattn_fm_w, L3_xattn_fm_b, L3_xattn_fc_w, L3_xattn_fc_b)
    x = x + _L3_ffn_ref(_layernorm(x, axis=-1), L3_ffn_weight, L3_ffn_alpha, L3_ffn_bias)
    return x

_drawn_inputs = setup_inputs


def setup_inputs(seed=0):
    import zlib

    import numpy as np

    out = dict(_drawn_inputs(seed))
    spreads = {'L0_xattn_bq': (0.0, 0.8),
     'L0_xattn_bk': (0.0, 2.0),
     'L0_xattn_bv': (0.0, 0.47),
     'L0_xattn_bo': (0.0, 0.1),
     'L0_ffn_fc_bias': (0.0, 0.73),
     'L0_ffn_proj_bias': (0.0, 0.1),
     'L1_xattn_bq': (0.0, 0.1),
     'L1_xattn_bk': (0.0, 2.0),
     'L1_xattn_bv': (0.0, 0.1),
     'L1_xattn_bo': (0.0, 0.1),
     'L1_ffn_bo': (0.0, 0.1),
     'L1_ffn_be1': (0.0, 0.8),
     'L1_ffn_be2': (0.0, 0.298),
     'L1_ffn_ln1_g': (1.0, 0.2),
     'L1_ffn_ln1_b': (0.0, 0.1),
     'L1_ffn_ln2_g': (1.0, 0.2),
     'L1_ffn_ln2_b': (0.0, 0.1),
     'L2_xattn_bq': (0.0, 0.8),
     'L2_xattn_bkv': (0.0, 0.1),
     'L2_xattn_bout': (0.0, 0.329),
     'L2_ffn_ln_w': (1.0, 0.6),
     'L2_ffn_ln_b': (0.0, 2.0),
     'L3_xattn_fc_b': (0.0, 0.704)}
    factors = {'L0_xattn_Wq': 8.0,
     'L0_xattn_Wk': 8.0,
     'L0_xattn_Wv': 3.064,
     'L0_xattn_Wo': 2.667,
     'L1_ffn_Wq': 8.0,
     'L1_ffn_Wk': 8.0,
     'L1_ffn_Wv': 3.445,
     'L1_ffn_Wo': 3.42,
     'L1_ffn_We1': 4.261,
     'L1_ffn_We2': 3.982,
     'L2_ffn_b1s': 23.886,
     'L2_ffn_b2s': 30.587,
     'L3_ffn_bias': 8.0}
    for name, (base, spread) in spreads.items():
        noise = np.random.default_rng([zlib.crc32(name.encode()), seed]).standard_normal(out[name].shape)
        drawn = base * np.exp(spread * noise) if base else spread * noise
        out[name] = jnp.asarray(drawn.astype(out[name].dtype))
    for name, factor in factors.items():
        out[name] = (out[name] * factor).astype(out[name].dtype)
    return out
```

```python
from contextlib import ExitStack

import numpy as np
import concourse.bass as bass
from concourse import mybir

F32 = mybir.dt.float32
BF16 = mybir.dt.bfloat16
I32 = mybir.dt.int32
ALU = mybir.AluOpType
ACT = mybir.ActivationFunctionType
X_AXIS = mybir.AxisListType.X

B, TQ, D = 8, 256, 128
N = B * TQ
NT = N // 128
TK = 64
H, HD = 16, 8
C = H // 2
HD1 = 64
E, F = 8, 512
FC = F // 128
CAP0 = int(1.25 * N * 2 / E)
TOP2 = N // E


def wait(eng, sem, value):
    if isinstance(value, int) and value <= 0:
        return
    eng.wait_ge(sem, value)


def pipelined(eng, body, lags=2):
    for i in range(lags):
        body(i, i % 2, lambda lag, i=i: 0 <= i - lag < B)
    with eng.Fori(lags // 2, B // 2) as pair:
        body(2 * pair, 0, lambda lag: True)
        body(2 * pair + 1, 1, lambda lag: True)
    for i in range(B, B + lags):
        body(i, i % 2, lambda lag, i=i: 0 <= i - lag < B)


class Pack:

    def __init__(self, rows):
        self.rows, self.at, self.width = rows, {}, 0

    def add(self, name, *shape):
        n = int(np.prod(shape))
        self.at[name] = (self.width, shape)
        self.width += n

    def view(self, tensor, name, parts=None):
        off, shape = self.at[name]
        n = int(np.prod(shape))
        v = tensor[0:parts or self.rows, off:off + n]
        if len(shape) == 2:
            v = v.rearrange("p (a b) -> p a b", a=shape[0])
        elif len(shape) == 3:
            v = v.rearrange("p (a b c) -> p a b c", a=shape[0], b=shape[1])
        return v


def packs():
    cols = Pack(128)
    cols.add("ident", 128)
    cols.add("head_mask", H)
    cols.add("feat_mask", H)
    cols.add("head_sel", C, 128)
    cols.add("ctxT2", B, 2, TK)
    for L in (0, 2):
        for w in ("wq", "wk", "wv", "wo"):
            cols.add(f"{w}{L}", D)
        cols.add(f"bq{L}", 1)
        cols.add(f"bk{L}", 1)
    cols.add("fm", D)
    cols.add("fmb", 1)
    cols.add("fcw", 2, D)
    cols.add("minus_half", 2)
    cols.add("gate0", E)
    cols.add("gate1", E)
    cols.add("gate2", E)
    for L in range(3):
        cols.add(f"b2_{L}", D)
    cols.add("tile_mask", NT)
    cols.add("descending", E)
    cols.add("before", 128)
    cols.add("all_ones", 128)
    cols.add("same_expert", 128)
    cols.add("earlier_tile", 128)
    for w in ("swq", "swk", "swv", "swo"):
        cols.add(w, D)
    cols.add("sbo", D)
    for n in ("ln1_g", "ln1_b", "ln2_g", "ln2_b", "lnw", "lnb"):
        cols.add(n, D)
    cols.add("bk1", C)
    cols.add("bv1", C)
    cols.add("bq1", C)
    cols.add("bo1", D)
    cols.add("pair_cols", 2)
    cols.add("w3", D)
    cols.add("alpha", 1)
    cols.add("b3", 1)
    cols.add("row0_ones", TQ)
    for n in ("bv0", "bo0", "bv2", "bo2", "fmb_row", "fcb"):
        cols.add(n, D)
    return cols


def build(nc, t):
    cols = packs()
    with ExitStack() as ctx:
        def sb(name, shape, dt=F32):
            return ctx.enter_context(nc.sbuf_tensor(name, shape, dt))

        def sem(name):
            return ctx.enter_context(nc.semaphore(name))

        ps = ctx.enter_context(nc.psum_tensor("ps", [128, 8, 512], F32))
        cw = sb("cw", [128, cols.width])
        x = sb("x", [128, NT, D])
        xn = sb("xn", [128, NT, D])
        xnT = sb("xnT", [128, N])
        K = lambda n, parts=None: cols.view(cw, n, parts)
        ident = K("ident")
        ones_row = K("row0_ones")[:, 0:128]

        kT = sb("kT", [128, 2, B * TK])
        vblk = sb("vblk", [128, B, C, 34])
        kblk = sb("kblk", [128, 2, 2, H, TK])
        qT = sb("qT", [128, 2, 2, TQ])
        nmax = sb("nmax", [128, 2, 2, 128])
        nmaxT = sb("nmaxT", [128, 2, TQ])
        pT = sb("pT", [128, 2, C, TQ])
        rsum = sb("rsum", [128, 2, H])
        on = sb("on", [128, 2, 2, D])
        oT = sb("oT", [128, 2, TQ])
        stats = sb("stats", [128, 2, 2, 6])
        xs = sb("xs", [128, 2, 2, D])
        mv = sb("mv", [128, 2, 2, 2])
        rstd = sb("rstd", [128, 2, 2])

        in_cw, in_x = sem("in_cw"), sem("in_x")
        passed, passed_pool = sem("passed"), sem("passed_pool")

        class AttnSignals:

            def __init__(self):
                self.k_raw = sem("attn_k_raw")
                self.k_done = sem("attn_k_done")
                self.v_raw = sem("attn_v_raw")
                self.v_done = sem("attn_v_done")
                self.v_zero = sem("attn_v_zero")
                self.kblk_done = sem("attn_kblk_done")
                self.mT_raw = sem("attn_mT_raw")
                self.mT_done = sem("attn_mT_done")
                self.q_raw = sem("attn_q_raw")
                self.q_done = sem("attn_q_done")
                self.nat_done = sem("attn_nat_done")
                self.max_done = sem("attn_max_done")
                self.s_done = sem("attn_s_done")
                self.p_done = sem("attn_p_done")
                self.o_done = sem("attn_o_done")
                self.rsum_done = sem("attn_rsum_done")
                self.on_done = sem("attn_on_done")
                self.oT_raw = sem("attn_oT_raw")
                self.oT_done = sem("attn_oT_done")
                self.y_done = sem("attn_y_done")

        class MoeSignals:

            def __init__(self):
                self.logits = sem("moe_logits")
                self.logits_read = sem("moe_logits_read")
                self.exp_out = sem("moe_exp_out")
                self.chain = sem("moe_chain")
                self.gates_done = sem("moe_gates_done")
                self.gT_raw = sem("moe_gT_raw")
                self.gT_done = sem("moe_gT_done")
                self.b2_done = sem("moe_b2_done")
                self.b2_raw = sem("moe_b2_raw")
                self.init_done = sem("moe_init_done")
                self.fc1_chunk = sem("moe_fc1_chunk")
                self.gelu_done = sem("moe_gelu_done")
                self.fc2_done = sem("moe_fc2_done")
                self.acc_done = sem("moe_acc_done")
                self.w1_in0 = sem("moe_w1_in0")
                self.w1_in1 = sem("moe_w1_in1")
                self.w2_in0 = sem("moe_w2_in0")
                self.w2_in1 = sem("moe_w2_in1")
                self.picked = sem("moe_picked")
                self.prefix = sem("moe_prefix")
                self.probs_done = sem("moe_probs_done")
                self.cand_done = sem("moe_cand_done")
                self.counted = sem("moe_counted")
                self.summed = sem("moe_summed")
                self.ok_done = sem("moe_ok_done")
                self.thr_done = sem("moe_thr_done")
                self.bit_done = sem("moe_bit_done")
                self.ties_counted = sem("moe_ties_counted")

        class WideSignals:

            def __init__(self):
                self.w_in = sem("wide_w_in")
                self.mask_in = sem("wide_mask_in")
                self.keep_done = sem("wide_keep_done")
                self.zero = sem("wide_zero")
                self.kv_raw = sem("wide_kv_raw")
                self.kv_done = sem("wide_kv_done")
                self.kv_masked = sem("wide_kv_masked")
                self.beta_raw = sem("wide_beta_raw")
                self.beta_done = sem("wide_beta_done")
                self.beta_out = sem("wide_beta_out")
                self.A_raw = sem("wide_A_raw")
                self.A_done = sem("wide_A_done")
                self.VW_raw = sem("wide_VW_raw")
                self.VW_done = sem("wide_VW_done")
                self.beta_in0 = sem("wide_beta_in0")
                self.beta_in1 = sem("wide_beta_in1")
                self.xb_done = sem("wide_xb_done")
                self.sum_done = sem("wide_sum_done")
                self.rs_done = sem("wide_rs_done")
                self.rT_raw = sem("wide_rT_raw")
                self.rT_done = sem("wide_rT_done")
                self.r_raw = sem("wide_r_raw")
                self.pn_done = sem("wide_pn_done")
                self.nat_done = attn_signals.nat_done
                self.max_done = attn_signals.max_done
                self.mT_raw = attn_signals.mT_raw
                self.mT_done = attn_signals.mT_done
                self.s_done = attn_signals.s_done
                self.p_done = attn_signals.p_done
                self.y_done = attn_signals.y_done

        class SelfSignals:

            def __init__(self):
                self.ones = sem("self_ones")
                self.xb_done = sem("self_xb_done")
                self.qk_raw = sem("self_qk_raw")
                self.qk_done = sem("self_qk_done")
                self.v_raw = sem("self_v_raw")
                self.v_done = sem("self_v_done")
                self.kblk_done = sem("self_kblk_done")
                self.nat_done = sem("self_nat_done")
                self.max_done = sem("self_max_done")
                self.s_done = sem("self_s_done")
                self.p_done = sem("self_p_done")
                self.pv_done = sem("self_pv_done")
                self.on_done = sem("self_on_done")
                self.rsum_done = sem("self_rsum_done")
                self.oT_raw = sem("self_oT_raw")
                self.oT_done = sem("self_oT_done")
                self.y_done = sem("self_y_done")

        class TernarySignals:

            def __init__(self):
                self.abs_done = sem("tern_abs_done")
                self.sum_done = sem("tern_sum_done")
                self.delta = sem("tern_delta")
                self.w_done = sem("tern_w_done")
                self.chain = sem("tern_chain")
                self.o_raw = sem("tern_o_raw")
                self.o_done = sem("tern_o_done")
                self.t_done = sem("tern_t_done")
                self.x_done = sem("tern_x_done")
                self.out_done = sem("tern_out_done")

        attn_signals, moe_signals = AttnSignals(), MoeSignals()
        norms = [0]
        stats_done, aggr_done, eps_done = sem("ln_stats_done"), sem("ln_aggr_done"), sem("ln_eps_done")
        rstd_done, xn_done, xT_raw = sem("ln_rstd_done"), sem("ln_xn_done"), sem("ln_xT_raw")

        class Norm:

            def __init__(self, name, src, eps, affine=None, keep=None):
                self.xT_done, self.x_done = sem(f"{name}_xT_done"), sem(f"{name}_x_done")
                if affine:
                    self.scaled, self.shifted = sem(f"{name}_scaled"), sem(f"{name}_shifted")
                if keep is not None:
                    self.saved = sem(f"{name}_saved")
                self.n0 = B * norms[0]
                norms[0] += 1
                self.src, self.eps, self.affine, self.keep = src, eps, affine, keep

            def tile(self, n):
                return self.src[:, bass.ds(n, 1), :].rearrange("p a d -> p (a d)")

            def dve_stats(self, v, b, u):
                v.wait_ge(in_x, 16)
                wait(v, rstd_done, self.n0 + b)
                v.sem_inc(passed, 1)
                for k in range(2):
                    v.bn_stats(stats[:, u, k, :], self.tile(2 * b + k)).then_inc(stats_done, 1)
                for k in range(2):
                    v.wait_ge(stats_done, 2 * (self.n0 + b) + k + 1)
                    v.sem_inc(passed, 1)
                    v.bn_aggr(mv[:, u, k, :], stats[:, u, k, :]).then_inc(aggr_done, 1)

            def pool_rstd(self, g, b, u):
                g.wait_ge(aggr_done, 2 * (self.n0 + b) + 2)
                g.sem_inc(passed_pool, 1)
                g.tensor_scalar(rstd[:, u, :], mv[:, u, :, 1], self.eps, None, ALU.add).then_inc(eps_done, 1)
                g.wait_ge(eps_done, self.n0 + b + 1)
                g.tensor_tensor(rstd[:, u, :], rstd[:, u, :], K("minus_half"), ALU.pow).then_inc(rstd_done, 1)

            def dve_apply(self, v, b, u):
                wait(v, xT_raw, self.n0 + b)
                v.wait_ge(rstd_done, self.n0 + b + 1)
                for k in range(2):
                    ins = v.tensor_scalar(xs[:, u, k, :], self.tile(2 * b + k),
                                          mv[:, u, k, 0:1], rstd[:, u, k:k + 1], ALU.subtract, ALU.mult)
                if self.affine is None:
                    ins.then_inc(xn_done, 1)
                    return
                ins.then_inc(self.scaled, 1)
                g, c = (K(n).unsqueeze(1).to_broadcast([128, 2, D]) for n in self.affine)
                v.wait_ge(self.scaled, b + 1)
                v.tensor_tensor(xs[:, u, :, :], xs[:, u, :, :], g, ALU.mult).then_inc(self.shifted, 1)
                v.wait_ge(self.shifted, b + 1)
                v.tensor_tensor(xs[:, u, :, :], xs[:, u, :, :], c, ALU.add).then_inc(xn_done, 1)

            def pe_transpose(self, p, b, u, bank):
                p.wait_ge(xn_done, self.n0 + b + 1)
                for k in range(2):
                    ins = p.transpose(bank[:, 128 * k:128 * k + 128], xs[:, u, k, :], ident)
                ins.then_inc(xT_raw, 1)

            def act_xT(self, a, b, u, bank):
                a.wait_ge(xT_raw, self.n0 + b + 1)
                a.activation(xnT[:, bass.ds(b * TQ, TQ)], bank, ACT.Copy).then_inc(self.xT_done, 1)

            def pool_save(self, g, b, u):
                g.wait_ge(xn_done, self.n0 + b + 1)
                g.tensor_copy(self.keep[:, bass.ds(2 * b, 2), :], xs[:, u, :, :]).then_inc(self.saved, 1)

        NAT = [ps[:, 0, :], ps[:, 1, :]]
        S4 = [ps[:, 2 + 2 * g:4 + 2 * g, :] for g in range(2)]
        O_BANK = ps[:, 6, :]
        Q_RAW = ps[:, 7, 0:256]
        Y = ps[:, 1, 0:256]
        OT_RAW = ps[:, 6, 0:256]
        MT_RAW = ps[:, 0, 0:256]
        XT_RAW = ps[:, 1, 256:512]

        class XAttn:

            def __init__(self, layer, order, before, ln, pe_after=()):
                self.pe_after = pe_after
                parts = 2 if layer == 3 else 1
                self.L, self.parts, self.before, self.ln = layer, parts, before, ln
                self.n0 = B * [0, 2, 3][order]
                self.m0, self.q0 = B * order, order
                self.s = attn_signals
                self.V = 16 * parts
                L = layer
                if parts == 1:
                    self.wq, self.wk, self.wv = K(f"wq{L}"), K(f"wk{L}"), K(f"wv{L}")
                    self.bv, self.bo, self.mask = K(f"bv{L}"), K(f"bo{L}"), K("head_mask")
                    self.wo = [K(f"wo{L}")]
                else:
                    self.wq = self.wk = self.wv = K("fm")
                    self.bv, self.bo, self.mask = K("fmb_row"), K("fcb"), K("feat_mask")
                    self.wo = [K("fcw")[:, 0, :], K("fcw")[:, 1, :]]

            def v_place(self, half, b0, s):
                return vblk[64 * half:64 * half + 64, b0:b0 + 4, :, 16 * s + 8 * half:16 * s + 8 * half + 8]

            def v_raw(self, half, b0):
                bank = ps[64 * half:64 * half + 64, 2 + b0 // 4, :].rearrange("p (b c j d) -> p b c j d", b=4, c=C, j=2)
                return bank[:, :, :, half, :]

            def pe_prepare(self, p):
                s = self.s
                for sm, value in self.pe_after:
                    p.wait_ge(sm, value)
                p.matmul(ps[:, 4, :], self.wk, K("ctxT2")[:, :, 0, :],
                         start=True, stop=True).then_inc(s.k_raw, 1)
                for b in range(B):
                    out = ps[:, 2 + b // 4, 128 * (b % 4):128 * (b % 4) + 128]
                    p.matmul(out, K("ctxT2")[:, b, :, :].rearrange("p j k -> p (j k)"), self.wv, start=True, stop=False)
                    ins = p.matmul(out, ones_row, self.bv, start=False, stop=True)
                ins.then_inc(s.v_raw, 1)

            def act_prepare(self, a):
                s = self.s
                a.wait_ge(s.k_raw, self.q0 + 1)
                if self.parts == 1:
                    a.activation(kT[:, 0, :], ps[:, 4, :], ACT.Identity, bias=K(f"bk{self.L}")).then_inc(s.k_done, 1)
                    a.wait_ge(s.v_raw, self.q0 + 1)
                    return
                a.activation(kT[:, 0, :], ps[:, 4, :], ACT.Exp, bias=K("fmb")).then_inc(s.k_done, 1)
                a.activation(kT[:, 1, :], ps[:, 4, :], ACT.Exp, bias=nfmb[:, 0:1], scale=-1.0).then_inc(s.k_done, 1)
                a.wait_ge(s.v_raw, self.q0 + 1)
                a.wait_ge(s.v_zero, 3 * self.q0 + 3)
                for half in range(2):
                    for b0 in (0, 4):
                        for sgn in range(2):
                            a.activation(self.v_place(half, b0, sgn), self.v_raw(half, b0), ACT.Exp,
                                         scale=1.0 - 2.0 * sgn).then_inc(s.v_done, 1)

            def dve_prepare(self, v):
                s = self.s
                v.memset(vblk[:, :, :, :], 0.0).then_inc(s.v_zero, 1)
                v.wait_ge(s.v_zero, 3 * self.q0 + 1)
                for half in range(2):
                    v.memset(vblk[64 * half:64 * half + 64, :, :, self.V + half:self.V + half + 1], 1.0).then_inc(s.v_zero, 1)
                v.wait_ge(s.v_zero, 3 * self.q0 + 3)
                if self.parts == 1:
                    v.wait_ge(s.v_raw, self.q0 + 1)
                    for half in range(2):
                        for b0 in (0, 4):
                            v.tensor_copy(self.v_place(half, b0, 0), self.v_raw(half, b0)).then_inc(s.v_done, 1)

            def pool_kblk(self, g, b, u):
                s = self.s
                wait(g, s.s_done, 2 * (self.n0 + b) - 2)
                for part in range(self.parts):
                    keys = kT[:, part, bass.ds(b * TK, TK)].unsqueeze(1).to_broadcast([128, H, TK])
                    mask = self.mask.unsqueeze(2).to_broadcast([128, H, TK])
                    g.tensor_tensor(kblk[:, u, part, :, :], keys, mask, ALU.mult).then_inc(s.kblk_done, 1)

            def pe(self, p):
                s, P = self.s, self.parts
                p.wait_ge(s.v_done, 4 * (self.q0 + P))

                def body(i, u, has):
                    n, m = self.n0 + i, self.m0 + self.parts * i
                    if has(0):
                        p.wait_ge(self.before.xT_done, i + 1)
                        wait(p, s.q_done, m)
                        p.matmul(Q_RAW, self.wq, xnT[:, bass.ds(i * TQ, TQ)], start=True, stop=True).then_inc(s.q_raw, 1)
                        p.wait_ge(s.q_done, m + P)
                        p.wait_ge(s.kblk_done, m + P)
                        wait(p, s.mT_done, n)
                        wait(p, self.ln.x_done, i - 1)
                        for k in range(2):
                            wait(p, s.max_done, 2 * n + k)
                            for half in range(2):
                                for part in range(P):
                                    ins = p.matmul(NAT[half], qT[:, u, part, 128 * k:128 * k + 128],
                                                   kblk[:, u, part, 8 * half:8 * half + 8, :].rearrange("p h k -> p (h k)"),
                                                   start=(part == 0), stop=(part == P - 1))
                            ins.then_inc(s.nat_done, 1)
                    if has(1):
                        b = i - 1
                        p.wait_ge(s.p_done, 2 * n)
                        wait(p, s.oT_done, m - P)
                        for k in range(2):
                            wait(p, s.on_done, 2 * self.m0 + P * (2 * b + k))
                            for c in range(C):
                                ins = p.matmul(O_BANK[:, c * (self.V + 2):(c + 1) * (self.V + 2)],
                                               pT[:, 1 - u, c, 128 * k:128 * k + 128],
                                               vblk[:, bass.ds(b, 1), c, 0:self.V + 2].rearrange("p a n -> p (a n)"),
                                               start=True, stop=True)
                            ins.then_inc(s.o_done, 1)
                    if has(0):
                        p.wait_ge(s.max_done, 2 * n + 2)
                        for k in range(2):
                            ins = p.transpose(MT_RAW[:, 128 * k:128 * k + 128], nmax[:, u, k, :], ident)
                        ins.then_inc(s.mT_raw, 1)
                    if has(2):
                        wait(p, self.ln.x_done, i - 1)
                        self.ln.pe_transpose(p, i - 2, u, XT_RAW)
                    for g in range(2):
                        if has(0):
                            wait(p, s.p_done, 2 * n - 1 + g)
                            p.wait_ge(s.mT_done, n + 1)
                            for c in range(4 * g, 4 * g + 4):
                                out = S4[g][:, (c % 4) // 2, 256 * (c % 2):256 * (c % 2) + 256]
                                for part in range(P):
                                    p.matmul(out, kblk[:, u, part, 2 * c:2 * c + 2, :].rearrange("p h k -> p (h k)"),
                                             qT[:, u, part, :], start=(part == 0), stop=False)
                                ins = p.matmul(out, K("head_sel")[:, c, :], nmaxT[:, u, :], start=False, stop=True)
                            ins.then_inc(s.s_done, 1)
                        if has(1) and g == 0:
                            b = i - 1
                            for part in range(P):
                                wait(p, s.oT_done, m - P + part)
                                p.wait_ge(s.on_done, 2 * self.m0 + P * (2 * b + 2))
                                for k in range(2):
                                    ins = p.transpose(OT_RAW[:, 128 * k:128 * k + 128], on[:, k, part, :], ident)
                                ins.then_inc(s.oT_raw, 1)
                    if has(1):
                        b = i - 1
                        p.wait_ge(s.oT_done, m)
                        wait(p, self.ln.xT_done, b)
                        for k in range(2):
                            out = Y[:, 128 * k:128 * k + 128]
                            for part in range(P):
                                p.matmul(out, oT[:, part, 128 * k:128 * k + 128], self.wo[part], start=(part == 0), stop=False)
                            ins = p.matmul(out, ones_row, self.bo, start=False, stop=True)
                        ins.then_inc(s.y_done, 1)
                pipelined(p, body)

            def act(self, a):
                s, P = self.s, self.parts

                def body(i, u, has):
                    n, m = self.n0 + i, self.m0 + self.parts * i
                    if has(0):
                        a.wait_ge(s.q_raw, self.m0 + i + 1)
                        if P == 1:
                            a.activation(qT[:, u, 0, :], Q_RAW, ACT.Identity, bias=K(f"bq{self.L}")).then_inc(s.q_done, 1)
                        else:
                            a.activation(qT[:, u, 0, :], Q_RAW, ACT.Exp, bias=K("fmb")).then_inc(s.q_done, 1)
                            a.activation(qT[:, u, 1, :], Q_RAW, ACT.Exp, bias=nfmb[:, 0:1], scale=-1.0).then_inc(s.q_done, 1)
                        a.wait_ge(s.mT_raw, n + 1)
                        a.activation(nmaxT[:, u, :], MT_RAW, ACT.Copy).then_inc(s.mT_done, 1)
                    if has(2):
                        self.ln.act_xT(a, i - 2, u, XT_RAW)
                    for g in range(2):
                        if has(0):
                            a.wait_ge(s.s_done, 2 * n + g + 1)
                            wait(a, s.o_done, 2 * (self.m0 + i - 1))
                            a.activation(pT[:, u, 4 * g:4 * g + 4, :].rearrange("p c q -> p (c q)"),
                                         S4[g].rearrange("p a n -> p (a n)"), ACT.Exp).then_inc(s.p_done, 1)
                        if has(1) and g == 0:
                            b = i - 1
                            for part in range(P):
                                a.wait_ge(s.oT_raw, m - P + part + 1)
                                wait(a, s.y_done, n - 1)
                                a.activation(oT[:, part, :], OT_RAW, ACT.Copy).then_inc(s.oT_done, 1)
                pipelined(a, body)

            def dve(self, v):
                s, P = self.s, self.parts

                def body(i, u, has):
                    n, m = self.n0 + i, self.m0 + self.parts * i
                    if has(0):
                        for k in range(2):
                            v.wait_ge(s.nat_done, 2 * n + k + 1)
                            v.tensor_reduce(nmax[:, u, k, 0:H], ps[:, 0:2, :].rearrange("p a (h k) -> p (a h) k", k=TK),
                                            X_AXIS, ALU.max, negate=True).then_inc(s.max_done, 1)
                    if has(2):
                        self.ln.dve_apply(v, i - 2, u)
                    if has(1):
                        b = i - 1
                        for k in range(2):
                            v.wait_ge(s.o_done, 2 * (self.m0 + b) + k + 1)
                            wait(v, s.oT_raw, m - P)
                            o = O_BANK[:, 0:C * (self.V + 2)].rearrange("p (c n) -> p c n", c=C)
                            v.reciprocal(rsum[:, k, :].rearrange("p (c j) -> p c j", j=2),
                                         o[:, :, self.V:self.V + 2]).then_inc(s.rsum_done, 1)
                            v.wait_ge(s.rsum_done, 2 * (self.m0 + b) + k + 1)
                            for part in range(P):
                                v.tensor_tensor(on[:, k, part, :].rearrange("p (c j d) -> p c j d", c=C, j=2),
                                                o[:, :, 16 * part:16 * part + 16].rearrange("p c (j d) -> p c j d", j=2),
                                                rsum[:, k, :].rearrange("p (c j) -> p c j", j=2).unsqueeze(3).to_broadcast([128, C, 2, HD]),
                                                ALU.mult).then_inc(s.on_done, 1)
                        v.wait_ge(s.y_done, n)
                        tiles = x[:, bass.ds(2 * b, 2), :]
                        v.tensor_tensor(tiles, tiles, Y.rearrange("p (a d) -> p a d", a=2), ALU.add).then_inc(self.ln.x_done, 1)
                        v.wait_ge(self.ln.x_done, b + 1)
                        self.ln.dve_stats(v, b, 1 - u)
                pipelined(v, body)

            def pool(self, g):
                def body(i, u, has):
                    n, m = self.n0 + i, self.m0 + self.parts * i
                    if has(0):
                        if isinstance(i, int) and i == 0:
                            g.wait_ge(self.s.k_done, self.q0 + self.parts)
                        self.pool_kblk(g, i, u)
                    if has(1):
                        self.ln.pool_rstd(g, i - 1, 1 - u)
                    if has(2) and self.ln.keep is not None:
                        self.ln.pool_save(g, i - 2, u)
                pipelined(g, body)

        nfmb = sb("nfmb", [128, 1])
        nf_done = sem("nf_done")
        beta_dram = nc.dram_tensor("beta_rows", (B, C, 128), F32).ap()

        kflat = kblk[:, :, :, :, :].rearrange("p u s h k -> p (u s h k)")
        vflat = vblk[:, :, :, :].rearrange("p b c n -> p (b c n)")
        big = sb("big", [128, 2 * B * C * 128])

        G = N // 512
        w1 = sb("w1", [128, 2, F + FC])
        w2 = sb("w2", [128, 2, FC, D])
        hT = big[:, 0:2 * F * FC].rearrange("p (u c n) -> p u c n", u=2, c=FC)
        gates = sb("gates", [128, NT, E])
        gatesT = sb("gatesT", [128, 128])
        b2blk = pT[:, 0, :, :].rearrange("p c q -> p (c q)").rearrange("p (t d) -> p t d", t=NT)
        res = kflat[:, 0:NT * D].rearrange("p (t d) -> p t d", t=NT)

        def tiles8(ap):
            return ap.rearrange("p (t e) -> p t e", e=E)

        def scratch(k, n=1):
            return vflat[:, 128 * k:128 * (k + n)]

        rt = {n: tiles8(scratch(k)) for k, n in enumerate(("val", "eq", "cand", "sel1", "sel2", "tmp"))}
        tot, scan = scratch(6, 2), scratch(8, 2)
        scT, gtm, eqm, cmp = (scratch(10 + k) for k in range(4))
        rc = {n: sb(f"rc_{n}", [128, NT]) for n in ("m1", "m2", "idx", "e2", "den", "p1", "p2")}
        thr, bit, cand_thr, okm = (sb(n, [128, 1], I32) for n in ("thr", "bit", "cand_thr", "okm"))
        cnt = sb("cnt", [128, 2])

        def bc(per_tile):
            return per_tile[:, :].unsqueeze(2).to_broadcast([128, NT, E])


        links = [0]

        class Moe:
            def __init__(self, layer, norm_before, gelu, dst):
                self.L, self.before, self.gelu, self.dst = layer, norm_before, gelu, dst
                self.s = moe_signals
                self.st0, self.r0 = layer * G * E, [0, 1, 3][layer]

            def pe_logits(self, p):
                p.wait_ge(self.before.xT_done, B)
                for t_ in range(NT):
                    ins = p.matmul(ps[:, 0, E * t_:E * t_ + E], xnT[:, 128 * t_:128 * t_ + 128], K(f"gate{self.L}"), start=True, stop=True)
                ins.then_inc(self.s.logits, 1)

            def link(self, ins):
                links[0] += 1
                ins.then_inc(self.s.chain, 1)
                return links[0]

            def probs(self, v):
                s = self.s
                after = lambda ins: v.wait_ge(s.chain, self.link(ins))
                v.wait_ge(s.logits, self.L + 1)
                lg = tiles8(ps[:, 0, 0:128])
                after(v.tensor_reduce(rc["m1"][:, :], lg, X_AXIS, ALU.max))
                v.tensor_tensor(rt["val"][:, :, :], lg, bc(rc["m1"]), ALU.subtract).then_inc(s.logits_read, 1)
                v.wait_ge(s.exp_out, self.r0 + 1)
                after(v.tensor_reduce(rc["den"][:, :], rt["tmp"][:, :, :], X_AXIS, ALU.add))
                after(v.reciprocal(rc["den"][:, :], rc["den"][:, :]))
                v.tensor_tensor(rt["val"][:, :, :], rt["tmp"][:, :, :], bc(rc["den"]), ALU.mult).then_inc(s.probs_done, 1)
                v.wait_ge(s.probs_done, self.L)

            def act_probs(self, a):
                a.wait_ge(self.s.logits_read, self.r0 + 1)
                a.activation(rt["tmp"][:, :, :], rt["val"][:, :, :], ACT.Exp).then_inc(self.s.exp_out, 1)

            def top2(self, v):
                s = self.s
                after = lambda ins: v.wait_ge(s.chain, self.link(ins))
                desc = K("descending").unsqueeze(1).to_broadcast([128, NT, E])
                for m, sel in (("m1", "sel1"), ("m2", "sel2")):
                    after(v.tensor_reduce(rc[m][:, :], rt["val"][:, :, :], X_AXIS, ALU.max))
                    after(v.tensor_tensor(rt["eq"][:, :, :], rt["val"][:, :, :], bc(rc[m]), ALU.is_equal))
                    after(v.tensor_tensor(rt["cand"][:, :, :], rt["eq"][:, :, :], desc, ALU.mult))
                    after(v.tensor_reduce(rc["idx"][:, :], rt["cand"][:, :, :], X_AXIS, ALU.max))
                    v.tensor_tensor(rt[sel][:, :, :], bc(rc["idx"]), desc, ALU.is_equal).then_inc(s.picked, 1)
                    v.wait_ge(s.picked, 2 * self.L + (1 if m == "m1" else 2))
                    if m == "m1":
                        after(v.scalar_tensor_tensor(rt["val"][:, :, :], rt[sel][:, :, :], -1e30, rt["val"][:, :, :], ALU.mult, ALU.add))
                v.tensor_tensor(rc["p2"][:, :], rc["m2"][:, :], rc["m1"][:, :], ALU.subtract).then_inc(s.logits_read, 1)

            def dve_logits(self, v):
                v.wait_ge(self.s.logits, self.L + 1)
                v.tensor_copy(rt["val"][:, :, :], tiles8(ps[:, 0, 0:128])).then_inc(self.s.chain, 1)
                links[0] += 1
                v.wait_ge(self.s.chain, links[0])

            def act_pair(self, a, n):
                a.wait_ge(self.s.logits_read, self.r0 + n)
                a.activation(rc["e2"][:, :], rc["p2"][:, :], ACT.Exp).then_inc(self.s.exp_out, 1)

            def pair_probs(self, v, n):
                after = lambda ins: v.wait_ge(self.s.chain, self.link(ins))
                v.wait_ge(self.s.exp_out, self.r0 + n)
                after(v.tensor_scalar(rc["den"][:, :], rc["e2"][:, :], 1.0, None, ALU.add))
                after(v.reciprocal(rc["p1"][:, :], rc["den"][:, :]))
                after(v.tensor_tensor(rc["p2"][:, :], rc["p1"][:, :], rc["e2"][:, :], ALU.mult))

            def combine(self, v):
                after = lambda ins: v.wait_ge(self.s.chain, self.link(ins))
                after(v.tensor_tensor(rt["eq"][:, :, :], rt["sel1"][:, :, :], bc(rc["p1"]), ALU.mult))
                after(v.tensor_tensor(rt["cand"][:, :, :], rt["sel2"][:, :, :], bc(rc["p2"]), ALU.mult))
                v.tensor_tensor(gates[:, :, :], rt["eq"][:, :, :], rt["cand"][:, :, :], ALU.add).then_inc(self.s.gates_done, 1)

            def pe_prefix(self, p):
                s = self.s
                p.wait_ge(s.picked, 2)
                for k, sel in enumerate(("sel1", "sel2")):
                    p.matmul(ps[:, 1, 128 * k:128 * k + 128], K("before"), rt[sel][:, :, :].rearrange("p t e -> p (t e)"), start=True, stop=True)
                    ins = p.matmul(ps[:, 2, 128 * k:128 * k + 128], K("all_ones"), rt[sel][:, :, :].rearrange("p t e -> p (t e)"), start=True, stop=True)
                ins.then_inc(s.prefix, 1)

            def capacity(self, v):
                s = self.s
                after = lambda ins: v.wait_ge(s.chain, self.link(ins))
                v.wait_ge(s.prefix, 1)
                after(v.tensor_copy(tot[:, :], ps[:, 2, 0:256]))
                for e in range(E):
                    ins = v.tensor_tensor_scan(scan[:, :].rearrange("p (k e) -> p k e", e=E)[:, :, e],
                                               K("all_ones")[:, 0:2 * NT],
                                               tot[:, :].rearrange("p (k e) -> p k e", e=E)[:, :, e],
                                               0.0, ALU.mult, ALU.add)
                    self.link(ins)
                v.wait_ge(s.chain, links[0])
                after(v.tensor_tensor(scan[:, :], scan[:, :], tot[:, :], ALU.subtract))
                after(v.tensor_tensor(scan[:, :], scan[:, :], ps[:, 1, 0:256], ALU.add))
                after(v.tensor_scalar(scan[:, :], scan[:, :], float(CAP0), None, ALU.is_lt))
                for k, sel in enumerate(("sel1", "sel2")):
                    after(v.tensor_tensor(rt[sel][:, :, :], rt[sel][:, :, :], tiles8(scan[:, 128 * k:128 * k + 128]), ALU.mult))

            def dve_threshold(self, v):
                s = self.s
                after = lambda ins: v.wait_ge(s.chain, self.link(ins))
                v.wait_ge(s.gT_raw, 3)
                after(v.tensor_copy(scT[:, :], ps[:, 3, 0:128]))
                after(v.memset(thr[:, :], 0))
                after(v.memset(bit[:, :], 1 << 29))
                with v.Fori(0, 30) as i:
                    v.tensor_tensor(cand_thr[:, :], thr[:, :], bit[:, :], ALU.bitwise_or).then_inc(s.cand_done, 1)
                    v.wait_ge(s.cand_done, i + 1)
                    v.tensor_scalar(cmp[:, :], scT[:, :], cand_thr[:, 0:1].bitcast(F32), None, ALU.is_ge, ALU.add, accum_out=cnt[:, 0:1]).then_inc(s.counted, 1)
                    v.wait_ge(s.summed, i + 1)
                    v.tensor_scalar(okm[:, :], ps[:, 4, 0:1], float(TOP2), -1.0, ALU.is_ge, ALU.mult).then_inc(s.ok_done, 1)
                    v.wait_ge(s.ok_done, i + 1)
                    v.scalar_tensor_tensor(thr[:, :], bit[:, :], okm[:, 0:1], thr[:, :], ALU.bitwise_and, ALU.bitwise_or).then_inc(s.thr_done, 1)
                    v.wait_ge(s.thr_done, i + 1)
                    v.tensor_scalar(bit[:, :], bit[:, :], 1, None, ALU.logical_shift_right).then_inc(s.bit_done, 1)
                    v.wait_ge(s.bit_done, i + 1)
                t_f = thr[:, 0:1].bitcast(F32)
                after(v.tensor_scalar(gtm[:, :], scT[:, :], t_f, None, ALU.is_gt, ALU.add, accum_out=cnt[:, 0:1]))
                v.tensor_scalar(eqm[:, :], scT[:, :], t_f, None, ALU.is_equal, ALU.add, accum_out=cnt[:, 1:2]).then_inc(s.ties_counted, 1)
                v.wait_ge(s.ties_counted, 1)
                after(v.tensor_tensor_scan(cmp[:, :], K("all_ones"), eqm[:, :], 0.0, ALU.mult, ALU.add))
                after(v.tensor_tensor(cmp[:, :], cmp[:, :], eqm[:, :], ALU.subtract))
                v.wait_ge(s.prefix, 2)
                after(v.tensor_copy(cnt[:, 0:2], ps[:, 4, 1:3]))
                after(v.tensor_tensor(cnt[:, 0:1], cnt[:, 0:1], cnt[:, 1:2], ALU.add))
                after(v.tensor_scalar(cnt[:, 0:1], cnt[:, 0:1], -1.0, float(TOP2), ALU.mult, ALU.add))
                after(v.tensor_scalar(cmp[:, :], cmp[:, :], cnt[:, 0:1], None, ALU.is_lt))
                after(v.tensor_tensor(cmp[:, :], cmp[:, :], eqm[:, :], ALU.mult))
                after(v.tensor_tensor(cmp[:, :], cmp[:, :], gtm[:, :], ALU.add))
                v.tensor_tensor(gatesT[:, :], cmp[:, :], scT[:, :], ALU.mult).then_inc(s.gT_done, 1)

            def pe_threshold(self, p):
                s = self.s
                p.wait_ge(s.probs_done, self.L)
                p.transpose(ps[:, 3, 0:128], rt["val"][:, :, :].rearrange("p t e -> p (t e)"), ident).then_inc(s.gT_raw, 1)
                with p.Fori(0, 30) as i:
                    p.wait_ge(s.counted, i + 1)
                    p.matmul(ps[:, 4, 0:1], K("same_expert"), cnt[:, 0:1], start=True, stop=True).then_inc(s.summed, 1)
                p.wait_ge(s.ties_counted, 1)
                p.matmul(ps[:, 4, 1:2], K("same_expert"), cnt[:, 0:1], start=True, stop=True)
                p.matmul(ps[:, 4, 2:3], K("earlier_tile"), cnt[:, 1:2], start=True, stop=True).then_inc(s.prefix, 1)

            def pool_b2(self, g):
                g.tensor_tensor(b2blk[:, :, :], K(f"b2_{self.L}").unsqueeze(1).to_broadcast([128, NT, D]),
                                K("tile_mask").unsqueeze(2).to_broadcast([128, NT, D]), ALU.mult).then_inc(self.s.b2_done, 1)

            def pe_init(self, p):
                s = self.s
                if self.L != 2:
                    p.wait_ge(s.gates_done, self.L + 1)
                    p.transpose(ps[:, 3, 0:128], gates[:, :, :].rearrange("p t e -> p (t e)"), ident).then_inc(s.gT_raw, 1)
                p.wait_ge(s.gT_done, self.L + 1)
                if self.L == 2:
                    p.transpose(ps[:, 3, 0:128], gatesT[:, :], ident).then_inc(s.gT_raw, 1)
                p.wait_ge(s.b2_done, self.L + 1)
                for k in range(4):
                    p.matmul(ps[:, 4 + k, :], gatesT[:, :], b2blk[:, 4 * k:4 * k + 4, :].rearrange("p t d -> p (t d)"), start=True, stop=True).then_inc(s.b2_raw, 1)

            def dve_init(self, v):
                s = self.s
                if self.L != 2:
                    v.wait_ge(s.gT_raw, self.L + 1)
                    v.tensor_copy(gatesT[:, :], ps[:, 3, 0:128]).then_inc(s.gT_done, 1)
                else:
                    v.wait_ge(s.gT_raw, 4)
                    v.tensor_copy(gates[:, :, :].rearrange("p t e -> p (t e)"), ps[:, 3, 0:128]).then_inc(s.gates_done, 1)
                if self.before.keep is not None:
                    v.wait_ge(self.before.saved, B)
                for k in range(4):
                    v.wait_ge(s.b2_raw, 4 * self.L + k + 1)
                    tiles = self.dst[:, 4 * k:4 * k + 4, :].rearrange("p t d -> p (t d)")
                    v.tensor_tensor(tiles, tiles, ps[:, 4 + k, :], ALU.add).then_inc(s.init_done, 1)
                if self.L == 2:
                    v.wait_ge(s.init_done, 4 * self.L + 4)
                    v.tensor_tensor(x[:, :, :], x[:, :, :], xn[:, :, :], ALU.add).then_inc(s.init_done, 1)
                v.wait_ge(s.init_done, 4 * self.L + (5 if self.L == 2 else 4))
                v.wait_ge(s.gates_done, self.L + 1)

            def experts(self, eng, body):
                for e in range(2):
                    body(e, e, 0)
                with eng.Fori(1, E // 2) as pair:
                    body(2 * pair, 0, pair)
                    body(2 * pair + 1, 1, pair)

            def sync(self, sp):
                s = self.s

                def body(e, u, pair):
                    for ww, src, landed in ((w1, t[f"w1_{self.L}"], (s.w1_in0, s.w1_in1)), (w2, t[f"w2_{self.L}"], (s.w2_in0, s.w2_in1))):
                        wait(sp, s.fc2_done, self.st0 + G * (e - 1))
                        dst = ww[:, u, :] if ww is w1 else ww[:, u, :, :].rearrange("p c d -> p (c d)")
                        sp.dma_start(dst, src[bass.ds(e, 1), :, :].rearrange("a p n -> (a p) n")).then_inc(landed[u], 16)
                self.experts(sp, body)

            def fc2(self, p, step, u, parity):
                s = self.s
                p.wait_ge(s.gelu_done, FC * step + FC)
                wait(p, s.acc_done, 4 * (step - 1))
                for k in range(4):
                    for c in range(FC):
                        ins = p.matmul(ps[:, 4 + parity, 128 * k:128 * k + 128], hT[:, parity, c, 128 * k:128 * k + 128],
                                       w2[:, u, c, :], start=(c == 0), stop=(c == FC - 1))
                ins.then_inc(s.fc2_done, 1)

            def pe(self, p):
                s = self.s
                p.wait_ge(s.init_done, 4 * self.L + 4)
                if self.L == 2:
                    p.wait_ge(ln_g.xT_done, B)

                def body(e, u, pair):
                    for g in range(G):
                        step = self.st0 + G * e + g
                        if g == 0:
                            p.wait_ge((s.w1_in0, s.w1_in1)[u], 16 * (self.L * (E // 2) + pair) + 16)
                        for c in range(FC):
                            wait(p, s.gelu_done, FC * (step - 1) + c + 1)
                            p.matmul(ps[:, c, :], w1[:, u, 128 * c:128 * c + 128], xnT[:, 512 * g:512 * g + 512], start=True, stop=True).then_inc(
                                s.fc1_chunk, 1)
                        if g == 0:
                            if not (isinstance(e, int) and e == 0):
                                self.fc2(p, step - 1, 1 - u, 1)
                            p.wait_ge((s.w2_in0, s.w2_in1)[u], 16 * (self.L * (E // 2) + pair) + 16)
                        else:
                            self.fc2(p, step - 1, u, (g - 1) % 2)
                self.experts(p, body)
                self.fc2(p, self.st0 + G * E - 1, 1, 1)

            def act(self, a):
                s = self.s

                def body(e, u, pair):
                    for g in range(G):
                        step = self.st0 + G * e + g
                        wait(a, s.fc2_done, step - 1)
                        for c in range(FC):
                            a.wait_ge(s.fc1_chunk, FC * step + c + 1)
                            a.activation(hT[:, g % 2, c, :], ps[:, c, :], self.gelu, bias=w1[:, u, F + c:F + c + 1]).then_inc(s.gelu_done, 1)
                self.experts(a, body)

            def dve(self, v):
                s = self.s

                def body(e, u, pair):
                    for g in range(G):
                        step = self.st0 + G * e + g
                        v.wait_ge(s.fc2_done, step + 1)
                        for k in range(4):
                            tile = self.dst[:, 4 * g + k, :]
                            v.scalar_tensor_tensor(tile, ps[:, 4 + g % 2, 128 * k:128 * k + 128],
                                                   gates[:, 4 * g + k, bass.ds(e, 1)], tile, ALU.mult, ALU.add).then_inc(s.acc_done, 1)
                self.experts(v, body)

        class NormPhase:

            def __init__(self, norm, add_to=None, pe_after=(), act_after=(), dve_after=()):
                self.n, self.add_to = norm, add_to
                self.pe_after, self.act_after, self.dve_after = pe_after, act_after, dve_after

            def pe(self, p):
                for sm, value in self.pe_after:
                    p.wait_ge(sm, value)

                def body(i, u, has):
                    if has(2):
                        wait(p, self.n.xT_done, i - 2)
                        self.n.pe_transpose(p, i - 2, u, XT_RAW)
                if self.add_to is None:
                    pipelined(p, body)

            def act(self, a):
                for sm, value in self.act_after:
                    a.wait_ge(sm, value)

                def body(i, u, has):
                    if has(2):
                        self.n.act_xT(a, i - 2, u, XT_RAW)
                if self.add_to is None:
                    pipelined(a, body)

            def dve(self, v):
                for sm, value in self.dve_after:
                    v.wait_ge(sm, value)

                def body(i, u, has):
                    if has(0):
                        self.n.dve_stats(v, i, u)
                    if has(1):
                        b = i - 1
                        self.n.dve_apply(v, b, 1 - u)
                        if self.add_to is not None:
                            v.wait_ge(xn_done, self.n.n0 + b + 1)
                            tiles = self.add_to[:, bass.ds(2 * b, 2), :]
                            v.tensor_tensor(tiles, tiles, xs[:, 1 - u, :, :], ALU.add).then_inc(xT_raw, 1)
                pipelined(v, body)

            def pool(self, g):
                def body(i, u, has):
                    if has(0):
                        self.n.pool_rstd(g, i, u)
                pipelined(g, body)

        A1 = big[:, 0:B * C * 128].rearrange("p (b c n) -> p b c n", b=B, c=C)
        VW = big[:, B * C * 128:2 * B * C * 128].rearrange("p (b c n) -> p b c n", b=B, c=C)
        wide_w = pT[:, :, :, :].rearrange("p u c q -> p (u c q)").rearrange("p (w n) -> p w n", w=4)
        khead = kflat[:, 0:4 * B * TK].rearrange("p (v b j k) -> p v b j k", v=2, b=B, j=2)
        keep = sb("keep", [128, B * TK])
        mask8 = sb("mask8", [128, B * TK], mybir.dt.uint8)
        drop = kflat[0:1, 3072:4096].rearrange("p (b j k) -> p b j k", b=B, j=2)
        beta = kflat[0:1, 2048:3072].rearrange("p (b n) -> p b n", b=B)
        betaz = sb("betaz", [128, 2, C * 128])
        xb = sb("xb", [128, 2, TQ])
        rs1 = sb("rs1", [128, 2, 128])
        rsT = sb("rsT", [128, TQ])

        class Wide:
            def __init__(self, before, ln):
                self.before, self.ln = before, ln
                self.s = WideSignals()
                self.n0 = B

            def sync_prepare(self, sp):
                s = self.s
                sp.dma_start(wide_w[:, :, :], t["wide_w"]).then_inc(s.w_in, 16)
                sp.dma_start(mask8[:, :], t["mask"].partition_broadcast(128).rearrange("a b n -> a (b n)")).then_inc(s.mask_in, 16)
                for c in range(C):
                    sp.wait_ge(s.beta_done, c + 1)
                    sp.dma_start(beta_dram[:, c, :], beta[:, :, :]).then_inc(s.beta_out, 16)

            def pe_prepare(self, p):
                s = self.s
                p.wait_ge(s.w_in, 16)
                for c in range(C):
                    col = slice(128 * c, 128 * c + 128)
                    if c >= 1:
                        p.wait_ge(s.kv_done, 2 * c)
                    p.matmul(ps[:, 2, :], wide_w[:, 1, col], K("ctxT2")[:, :, 0, :], start=True, stop=True)
                    p.matmul(ps[:, 3, :], wide_w[:, 2, col], K("ctxT2")[:, :, 0, :], start=True, stop=True).then_inc(s.kv_raw, 1)
                    p.wait_ge(s.kv_masked, c + 1)
                    p.wait_ge(s.kv_done, 2 * c + 2)
                    if c >= 1:
                        p.wait_ge(s.A_done, 2 * c)
                        p.wait_ge(s.beta_done, c)
                        p.wait_ge(s.VW_done, 2 * c)
                    for n in range(2):
                        keys = khead[:, 0, 4 * n:4 * n + 4, :, :].rearrange("p b j k -> p (b j k)")
                        p.matmul(ps[:, 4 + n, :], wide_w[:, 0, col], keys, start=True, stop=True).then_inc(s.A_raw, 1)
                    for n in range(2):
                        keys = khead[:, 0, 4 * n:4 * n + 4, :, :].rearrange("p b j k -> p (b j k)")
                        ins = p.matmul(ps[0:1, n, :], K("bq1")[:, c:c + 1], keys, start=True, stop=True)
                    ins.then_inc(s.beta_raw, 1)
                    for b in range(B):
                        ins = p.matmul(ps[:, 6 + b // 4, 128 * (b % 4):128 * (b % 4) + 128], khead[:, 1, b, :, :].rearrange("p j k -> p (j k)"),
                                       wide_w[:, 3, col], start=True, stop=True)
                    ins.then_inc(s.VW_raw, 1)

            def act_prepare(self, a):
                s = self.s
                a.wait_ge(s.zero, 1)
                for c in range(C):
                    a.wait_ge(s.kv_raw, c + 1)
                    if c >= 1:
                        a.wait_ge(s.VW_raw, c)
                    for kind in range(2):
                        bias = K("bk1" if kind == 0 else "bv1")
                        for j in range(2):
                            rows = slice(64 * j, 64 * j + 64)
                            ins = a.activation(khead[rows, kind, :, j, :], ps[rows, 2 + kind, :].rearrange("p (b k) -> p b k", b=B),
                                               ACT.Identity, bias=bias[rows, c:c + 1])
                        ins.then_inc(s.kv_done, 1)
                    for n in range(2):
                        a.wait_ge(s.A_raw, 2 * c + n + 1)
                        a.activation(A1[:, 4 * n:4 * n + 4, c, :], ps[:, 4 + n, :].rearrange("p (b n) -> p b n", b=4), ACT.Copy).then_inc(s.A_done, 1)

            def dve_prepare(self, v):
                s = self.s
                v.wait_ge(m0.s.fc2_done, 1 * G * E)
                v.memset(khead[:, :, :, :, :], 0.0).then_inc(s.zero, 1)
                v.memset(betaz[:, :, :], 0.0).then_inc(s.keep_done, 1)
                v.memset(rs1[:, :, :], 0.0).then_inc(s.keep_done, 1)
                v.wait_ge(s.mask_in, 16)
                v.tensor_copy(keep[:, :], mask8[:, :]).then_inc(s.keep_done, 1)
                v.wait_ge(s.keep_done, 3)
                for j in range(2):
                    v.tensor_scalar(drop[:, :, j, :], keep[0:1, :].rearrange("p (b k) -> p b k", b=B), -1e9, None, ALU.mult).then_inc(s.keep_done, 1)
                v.wait_ge(s.keep_done, 5)
                v.tensor_scalar(keep[:, :], keep[:, :], -(HD1 ** -0.5), HD1 ** -0.5, ALU.mult, ALU.add).then_inc(s.keep_done, 1)
                v.wait_ge(s.keep_done, 6)
                for c in range(C):
                    v.wait_ge(s.kv_done, 2 * c + 1)
                    for j in range(2):
                        rows = slice(64 * j, 64 * j + 64)
                        ins = v.tensor_tensor(khead[rows, 0, :, j, :], khead[rows, 0, :, j, :], keep[rows, :].rearrange("p (b k) -> p b k", b=B), ALU.mult)
                    ins.then_inc(s.kv_masked, 1)
                    v.wait_ge(s.beta_raw, c + 1)
                    if c >= 1:
                        v.wait_ge(s.beta_out, 16 * c)
                    v.tensor_tensor(beta[:, :, :].rearrange("p (n b) k -> p n (b k)", n=2), ps[0:1, 0:2, :],
                                    drop[:, :, :, :].rearrange("p (n b) j k -> p n (b j k)", n=2), ALU.add).then_inc(s.beta_done, 1)
                    v.wait_ge(s.VW_raw, c + 1)
                    for n in range(2):
                        v.tensor_copy(VW[:, 4 * n:4 * n + 4, c, :], ps[:, 6 + n, :].rearrange("p (b n) -> p b n", b=4)).then_inc(s.VW_done, 1)

            def sync(self, sp):
                s = self.s
                sp.wait_ge(s.beta_out, 16 * C)
                sp.wait_ge(s.keep_done, 6)

                def body(b, u):
                    wait(sp, s.s_done, 2 * (self.n0 + b) - 2)
                    sp.dma_start(betaz[0:1, u, :], beta_dram[bass.ds(b, 1), :, :].rearrange("a c n -> a (c n)")).then_inc((s.beta_in0, s.beta_in1)[u], 16)
                for b in range(2):
                    body(b, b)
                with sp.Fori(1, B // 2) as pair:
                    body(2 * pair, 0)
                    body(2 * pair + 1, 1)

            def pe(self, p):
                s = self.s
                p.wait_ge(s.VW_done, 2 * C)
                p.wait_ge(self.before.xT_done, B)
                p.wait_ge(s.A_done, 2 * C)

                def body(i, u, has, pair):
                    n = self.n0 + i
                    if has(0):
                        p.wait_ge(s.xb_done, i + 1)
                        p.wait_ge((s.beta_in0, s.beta_in1)[u], 16 * pair + 16)
                        wait(p, s.mT_done, n)
                        wait(p, self.ln.x_done, i - 1)
                        for k in range(2):
                            wait(p, s.max_done, 2 * n + k)
                            for half in range(2):
                                p.matmul(NAT[half], xb[:, u, 128 * k:128 * k + 128],
                                         A1[:, bass.ds(i, 1), 4 * half:4 * half + 4, :].rearrange("p a c n -> p (a c n)"), start=True, stop=False)
                                ins = p.matmul(NAT[half], ones_row, betaz[:, u, 512 * half:512 * half + 512], start=False, stop=True)
                            ins.then_inc(s.nat_done, 1)
                    if has(1):
                        b = i - 1
                        p.wait_ge(s.p_done, 2 * n)
                        wait(p, s.pn_done, 4 * b)
                        for k in range(2):
                            for c in range(C):
                                ins = p.matmul(ps[:, 6, 16 * k + 2 * c:16 * k + 2 * c + 2], pT[:, 1 - u, c, 128 * k:128 * k + 128],
                                               K("pair_cols"), start=True, stop=True)
                        ins.then_inc(s.sum_done, 1)
                    if has(0):
                        p.wait_ge(s.max_done, 2 * n + 2)
                        for k in range(2):
                            ins = p.transpose(MT_RAW[:, 128 * k:128 * k + 128], nmax[:, u, k, :], ident)
                        ins.then_inc(s.mT_raw, 1)
                    if has(2):
                        wait(p, self.ln.x_done, i - 1)
                        self.ln.pe_transpose(p, i - 2, u, XT_RAW)
                    if has(0):
                        for g in range(2):
                            wait(p, s.p_done, 2 * n - 1 + g)
                            p.wait_ge(s.mT_done, n + 1)
                            for c in range(4 * g, 4 * g + 4):
                                out = S4[g][:, (c % 4) // 2, 256 * (c % 2):256 * (c % 2) + 256]
                                p.matmul(out, Ab[:, u, c, :], xb[:, u, :], start=True, stop=False)
                                p.matmul(out, betaz[:, u, 128 * c:128 * c + 128], K("row0_ones"), start=False, stop=False)
                                ins = p.matmul(out, K("head_sel")[:, c, :], nmaxT[:, u, :], start=False, stop=True)
                            ins.then_inc(s.s_done, 1)
                    if has(1):
                        b = i - 1
                        p.wait_ge(s.rs_done, b + 1)
                        for k in range(2):
                            ins = p.transpose(ps[:, 7, 128 * k:128 * k + 128], rs1[:, k, :], ident)
                        ins.then_inc(s.rT_raw, 1)
                        p.wait_ge(s.rT_done, b + 1)
                        for r in range(4):
                            if r >= 2:
                                p.wait_ge(s.pn_done, 4 * b + r - 1)
                            for c in (2 * r, 2 * r + 1):
                                ins = p.matmul(ps[:, 6 + r % 2, 256 * (c % 2):256 * (c % 2) + 256], K("head_sel")[:, c, :], rsT[:, :], start=True, stop=True)
                            ins.then_inc(s.r_raw, 1)
                        wait(p, self.ln.xT_done, b)
                        p.wait_ge(s.pn_done, 4 * b + 4)
                        for k in range(2):
                            out = Y[:, 128 * k:128 * k + 128]
                            for c in range(C):
                                p.matmul(out, pT[:, 1 - u, c, 128 * k:128 * k + 128],
                                         VW[:, bass.ds(b, 1), c, :].rearrange("p a n -> p (a n)"), start=(c == 0), stop=False)
                            ins = p.matmul(out, ones_row, K("bo1"), start=False, stop=True)
                        ins.then_inc(s.y_done, 1)
                for i in range(2):
                    body(i, i % 2, lambda lag, i=i: 0 <= i - lag < B, 0)
                with p.Fori(1, B // 2) as pair:
                    body(2 * pair, 0, lambda lag: True, pair)
                    body(2 * pair + 1, 1, lambda lag: True, pair)
                for i in range(B, B + 2):
                    body(i, i % 2, lambda lag, i=i: 0 <= i - lag < B, 0)

            def act(self, a):
                s = self.s

                def body(i, u, has):
                    n = self.n0 + i
                    if has(0):
                        a.wait_ge(s.mT_raw, n + 1)
                        a.activation(nmaxT[:, u, :], MT_RAW, ACT.Copy).then_inc(s.mT_done, 1)
                    if has(2):
                        self.ln.act_xT(a, i - 2, u, XT_RAW)
                    if has(0):
                        for g in range(2):
                            a.wait_ge(s.s_done, 2 * n + g + 1)
                            wait(a, s.y_done, n - 1)
                            a.activation(pT[:, u, 4 * g:4 * g + 4, :].rearrange("p c q -> p (c q)"),
                                         S4[g].rearrange("p a n -> p (a n)"), ACT.Exp).then_inc(s.p_done, 1)
                    if has(1):
                        a.wait_ge(s.rT_raw, i)
                        a.activation(rsT[:, :], ps[:, 7, 0:256], ACT.Copy).then_inc(s.rT_done, 1)
                pipelined(a, body)

            def dve(self, v):
                s = self.s

                def body(i, u, has):
                    n = self.n0 + i
                    if has(0):
                        for k in range(2):
                            v.wait_ge(s.nat_done, 2 * n + k + 1)
                            v.tensor_reduce(nmax[:, u, k, 0:H], ps[:, 0:2, :].rearrange("p a (h k) -> p (a h) k", k=TK),
                                            X_AXIS, ALU.max, negate=True).then_inc(s.max_done, 1)
                    if has(2):
                        self.ln.dve_apply(v, i - 2, u)
                    if has(1):
                        b = i - 1
                        v.wait_ge(s.sum_done, b + 1)
                        wait(v, s.rT_raw, b)
                        v.reciprocal(rs1[:, :, 0:H], ps[:, 6, 0:32].rearrange("p (k h) -> p k h", k=2)).then_inc(s.rs_done, 1)
                        for r in range(4):
                            v.wait_ge(s.r_raw, 4 * b + r + 1)
                            part = pT[:, 1 - u, 2 * r:2 * r + 2, :].rearrange("p c q -> p (c q)")
                            v.tensor_tensor(part, part, ps[:, 6 + r % 2, :], ALU.mult).then_inc(s.pn_done, 1)
                        v.wait_ge(s.y_done, n)
                        tiles = x[:, bass.ds(2 * b, 2), :]
                        v.tensor_tensor(tiles, tiles, Y.rearrange("p (a d) -> p a d", a=2), ALU.add).then_inc(self.ln.x_done, 1)
                        v.wait_ge(self.ln.x_done, b + 1)
                        self.ln.dve_stats(v, b, 1 - u)
                pipelined(v, body)

            def pool(self, g):
                s = self.s

                def body(i, u, has):
                    n = self.n0 + i
                    if has(0):
                        g.wait_ge(self.before.xT_done, i + 1)
                        wait(g, s.s_done, 2 * n - 2)
                        if isinstance(i, int) and i == 0:
                            g.wait_ge(s.A_done, 2 * C)
                            g.wait_ge(s.VW_raw, C)
                            g.wait_ge(s.beta_out, 16 * C)
                        g.tensor_copy(xb[:, u, :], xnT[:, bass.ds(i * TQ, TQ)])
                        g.tensor_copy(Ab[:, u, :, :], A1[:, bass.ds(i, 1), :, :].rearrange("p a c n -> p (a c) n")).then_inc(s.xb_done, 1)
                    if has(1):
                        self.ln.pool_rstd(g, i - 1, 1 - u)
                    if has(2):
                        self.ln.pool_save(g, i - 2, u)
                pipelined(g, body)

        Ab = kblk[:, :, 0, :, :].rearrange("p u h k -> p u (h k)").rearrange("p u (c n) -> p u c n", c=C)

        SK = TQ
        skblk = big[:, 0:2 * H * SK].rearrange("p (u h k) -> p u h k", u=2, h=H)
        spT = big[:, 2 * H * SK:2 * H * SK + 2 * 1024].rearrange("p (u h c q) -> p u h c q", u=2, h=2, c=2)
        sq = qT
        sv = sb("sv", [128, 2, 2, H, 9])
        snmax = sb("snmax", [128, 2, 2, H])

        class SelfAttn:
            def __init__(self, before, ln):
                self.before, self.ln = before, ln
                self.s = SelfSignals()

            def pe(self, p):
                s = self.s
                NG = H // 2

                def pv(b, u, g):
                    p.wait_ge(s.p_done, NG * b + g + 1)
                    for k in range(2):
                        for j in range(2):
                            for c in range(2):
                                ins = p.matmul(ps[:, 6, 144 * k + 9 * (2 * g + j):144 * k + 9 * (2 * g + j) + 9],
                                               spT[:, g % 2, j, c, 128 * k:128 * k + 128], sv[:, u, c, 2 * g + j, :],
                                               start=(c == 0), stop=(c == 1))
                    ins.then_inc(s.pv_done, 1)

                def body(i, u, has):
                    if has(0):
                        p.wait_ge(s.xb_done, i + 1)
                        wait(p, s.v_done, i)
                        wait(p, self.ln.x_done, i - 1)
                        wait(p, self.ln.xT_done, i - 2)
                        for n, w in enumerate(("swq", "swk")):
                            ins = p.matmul(ps[:, 7, 256 * n:256 * n + 256], K(w), xb[:, u, :], start=True, stop=True)
                        ins.then_inc(s.qk_raw, 1)
                        p.wait_ge(s.qk_done, i + 1)
                        for k in range(2):
                            ins = p.matmul(ps[:, 7, 128 * k:128 * k + 128], xb[:, u, 128 * k:128 * k + 128], K("swv"), start=True, stop=True)
                        ins.then_inc(s.v_raw, 1)
                        p.wait_ge(s.kblk_done, i + 1)
                    if has(1):
                        b = i - 1
                        p.wait_ge(s.on_done, 2 * b + 2)
                        if has(0):
                            p.wait_ge(s.v_done, i + 1)
                        wait(p, self.ln.x_done, b)
                        wait(p, self.ln.xT_done, b - 1)
                        for k in range(2):
                            ins = p.transpose(ps[:, 7, 128 * k:128 * k + 128], on[:, k, 0, :], ident)
                        ins.then_inc(s.oT_raw, 1)
                        p.wait_ge(s.oT_done, b + 1)
                        for k in range(2):
                            out = ps[:, 7, 256 + 128 * k:256 + 128 * k + 128]
                            p.matmul(out, oT[:, 0, 128 * k:128 * k + 128], K("swo"), start=True, stop=False)
                            ins = p.matmul(out, ones_row, K("sbo"), start=False, stop=True)
                        ins.then_inc(s.y_done, 1)
                    if has(0):
                        for g in range(NG + 1):
                            if g < NG:
                                for k in range(2):
                                    wait(p, s.max_done, 2 * (NG * i + g) + k - 1)
                                    p.matmul(ps[:, k, :], sq[:, u, 0, 128 * k:128 * k + 128],
                                             skblk[:, u, 2 * g:2 * g + 2, :].rearrange("p h k -> p (h k)"), start=True, stop=True).then_inc(s.nat_done, 1)
                            if g >= 1:
                                h0 = 2 * (g - 1)
                                wait(p, s.p_done, NG * i + g - 2)
                                p.wait_ge(s.max_done, 2 * (NG * i + g))
                                for j in range(2):
                                    for c in range(2):
                                        out = ps[:, 2 + 2 * ((g - 1) % 2) + j, 256 * c:256 * c + 256]
                                        for k in range(2):
                                            p.matmul(out[:, 128 * k:128 * k + 128], skblk[:, u, h0 + j, 128 * c:128 * c + 128],
                                                     sq[:, u, 0, 128 * k:128 * k + 128], start=True, stop=False)
                                            ins = p.matmul(out[:, 128 * k:128 * k + 128], snmax[:, u, k, h0 + j:h0 + j + 1].to_broadcast([128, 128]),
                                                           ident, start=False, stop=True)
                                ins.then_inc(s.s_done, 1)
                                if g == 2:
                                    wait(p, s.on_done, 2 * i)
                                if g >= 2:
                                    pv(i, u, g - 2)
                        pv(i, u, NG - 1)
                    if has(2):
                        wait(p, self.ln.x_done, i if has(1) else i - 1)
                        wait(p, self.ln.xT_done, i - 2)
                        self.ln.pe_transpose(p, i - 2, u, ps[:, 7, 0:256])
                pipelined(p, body)

            def act(self, a):
                s = self.s
                NG = H // 2

                def body(i, u, has):
                    if has(0):
                        a.wait_ge(s.qk_raw, i + 1)
                        wait(a, s.s_done, NG * (i - 1))
                        a.activation(sq[:, u, :, :].rearrange("p a q -> p (a q)"), ps[:, 7, :], ACT.Copy).then_inc(s.qk_done, 1)
                        a.wait_ge(s.v_raw, i + 1)
                        wait(a, s.pv_done, NG * (i - 1))
                        a.activation(sv[:, u, :, :, 0:8].rearrange("p c h d -> p c h d"),
                                     ps[:, 7, 0:256].rearrange("p (c h d) -> p c h d", c=2, h=H), ACT.Copy).then_inc(s.v_done, 1)
                    if has(1):
                        a.wait_ge(s.oT_raw, i)
                        a.activation(oT[:, 0, :], ps[:, 7, 0:256], ACT.Copy).then_inc(s.oT_done, 1)
                    if has(0):
                        for g in range(NG):
                            a.wait_ge(s.s_done, NG * i + g + 1)
                            wait(a, s.pv_done, NG * i + g - 1)
                            a.activation(spT[:, g % 2, :, :, :].rearrange("p h c q -> p (h c q)"),
                                         ps[:, 2 + 2 * (g % 2):4 + 2 * (g % 2), :].rearrange("p a n -> p (a n)"), ACT.Exp).then_inc(s.p_done, 1)
                    if has(2):
                        self.ln.act_xT(a, i - 2, u, ps[:, 7, 0:256])
                pipelined(a, body)

            def dve(self, v):
                s = self.s
                NG = H // 2
                v.memset(sv[:, :, :, :, 8:9], 1.0).then_inc(s.ones, 1)

                def body(i, u, has):
                    if has(1):
                        b = i - 1
                        v.wait_ge(s.y_done, b + 1)
                        v.tensor_tensor(res[:, bass.ds(2 * b, 2), :], xn[:, bass.ds(2 * b, 2), :],
                                        ps[:, 7, 256:512].rearrange("p (a d) -> p a d", a=2), ALU.add).then_inc(self.ln.x_done, 1)
                        v.wait_ge(self.ln.x_done, b + 1)
                        self.ln.dve_stats(v, b, 1 - u)
                    if has(0):
                        for g in range(NG):
                            for k in range(2):
                                v.wait_ge(s.nat_done, 2 * (NG * i + g) + k + 1)
                                v.tensor_reduce(snmax[:, u, k, 2 * g:2 * g + 2], ps[:, k, :].rearrange("p (h k) -> p h k", h=2),
                                                X_AXIS, ALU.max, negate=True).then_inc(s.max_done, 1)
                    if has(1):
                        self.ln.dve_apply(v, i - 1, 1 - u)
                    if has(0):
                        v.wait_ge(s.pv_done, NG * i + NG)
                        wait(v, s.oT_raw, i)
                        for k in range(2):
                            o = ps[:, 6, 144 * k:144 * k + 144].rearrange("p (h n) -> p h n", h=H)
                            v.reciprocal(rsum[:, k, :].unsqueeze(2), o[:, :, 8:9]).then_inc(s.rsum_done, 1)
                            v.wait_ge(s.rsum_done, 2 * i + k + 1)
                            v.tensor_tensor(on[:, k, 0, :].rearrange("p (h d) -> p h d", h=H), o[:, :, 0:8],
                                            rsum[:, k, :].unsqueeze(2).to_broadcast([128, H, HD]), ALU.mult).then_inc(s.on_done, 1)
                pipelined(v, body)

            def pool(self, g):
                s = self.s

                def body(i, u, has):
                    if has(0):
                        g.wait_ge(self.before.xT_done, i + 1)
                        if not (isinstance(i, int) and i < 2):
                            g.wait_ge(s.v_raw, i - 1)
                        g.tensor_copy(xb[:, u, :], xnT[:, bass.ds(i * TQ, TQ)]).then_inc(s.xb_done, 1)
                        if not (isinstance(i, int) and i < 2):
                            g.wait_ge(s.s_done, 8 * i - 8)
                        g.wait_ge(s.qk_done, i + 1)
                        g.tensor_tensor(skblk[:, u, :, :], sq[:, u, 1, :].unsqueeze(1).to_broadcast([128, H, SK]),
                                        K("head_mask").unsqueeze(2).to_broadcast([128, H, SK]), ALU.mult).then_inc(s.kblk_done, 1)
                    if has(1):
                        self.ln.pool_rstd(g, i - 1, 1 - u)
                    if has(2):
                        self.ln.pool_save(g, i - 2, u)
                pipelined(g, body)

        wq3 = sb("wq3", [128, D])
        tern = sb("tern", [128, 4])
        yT3 = qT[:, 0, :, :]

        class Ternary:
            def __init__(self, before):
                self.before = before
                self.s = TernarySignals()

            def dve_prepare(self, v):
                s = self.s
                v.tensor_reduce(tern[:, 0:1], K("w3"), X_AXIS, ALU.add, apply_absolute_value=True).then_inc(s.abs_done, 1)
                v.wait_ge(s.sum_done, 1)
                v.tensor_scalar(tern[:, 1:2], ps[:, 3, 0:1], 1.0 / (D * D), 0.7, ALU.mult, ALU.mult).then_inc(s.chain, 1)
                v.wait_ge(s.chain, 1)
                v.tensor_scalar(tern[:, 2:3], tern[:, 1:2], -1.0, None, ALU.mult).then_inc(s.chain, 1)
                v.tensor_scalar(wq3[:, :], K("w3"), tern[:, 1:2], None, ALU.is_gt).then_inc(s.chain, 1)
                v.wait_ge(s.chain, 3)
                v.tensor_scalar(b2blk[:, 0, :], K("w3"), tern[:, 2:3], None, ALU.is_lt).then_inc(s.chain, 1)
                v.wait_ge(s.chain, 4)
                v.tensor_tensor(wq3[:, :], wq3[:, :], b2blk[:, 0, :], ALU.subtract).then_inc(s.chain, 1)
                v.wait_ge(s.chain, 5)
                v.tensor_scalar(wq3[:, :], wq3[:, :], K("alpha"), None, ALU.mult).then_inc(s.w_done, 1)

            def pe_prepare(self, p):
                s = self.s
                p.wait_ge(s.abs_done, 1)
                p.matmul(ps[:, 3, 0:1], K("all_ones"), tern[:, 0:1], start=True, stop=True).then_inc(s.sum_done, 1)

            def pe(self, p):
                s = self.s
                p.wait_ge(s.w_done, 1)

                def body(i, u, has):
                    if has(0):
                        p.wait_ge(self.before.xT_done, i + 1)
                        wait(p, s.o_done, i - 1)
                        p.matmul(ps[:, 2 + u, 0:256], wq3[:, :], xnT[:, bass.ds(i * TQ, TQ)], start=True, stop=True).then_inc(s.o_raw, 1)
                    if has(1):
                        p.wait_ge(s.o_done, i)
                        wait(p, s.x_done, i - 1)
                        for k in range(2):
                            ins = p.transpose(ps[:, 4, 128 * k:128 * k + 128], yT3[:, 1 - u, 128 * k:128 * k + 128], ident)
                        ins.then_inc(s.t_done, 1)
                pipelined(p, body)

            def act(self, a):
                s = self.s

                def body(i, u, has):
                    if has(0):
                        a.wait_ge(s.o_raw, i + 1)
                        wait(a, s.t_done, i - 1)
                        a.activation(yT3[:, u, :], ps[:, 2 + u, 0:256], ACT.Identity, bias=K("b3")).then_inc(s.o_done, 1)
                pipelined(a, body)

            def dve(self, v):
                s = self.s

                def body(i, u, has):
                    if has(1):
                        v.wait_ge(s.t_done, i)
                        tiles = x[:, bass.ds(2 * (i - 1), 2), :]
                        v.tensor_tensor(tiles, tiles, ps[:, 4, 0:256].rearrange("p (a d) -> p a d", a=2), ALU.add).then_inc(s.x_done, 1)
                pipelined(v, body)

            def sync(self, sp):
                s = self.s
                for b in range(B):
                    sp.wait_ge(s.x_done, b + 1)
                    sp.dma_start(t["out"][:, 2 * b:2 * b + 2, :], x[:, 2 * b:2 * b + 2, :]).then_inc(s.out_done, 16)
                sp.wait_ge(s.out_done, 16 * B)

        ln0 = Norm("ln0", x, 1e-5)
        first = NormPhase(ln0)
        ln_a = Norm("ln_after_x0", x, 1e-5)
        a0 = XAttn(0, 0, ln0, ln_a)
        m0 = Moe(0, ln_a, ACT.Gelu, x)
        ln_b = Norm("ln_after_m0", x, 1e-5)
        nb = NormPhase(ln_b, dve_after=[(m0.s.acc_done, 1 * 4 * G * E)], pe_after=[(m0.s.gelu_done, 1 * FC * G * E)])
        ln_c = Norm("ln_after_wide", x, 1e-5, keep=xn)
        wide = Wide(ln_b, ln_c)
        ln_d = Norm("ln1", res, 1e-6, affine=("ln1_g", "ln1_b"), keep=res)
        selfa = SelfAttn(ln_c, ln_d)
        m1 = Moe(1, ln_d, ACT.Gelu, res)
        ln_e = Norm("ln2", res, 1e-6, affine=("ln2_g", "ln2_b"))
        ne = NormPhase(ln_e, add_to=x, dve_after=[(m1.s.acc_done, 2 * 4 * G * E)])
        ln_f = Norm("ln_after_m1", x, 1e-5)
        nf = NormPhase(ln_f, dve_after=[(xT_raw, ln_e.n0 + B)], pe_after=[(m1.s.gelu_done, 2 * FC * G * E)])
        a2 = XAttn(2, 1, ln_f, Norm("ln_after_x2", x, 1e-5, keep=xn), [(m1.s.gelu_done, 2 * FC * G * E), (m1.s.acc_done, 2 * 4 * G * E)])
        ln_g = Norm("ln_inner", xn, 1e-5, affine=("lnw", "lnb"))
        m2 = Moe(2, a2.ln, ACT.Gelu_apprx_tanh, x)
        ng = NormPhase(ln_g, pe_after=[(a2.ln.xT_done, B)], act_after=[(m2.s.logits, 3)], dve_after=[(a2.ln.saved, B)])
        ln_h = Norm("ln_after_m2", x, 1e-5)
        nh = NormPhase(ln_h, dve_after=[(m2.s.acc_done, 3 * 4 * G * E)], pe_after=[(m2.s.gelu_done, 3 * FC * G * E)])
        a3 = XAttn(3, 2, ln_h, Norm("ln_after_x3", x, 1e-5), [(m2.s.gelu_done, 3 * FC * G * E), (m2.s.acc_done, 3 * 4 * G * E)])
        fin = Ternary(a3.ln)

        block = ctx.enter_context(nc.Block())

        @block.sync
        def _(sp):
            sp.dma_start(cw[:, :], t["cols"]).then_inc(in_cw, 16)
            sp.dma_start(x[:, :, :], t["x"]).then_inc(in_x, 16)
            m0.sync(sp)
            sp.wait_ge(m0.s.b2_raw, 4)
            sp.wait_ge(m0.s.acc_done, 1 * 4 * G * E)
            wide.sync_prepare(sp)
            wide.sync(sp)
            sp.wait_ge(m0.s.fc2_done, 1 * G * E)
            m1.sync(sp)
            sp.wait_ge(m1.s.fc2_done, 2 * G * E)
            m2.sync(sp)
            fin.sync(sp)

        @block.vector
        def _(v):
            v.wait_ge(in_cw, 16)
            v.memset(nmax[:, :, :, :], 0.0).then_inc(nf_done, 1)
            v.wait_ge(nf_done, 1)
            v.tensor_scalar(nfmb[:, 0:1], K("fmb"), -1.0, None, ALU.mult).then_inc(nf_done, 1)
            v.wait_ge(in_x, 16)
            a0.dve_prepare(v)
            first.dve(v)
            a0.dve(v)
            m0.dve_logits(v)
            m0.top2(v)
            m0.capacity(v)
            m0.pair_probs(v, 1)
            m0.combine(v)
            m0.dve_init(v)
            m0.dve(v)
            wide.dve_prepare(v)
            nb.dve(v)
            wide.dve(v)
            selfa.dve(v)
            m1.probs(v)
            m1.top2(v)
            m1.pair_probs(v, 2)
            m1.combine(v)
            m1.dve_init(v)
            m1.dve(v)
            ne.dve(v)
            a2.dve_prepare(v)
            nf.dve(v)
            a2.dve(v)
            m2.probs(v)
            ng.dve(v)
            m2.dve_threshold(v)
            m2.dve_init(v)
            m2.dve(v)
            a3.dve_prepare(v)
            nh.dve(v)
            a3.dve(v)
            fin.dve_prepare(v)
            fin.dve(v)

        @block.tensor
        def _(p):
            p.wait_ge(in_cw, 16)
            a0.pe_prepare(p)
            first.pe(p)
            a0.pe(p)
            m0.pe_logits(p)
            m0.pe_prefix(p)
            m0.pe_init(p)
            m0.pe(p)
            wide.pe_prepare(p)
            nb.pe(p)
            wide.pe(p)
            selfa.pe(p)
            m1.pe_logits(p)
            m1.pe_init(p)
            m1.pe(p)
            a2.pe_prepare(p)
            nf.pe(p)
            a2.pe(p)
            m2.pe_logits(p)
            ng.pe(p)
            m2.pe_threshold(p)
            m2.pe_init(p)
            m2.pe(p)
            a3.pe_prepare(p)
            nh.pe(p)
            a3.pe(p)
            fin.pe_prepare(p)
            fin.pe(p)

        @block.scalar
        def _(a):
            a.wait_ge(in_cw, 16)
            a0.act_prepare(a)
            first.act(a)
            a0.act(a)
            m0.act_pair(a, 1)
            m0.act(a)
            wide.act_prepare(a)
            nb.act(a)
            wide.act(a)
            selfa.act(a)
            m1.act_probs(a)
            m1.act_pair(a, 2)
            m1.act(a)
            a2.act_prepare(a)
            nf.act(a)
            a2.act(a)
            m2.act_probs(a)
            ng.act(a)
            m2.act(a)
            a3.act_prepare(a)
            nh.act(a)
            a3.act(a)
            fin.act(a)

        @block.gpsimd
        def _(g):
            g.wait_ge(in_cw, 16)
            first.pool(g)
            a0.pool(g)
            g.wait_ge(a0.s.y_done, B)
            m0.pool_b2(g)
            nb.pool(g)
            wide.pool(g)
            g.wait_ge(wide.s.y_done, 2 * B)
            m1.pool_b2(g)
            selfa.pool(g)
            ne.pool(g)
            nf.pool(g)
            a2.pool(g)
            g.wait_ge(a2.s.y_done, 3 * B)
            m2.pool_b2(g)
            ng.pool(g)
            nh.pool(g)
            a3.pool(g)


def kernel(**inputs):
    import concourse.bacc as bacc
    from concourse.bass_utils import run_bass_kernel_spmd as run

    a = {k: np.ascontiguousarray(v) for k, v in inputs.items()}
    cols = packs()
    cp = np.zeros((128, cols.width), np.float32)

    def put(pack, arr, name, value):
        off, shape = pack.at[name]
        n = int(np.prod(shape))
        v = np.asarray(value).reshape(value.shape[0], n)
        arr[0:v.shape[0], off:off + n] = v

    d = np.arange(128)
    put(cols, cp, "ident", np.eye(128, dtype=np.float32))
    in_head = (d[:, None] // HD == np.arange(H)[None, :]).astype(np.float32)
    put(cols, cp, "head_mask", in_head * np.float32(HD ** -0.5))
    put(cols, cp, "feat_mask", in_head * np.float32(D ** -0.5))
    put(cols, cp, "head_sel", (np.arange(H)[:, None, None] == 2 * np.arange(C)[None, :, None] + (d // TK)[None, None, :]).astype(np.float32))
    put(cols, cp, "minus_half", np.full((128, 2), -0.5, np.float32))
    ctxT = a["ctx_1024"].transpose(2, 0, 1)
    put(cols, cp, "ctxT2", np.stack([ctxT, ctxT], axis=2))
    put(cols, cp, "wq0", a["L0_xattn_Wq"].T)
    put(cols, cp, "wk0", a["L0_xattn_Wk"].T)
    put(cols, cp, "wv0", a["L0_xattn_Wv"].T)
    put(cols, cp, "wo0", a["L0_xattn_Wo"].T)
    put(cols, cp, "bq0", a["L0_xattn_bq"][:, None])
    put(cols, cp, "bk0", a["L0_xattn_bk"][:, None])
    put(cols, cp, "wq2", a["L2_xattn_Wq"])
    put(cols, cp, "wk2", a["L2_xattn_Wkv"][:, 0::2])
    put(cols, cp, "wv2", a["L2_xattn_Wkv"][:, 1::2])
    put(cols, cp, "wo2", a["L2_xattn_Wout"])
    put(cols, cp, "bq2", a["L2_xattn_bq"][:, None])
    put(cols, cp, "bk2", a["L2_xattn_bkv"][0::2][:, None])
    fm = np.zeros((128, 128), np.float32)
    for h in range(H):
        fm[HD * h:HD * h + HD, HD * h:HD * h + HD] = a["L3_xattn_fm_w"].T
    put(cols, cp, "fm", fm)
    put(cols, cp, "fmb", np.tile(a["L3_xattn_fm_b"], H)[:, None])
    put(cols, cp, "fcw", a["L3_xattn_fc_w"].reshape(D, H, 2, HD).transpose(1, 3, 2, 0).reshape(128, 2 * D))
    put(cols, cp, "row0_ones", np.ones((1, TQ), np.float32))
    put(cols, cp, "bv0", a["L0_xattn_bv"][None])
    put(cols, cp, "bo0", a["L0_xattn_bo"][None])
    put(cols, cp, "bv2", a["L2_xattn_bkv"][1::2][None])
    put(cols, cp, "bo2", a["L2_xattn_bout"][None])
    put(cols, cp, "fmb_row", np.tile(a["L3_xattn_fm_b"], H)[None])
    put(cols, cp, "fcb", a["L3_xattn_fc_b"][None])
    put(cols, cp, "gate0", a["L0_ffn_gate_w"])
    put(cols, cp, "gate1", a["L1_ffn_Wr"])
    put(cols, cp, "gate2", a["L2_ffn_gate_w"].T)
    b2 = [a["L0_ffn_proj_bias"].reshape(E, D), a["L1_ffn_be2"], a["L2_ffn_b2s"]]
    for L in range(3):
        put(cols, cp, f"b2_{L}", np.tile(b2[L], (NT, 1)))
    put(cols, cp, "tile_mask", (d[:, None] // E == np.arange(NT)[None]).astype(np.float32))
    put(cols, cp, "descending", np.tile(np.arange(E, 0, -1, dtype=np.float32), (128, 1)))
    put(cols, cp, "before", (d[:, None] < d[None]).astype(np.float32))
    put(cols, cp, "all_ones", np.ones((128, 128), np.float32))
    put(cols, cp, "same_expert", (d[:, None] % E == d[None] % E).astype(np.float32))
    put(cols, cp, "earlier_tile", ((d[:, None] % E == d[None] % E) & (d[:, None] // E < d[None] // E)).astype(np.float32))
    for n, w in (("swq", "Wq"), ("swk", "Wk"), ("swv", "Wv"), ("swo", "Wo")):
        put(cols, cp, n, a[f"L1_ffn_{w}"])
    put(cols, cp, "sbo", a["L1_ffn_bo"][None])
    for n in ("ln1_g", "ln1_b", "ln2_g", "ln2_b"):
        put(cols, cp, n, np.tile(a[f"L1_ffn_{n}"][None], (128, 1)))
    put(cols, cp, "lnw", np.tile(a["L2_ffn_ln_w"][None], (128, 1)))
    put(cols, cp, "lnb", np.tile(a["L2_ffn_ln_b"][None], (128, 1)))
    for n in ("bq", "bk", "bv"):
        put(cols, cp, n + "1", a[f"L1_xattn_{n}"].reshape(C, 128).T)
    put(cols, cp, "bo1", a["L1_xattn_bo"][None])
    put(cols, cp, "pair_cols", (d[:, None] // TK == np.arange(2)[None]).astype(np.float32))
    put(cols, cp, "w3", a["L3_ffn_weight"].T)
    put(cols, cp, "alpha", np.tile(a["L3_ffn_alpha"][None], (128, 1)))
    put(cols, cp, "b3", a["L3_ffn_bias"][:, None])
    by_rows = lambda w: w.reshape(C, 128, D).transpose(1, 0, 2).reshape(128, C * D)
    wide_w = np.stack([by_rows(a["L1_xattn_Wq"]), a["L1_xattn_Wk"].T, a["L1_xattn_Wv"].T, by_rows(a["L1_xattn_Wo"].T)], axis=1)

    def first_weights(w, b):
        return np.concatenate([w, b.reshape(E, FC, 128).transpose(0, 2, 1)], axis=2)

    def second_weights(w):
        return w.reshape(E, FC, 128, D).transpose(0, 2, 1, 3).reshape(E, 128, F)

    arrays = {"wide_w": wide_w, "mask": a["mask_BxS2_bk0"].reshape(1, B * TK),
              "w1_0": first_weights(a["L0_ffn_c_fc"], a["L0_ffn_fc_bias"].reshape(E, F)), "w2_0": second_weights(a["L0_ffn_c_proj"]),
              "w1_1": first_weights(a["L1_ffn_We1"], a["L1_ffn_be1"]), "w2_1": second_weights(a["L1_ffn_We2"]),
              "w1_2": first_weights(a["L2_ffn_fc1s"].transpose(0, 2, 1), a["L2_ffn_b1s"]),
              "w2_2": second_weights(a["L2_ffn_fc2s"].transpose(0, 2, 1)),
              "cols": cp, "x": np.ascontiguousarray(a["x"].reshape(NT, 128, D).transpose(1, 0, 2))}

    arrays = {k: np.ascontiguousarray(v) for k, v in arrays.items()}
    nc = bacc.Bacc("TRN2", target_bir_lowering=False, num_devices=1)
    t = {k: nc.dram_tensor(f"in_{k}", v.shape, mybir.dt.from_np(v.dtype), kind="ExternalInput").ap() for k, v in arrays.items()}
    t["out"] = nc.dram_tensor("out_x", (128, NT, D), F32, kind="ExternalOutput").ap()
    build(nc, t)
    got = run(nc, [{f"in_{k}": v for k, v in arrays.items()}], core_ids=[0]).results[0]["out_x"]
    return np.ascontiguousarray(got.transpose(1, 0, 2)).reshape(B, TQ, D)
```

```python
from contextlib import ExitStack

import numpy as np
import concourse.bass as bass
from concourse import mybir

F32 = mybir.dt.float32
F32R = mybir.dt.float32r
I32 = mybir.dt.int32
ALU = mybir.AluOpType
ACT = mybir.ActivationFunctionType
X_AXIS = mybir.AxisListType.X

B, TQ, D = 8, 256, 128
N = B * TQ
NT = N // 128
TK = 64
H, HD = 16, 8
C = H // 2
HD1 = 64
E, F = 8, 512
FC = F // 128
CAP0 = int(1.25 * N * 2 / E)
TOP2 = N // E


def wait(eng, sem, value):
    if isinstance(value, int) and value <= 0:
        return
    eng.wait_ge(sem, value)


def pipelined(eng, body, lags=2):
    peeled = lags + lags % 2
    for i in range(peeled):
        body(i, i % 2, lambda lag, i=i: 0 <= i - lag < B)
    with eng.Fori(peeled // 2, B // 2) as pair:
        body(2 * pair, 0, lambda lag: True)
        body(2 * pair + 1, 1, lambda lag: True)
    for i in range(B, B + lags):
        body(i, i % 2, lambda lag, i=i: 0 <= i - lag < B)


class Pack:

    def __init__(self, rows):
        self.rows, self.at, self.width, self.first = rows, {}, 0, 0

    def add(self, name, *shape):
        n = int(np.prod(shape))
        self.at[name] = (self.width, shape)
        self.width += n

    def view(self, tensor, name, parts=None):
        off, shape = self.at[name]
        n = int(np.prod(shape))
        v = tensor[0:parts or self.rows, off:off + n]
        if len(shape) == 2:
            v = v.rearrange("p (a b) -> p a b", a=shape[0])
        elif len(shape) == 3:
            v = v.rearrange("p (a b c) -> p a b c", a=shape[0], b=shape[1])
        return v


def packs():
    cols = Pack(128)
    cols.add("ident", 128)
    cols.add("ctxT2", B, 2, TK)
    for n in ("bq0", "bk0", "bq2", "bk2"):
        cols.add(n, 4)
    cols.add("fmb", 1)
    cols.add("minus_half", 2)
    cols.add("bv0", D)
    cols.add("bo0", D)
    cols.add("split_sign", 2)
    cols.add("split_all", 2)
    cols.add("quad_mask", 4)
    cols.add("row0_ones", TQ)
    cols.first = cols.width
    cols.add("gate0", E)
    cols.add("gate1", E)
    cols.add("gate2", E)
    for L in range(3):
        cols.add(f"b2_{L}", D)
    cols.add("tile_mask", NT)
    cols.add("descending", E)
    cols.add("before", 128)
    cols.add("all_ones", 128)
    cols.add("same_expert", 128)
    cols.add("earlier_tile", 128)
    for w in ("sqp", "skp"):
        cols.add(w, 4, 128)
    for w in ("swv", "swo"):
        cols.add(w, D)
    cols.add("sbo", D)
    for n in ("ln1_g", "ln1_b", "ln2_g", "ln2_b", "lnw", "lnb"):
        cols.add(n, D)
    cols.add("bk1", C)
    cols.add("bv1", C)
    cols.add("bq1", C)
    cols.add("bo1", D)
    cols.add("pair_rows", 62)
    cols.add("rec_sign", 1)
    cols.add("rec_all", 1)
    cols.add("w3", D)
    cols.add("alpha", 1)
    cols.add("b3", 1)
    cols.add("rows01_ones", TQ)
    for n in ("bv2", "bo2", "fmb_row", "fcb"):
        cols.add(n, D)
    return cols


def build(nc, t):
    cols = packs()
    with ExitStack() as ctx:
        def sb(name, shape, dt=F32):
            return ctx.enter_context(nc.sbuf_tensor(name, shape, dt))

        def sem(name):
            return ctx.enter_context(nc.semaphore(name))

        ps = ctx.enter_context(nc.psum_tensor("ps", [128, 8, 512], F32))
        cw = sb("cw", [128, cols.width])
        x = sb("x", [128, NT, D])
        xn = sb("xn", [128, NT, D])
        xnT = sb("xnT", [128, N])
        K = lambda n, parts=None: cols.view(cw, n, parts)
        ident = K("ident")
        ones_row = K("row0_ones")[:, 0:128]

        kT = sb("kT", [128, 2, B * TK])
        big = sb("big", [128, 2 * B * C * 128])
        kblk = sb("kblk", [128, 2, 2, H, TK])
        nmax = sb("nmax", [128, 2, 2, 128])
        nmaxT = sb("nmaxT", [128, 2, TQ], F32R)
        pT = sb("pT", [128, 2, C, TQ])
        rsum = sb("rsum", [128, 2, H])
        on = sb("on", [128, 2, 2, D])
        oT = sb("oT", [128, 2, TQ])
        stats = sb("stats", [128, 2, 2, 6])
        xs = sb("xs", [128, 2, 2, D])
        mv = sb("mv", [128, 2, 2, 2])
        rstd = sb("rstd", [128, 2, 2])

        in_cw, in_rest, in_x, in_sel = sem("in_cw"), sem("in_rest"), sem("in_x"), sem("in_sel")
        passed, passed_pool = sem("passed"), sem("passed_pool")

        class AttnSignals:

            def __init__(self):
                self.w_in = sem("attn_w_in")
                self.k_raw = sem("attn_k_raw")
                self.k_done = sem("attn_k_done")
                self.k_upper = sem("attn_k_upper")
                self.k_split = sem("attn_k_split")
                self.v_raw = sem("attn_v_raw")
                self.v_done = sem("attn_v_done")
                self.v_zeroing = sem("attn_v_zeroing")
                self.v_zero = sem("attn_v_zero")
                self.v_now_done = sem("attn_v_now_done")
                self.kb_done = sem("attn_kb_done")
                self.q_raw = sem("attn_q_raw")
                self.raw_done = sem("attn_raw_done")
                self.q_upper = sem("attn_q_upper")
                self.q_split = sem("attn_q_split")
                self.nat_done = sem("attn_nat_done")
                self.max_done = sem("attn_max_done")
                self.mT_raw = sem("attn_mT_raw")
                self.mT_done = sem("attn_mT_done")
                self.s_done = sem("attn_s_done")
                self.p_done = sem("attn_p_done")
                self.pv_done = sem("attn_pv_done")
                self.acc_out = sem("attn_acc_out")
                self.o_done = sem("attn_o_done")
                self.rsum_done = sem("attn_rsum_done")
                self.on_done = sem("attn_on_done")
                self.oT_raw = sem("attn_oT_raw")
                self.oT_done = sem("attn_oT_done")
                self.y_done = sem("attn_y_done")

        class MoeSignals:

            def __init__(self):
                self.logits = sem("moe_logits")
                self.logits_read = sem("moe_logits_read")
                self.exp_out = sem("moe_exp_out")
                self.chain = sem("moe_chain")
                self.gates_done = sem("moe_gates_done")
                self.gT_raw = sem("moe_gT_raw")
                self.gT_done = sem("moe_gT_done")
                self.b2_done = sem("moe_b2_done")
                self.b2_raw = sem("moe_b2_raw")
                self.init_done = sem("moe_init_done")
                self.fc1_chunk = sem("moe_fc1_chunk")
                self.gelu_done = sem("moe_gelu_done")
                self.fc2_done = sem("moe_fc2_done")
                self.acc_done = sem("moe_acc_done")
                self.w1_in0 = sem("moe_w1_in0")
                self.w1_in1 = sem("moe_w1_in1")
                self.w2_in0 = sem("moe_w2_in0")
                self.w2_in1 = sem("moe_w2_in1")
                self.picked = sem("moe_picked")
                self.prefix = sem("moe_prefix")
                self.probs_done = sem("moe_probs_done")
                self.cand_done = sem("moe_cand_done")
                self.counted = sem("moe_counted")
                self.summed = sem("moe_summed")
                self.ok_done = sem("moe_ok_done")
                self.thr_done = sem("moe_thr_done")
                self.bit_done = sem("moe_bit_done")
                self.ties_counted = sem("moe_ties_counted")

        class WideSignals:

            def __init__(self):
                self.w_in = sem("wide_w_in")
                self.mask_in = sem("wide_mask_in")
                self.keep_done = sem("wide_keep_done")
                self.zero = sem("wide_zero")
                self.kv_raw = sem("wide_kv_raw")
                self.kv_done = sem("wide_kv_done")
                self.kv_masked = sem("wide_kv_masked")
                self.beta_raw = sem("wide_beta_raw")
                self.beta_done = sem("wide_beta_done")
                self.beta_out = sem("wide_beta_out")
                self.A_raw = sem("wide_A_raw")
                self.A_done = sem("wide_A_done")
                self.VW_raw = sem("wide_VW_raw")
                self.VW_done = sem("wide_VW_done")
                self.beta_in0 = sem("wide_beta_in0")
                self.beta_in1 = sem("wide_beta_in1")
                self.xb_done = sem("wide_xb_done")
                self.sum_done = sem("wide_sum_done")
                self.rs_done = sem("wide_rs_done")
                self.rec_done = sem("wide_rec_done")
                self.beta_back = sem("wide_beta_back")
                self.part_done = sem("wide_part_done")
                self.parts_out = sem("wide_parts_out")
                self.beta_r_done = sem("wide_beta_r_done")
                self.upper_done = sem("wide_upper_done")
                self.r_raw = sem("wide_r_raw")
                self.pn_done = sem("wide_pn_done")
                self.nat_done = attn_signals.nat_done
                self.max_done = attn_signals.max_done
                self.mT_raw = attn_signals.mT_raw
                self.mT_done = attn_signals.mT_done
                self.s_done = attn_signals.s_done
                self.p_done = attn_signals.p_done
                self.y_done = attn_signals.y_done

        class SelfSignals:

            def __init__(self):
                self.ones = sem("self_ones")
                self.xb_done = sem("self_xb_done")
                self.qk_raw = sem("self_qk_raw")
                self.raw_done = sem("self_raw_done")
                self.upper_done = sem("self_upper_done")
                self.split_done = sem("self_split_done")
                self.v_raw = sem("self_v_raw")
                self.v_done = sem("self_v_done")
                self.kblk_done = sem("self_kblk_done")
                self.nat_done = sem("self_nat_done")
                self.max_done = sem("self_max_done")
                self.mT_raw = sem("self_mT_raw")
                self.mT_done = sem("self_mT_done")
                self.s_done = sem("self_s_done")
                self.p_done = sem("self_p_done")
                self.pv_done = sem("self_pv_done")
                self.acc_out = sem("self_acc_out")
                self.o_done = sem("self_o_done")
                self.on_done = sem("self_on_done")
                self.rsum_done = sem("self_rsum_done")
                self.oT_raw = sem("self_oT_raw")
                self.oT_done = sem("self_oT_done")
                self.y_done = sem("self_y_done")

        class TernarySignals:

            def __init__(self):
                self.abs_done = sem("tern_abs_done")
                self.sum_done = sem("tern_sum_done")
                self.w_done = sem("tern_w_done")
                self.chain = sem("tern_chain")
                self.o_raw = sem("tern_o_raw")
                self.o_done = sem("tern_o_done")
                self.t_done = sem("tern_t_done")
                self.x_done = sem("tern_x_done")
                self.out_done = sem("tern_out_done")

        attn_signals, moe_signals = AttnSignals(), MoeSignals()
        norms = [0]
        stats_done, aggr_done, eps_done = sem("ln_stats_done"), sem("ln_aggr_done"), sem("ln_eps_done")
        rstd_done, xn_done, xT_raw = sem("ln_rstd_done"), sem("ln_xn_done"), sem("ln_xT_raw")

        class Norm:

            def __init__(self, name, src, eps, affine=None, keep=None, residual=True):
                self.xT_done = sem(f"{name}_xT_done")
                if residual:
                    self.x_done = sem(f"{name}_x_done")
                if affine:
                    self.scaled, self.shifted = sem(f"{name}_scaled"), sem(f"{name}_shifted")
                if keep is not None:
                    self.saved = sem(f"{name}_saved")
                self.n0 = B * norms[0]
                norms[0] += 1
                self.src, self.eps, self.affine, self.keep = src, eps, affine, keep

            def tile(self, n):
                return self.src[:, bass.ds(n, 1), :].rearrange("p a d -> p (a d)")

            def dve_stats(self, v, b, u):
                v.wait_ge(in_x, 16)
                wait(v, rstd_done, self.n0 + b)
                v.sem_inc(passed, 1)
                for k in range(2):
                    v.bn_stats(stats[:, u, k, :], self.tile(2 * b + k)).then_inc(stats_done, 1)
                for k in range(2):
                    v.wait_ge(stats_done, 2 * (self.n0 + b) + k + 1)
                    v.sem_inc(passed, 1)
                    v.bn_aggr(mv[:, u, k, :], stats[:, u, k, :]).then_inc(aggr_done, 1)

            def pool_rstd(self, g, b, u):
                g.wait_ge(aggr_done, 2 * (self.n0 + b) + 2)
                g.sem_inc(passed_pool, 1)
                g.tensor_scalar(rstd[:, u, :], mv[:, u, :, 1], self.eps, None, ALU.add).then_inc(eps_done, 1)
                g.wait_ge(eps_done, self.n0 + b + 1)
                g.tensor_tensor(rstd[:, u, :], rstd[:, u, :], K("minus_half"), ALU.pow).then_inc(rstd_done, 1)

            def dve_apply(self, v, b, u):
                wait(v, xT_raw, self.n0 + b)
                v.wait_ge(rstd_done, self.n0 + b + 1)
                for k in range(2):
                    ins = v.tensor_scalar(xs[:, u, k, :], self.tile(2 * b + k),
                                          mv[:, u, k, 0:1], rstd[:, u, k:k + 1], ALU.subtract, ALU.mult)
                if self.affine is None:
                    ins.then_inc(xn_done, 1)
                    return
                ins.then_inc(self.scaled, 1)
                g, c = (K(n).unsqueeze(1).to_broadcast([128, 2, D]) for n in self.affine)
                v.wait_ge(self.scaled, b + 1)
                v.tensor_tensor(xs[:, u, :, :], xs[:, u, :, :], g, ALU.mult).then_inc(self.shifted, 1)
                v.wait_ge(self.shifted, b + 1)
                v.tensor_tensor(xs[:, u, :, :], xs[:, u, :, :], c, ALU.add).then_inc(xn_done, 1)

            def pe_transpose(self, p, b, u, bank):
                p.wait_ge(xn_done, self.n0 + b + 1)
                for k in range(2):
                    ins = p.transpose(bank[:, 128 * k:128 * k + 128], xs[:, u, k, :], ident)
                ins.then_inc(xT_raw, 1)

            def act_xT(self, a, b, u, bank):
                a.wait_ge(xT_raw, self.n0 + b + 1)
                a.activation(xnT[:, bass.ds(b * TQ, TQ)], bank, ACT.Copy).then_inc(self.xT_done, 1)

            def pool_save(self, g, b, u):
                g.wait_ge(xn_done, self.n0 + b + 1)
                g.tensor_copy(self.keep[:, bass.ds(2 * b, 2), :], xs[:, u, :, :]).then_inc(self.saved, 1)

        S4 = [ps[:, 2 + 2 * g:4 + 2 * g, :] for g in range(2)]
        Y = ps[:, 1, 0:256]
        MT_RAW = ps[:, 0, 0:256]
        XT_RAW = ps[:, 1, 256:512]

        keys_r = sb("keys_r", [128, H, TQ], F32R)
        queries_r = sb("queries_r", [128, 2, 2, 4, TQ], F32R)
        kb = keys_r[:, :, :].rearrange("p h k -> p (h k)").rearrange("p (u a h k) -> p u a h k", u=2, a=2, h=H)
        k_split = big[:, 0:4096].rearrange("p (a t n) -> p a t n", a=2, t=4)
        q_raw = big[:, 4096:6144]
        q_upper = big[:, 6144:8192]
        v_all = big[:, 8192:8192 + B * C * 72].rearrange("p (b c n) -> p b c n", b=B, c=C)
        v_now = big[:, 12800:12800 + 2 * C * 72].rearrange("p (u c n) -> p u c n", u=2, c=C)
        acc = big[0:72, 13952:14976]
        weights = big[:, 14976:14976 + 1408]

        class XAttn:

            def __init__(self, layer, order, before, ln, pe_after=()):
                self.pe_after = pe_after
                parts = 2 if layer == 3 else 1
                self.L, self.parts, self.before, self.ln = layer, parts, before, ln
                self.n0 = B * [0, 2, 3][order]
                self.m0, self.q0 = B * order, order
                self.s = attn_signals
                self.CG = 4 // parts
                self.wq = weights[:, 0:512].rearrange("p (t n) -> p t n", t=4)
                self.wk = weights[:, 512:1024].rearrange("p (t n) -> p t n", t=4)
                self.wv = weights[:, 1024:1152]
                self.wo = [weights[:, 1152:1280], weights[:, 1280:1408]]
                self.scale = D ** -0.5 if parts == 2 else HD ** -0.5
                self.bv, self.bo = (K("fmb_row"), K("fcb")) if parts == 2 else (K(f"bv{layer}"), K(f"bo{layer}"))

            def sync_prepare(self, sp):
                for sm, value in self.pe_after:
                    sp.wait_ge(sm, value)
                sp.dma_start(weights, t[f"xw_{self.L}"]).then_inc(self.s.w_in, 16)

            def v_place(self, j, b0, cc, sg):
                groups = v_all[64 * j:64 * j + 64, b0:b0 + 4, :, :].rearrange("p b (g e) n -> p b g e n", e=self.CG)
                at = 16 * self.parts * cc + 16 * sg + 8 * j
                return groups[:, :, :, cc, at:at + 8]

            def v_raw(self, j, b0, cc):
                bank = ps[64 * j:64 * j + 64, 6 + b0 // 4, :].rearrange("p (b g e i d) -> p b g e i d", b=4, e=self.CG, i=2, d=HD)
                return bank[:, :, :, cc, j, :]

            def pe_prepare(self, p):
                s = self.s
                for sm, value in self.pe_after:
                    p.wait_ge(sm, value)
                p.wait_ge(s.w_in, 16 * self.q0 + 16)
                for t_ in range(4):
                    p.matmul(ps[:, 2 + t_, :], self.wk[:, t_, :], K("ctxT2")[:, :, 0, :], start=True, stop=True).then_inc(s.k_raw, 1)
                for b in range(B):
                    out = ps[:, 6 + b // 4, 128 * (b % 4):128 * (b % 4) + 128]
                    p.matmul(out, K("ctxT2")[:, b, :, :].rearrange("p j k -> p (j k)"), self.wv, start=True, stop=False)
                    ins = p.matmul(out, ones_row, self.bv, start=False, stop=True)
                ins.then_inc(s.v_raw, 1)

            def act_prepare(self, a):
                s, P = self.s, self.parts
                for part in range(P):
                    if part > 0:
                        a.wait_ge(s.k_split, self.q0 + part)
                    for t_ in range(4):
                        a.wait_ge(s.k_raw, 4 * self.q0 + t_ + 1)
                        dst = q_raw[:, 512 * t_:512 * t_ + 512]
                        if P == 1:
                            ins = a.activation(dst, ps[:, 2 + t_, :], ACT.Identity, bias=K(f"bk{self.L}")[:, t_:t_ + 1])
                        elif part == 0:
                            ins = a.activation(dst, ps[:, 2 + t_, :], ACT.Exp, bias=K("fmb"))
                        else:
                            ins = a.activation(dst, ps[:, 2 + t_, :], ACT.Exp, bias=nfmb[:, 0:1], scale=-1.0)
                    ins.then_inc(s.k_done, 1)
                if P == 2:
                    a.wait_ge(s.v_raw, self.q0 + 1)
                    a.wait_ge(s.v_zero, self.q0 + 1)
                    for j in range(2):
                        for b0 in (0, 4):
                            for cc in range(self.CG):
                                for sg in range(2):
                                    ins = a.activation(self.v_place(j, b0, cc, sg), self.v_raw(j, b0, cc), ACT.Exp, scale=1.0 - 2.0 * sg)
                    ins.then_inc(s.v_done, 1)

            def dve_prepare(self, v):
                s, P = self.s, self.parts
                v.wait_ge(s.v_zeroing, self.q0 + 1)
                for j in range(2):
                    for cc in range(self.CG):
                        groups = v_all[64 * j:64 * j + 64, :, :, :].rearrange("p b (g e) n -> p (b g) e n", e=self.CG)
                        ins = v.memset(groups[:, :, cc, 64 + 2 * cc + j:65 + 2 * cc + j], 1.0)
                ins.then_inc(s.v_zero, 1)
                for part in range(P):
                    v.wait_ge(s.k_done, self.q0 + part + 1)
                    v.tensor_scalar(q_upper.bitcast(I32), q_raw.bitcast(I32), -4096, K("split_sign")[:, 1:2].bitcast(I32),
                                    ALU.bitwise_and, ALU.bitwise_xor).then_inc(s.k_upper, 1)
                    v.wait_ge(s.k_upper, self.q0 + part + 1)
                    v.scalar_tensor_tensor(k_split[:, part, :, :].rearrange("p t n -> p (t n)"), q_raw, K("split_all")[:, 1:2], q_upper,
                                           ALU.mult, ALU.add).then_inc(s.k_split, 1)
                    v.wait_ge(s.k_split, self.q0 + part + 1)
                if P == 1:
                    v.wait_ge(s.v_zero, self.q0 + 1)
                    v.wait_ge(s.v_raw, self.q0 + 1)
                    for j in range(2):
                        for b0 in (0, 4):
                            for cc in range(self.CG):
                                ins = v.tensor_copy(self.v_place(j, b0, cc, 0), self.v_raw(j, b0, cc))
                    ins.then_inc(s.v_done, 1)

            def pool_prepare(self, g):
                if self.q0 > 0:
                    g.wait_ge(moe_signals.gT_done, self.q0 + 1)
                g.memset(v_all, 0.0).then_inc(self.s.v_zeroing, 1)

            def pe(self, p):
                s, P, CG = self.s, self.parts, self.CG
                p.wait_ge(s.v_done, self.q0 + 1)
                p.wait_ge(s.k_split, self.q0 + P)
                p.wait_ge(self.before.xT_done, B)

                def body(i, u, has):
                    w = 1 - u
                    if has(1):
                        b = i - 1
                        n = self.n0 + b
                        p.wait_ge(s.q_split, self.m0 + b + 1)
                        p.wait_ge(s.kb_done, self.m0 + P * b + P)
                        wait(p, s.mT_done, n)
                        wait(p, s.on_done, 2 * (self.m0 + b - 1))
                        for k in range(2):
                            if k == 1:
                                wait(p, s.p_done, 2 * n - 1)
                            for t_ in range(4):
                                for part in range(P):
                                    ins = p.matmul(ps[:, 2 * k + t_ // 2, 256 * (t_ % 2):256 * (t_ % 2) + 256],
                                                   queries_r[:, w, part, t_, 128 * k:128 * k + 128],
                                                   kb[:, w, part, 4 * t_:4 * t_ + 4, :].rearrange("p h k -> p (h k)"),
                                                   start=(part == 0), stop=(part == P - 1))
                            ins.then_inc(s.nat_done, 1)
                    if has(0):
                        for r in range(2):
                            wait(p, s.raw_done, 2 * (self.m0 + i) + r)
                            if r == 0:
                                wait(p, self.ln.x_done, i - 2)
                            for k in range(2):
                                ins = p.matmul(ps[:, 7, 256 * k:256 * k + 256], self.wq[:, 2 * r + k, :], xnT[:, bass.ds(i * TQ, TQ)],
                                               start=True, stop=True)
                            ins.then_inc(s.q_raw, 1)
                    if has(2):
                        b = i - 2
                        p.wait_ge(s.p_done, 2 * (self.n0 + b) + 2)
                        p.wait_ge(s.v_now_done, self.m0 + b + 1)
                        wait(p, s.on_done, 2 * (self.m0 + b))
                        for r in range(P):
                            wait(p, s.acc_out, self.m0 + P * b + r)
                            for c in range(r * 2 * CG, (r + 1) * 2 * CG):
                                g = c // CG
                                ins = p.matmul(ps[0:72, 6, 256 * (g % 2):256 * (g % 2) + 256], v_now[:, u, c, :], pT[:, u, c, :],
                                               start=(c % CG == 0), stop=(c % CG == CG - 1))
                            ins.then_inc(s.pv_done, 1)
                    if has(1):
                        p.wait_ge(s.max_done, 2 * n + 2)
                        for k in range(2):
                            ins = p.transpose(MT_RAW[:, 128 * k:128 * k + 128], nmax[:, w, k, :], ident)
                        ins.then_inc(s.mT_raw, 1)
                    if has(3):
                        if has(0):
                            p.wait_ge(s.raw_done, 2 * (self.m0 + i) + 2)
                        wait(p, self.ln.x_done, i - 2)
                        self.ln.pe_transpose(p, i - 3, w, ps[:, 7, 0:256])
                    if has(2):
                        b = i - 2
                        p.wait_ge(s.acc_out, self.m0 + P * b + P)
                        for k in range(2):
                            for g in range(2 * P):
                                ins = p.transpose(ps[:, (6, 1)[k], 72 * g:72 * g + 72], acc[:, 256 * g + 128 * k:256 * g + 128 * k + 128],
                                                  ident[0:72, 0:72])
                            ins.then_inc(s.o_done, 1)
                    for g in range(2):
                        if has(1):
                            if g == 0:
                                p.wait_ge(s.mT_done, n + 1)
                            wait(p, s.p_done, 2 * n - 1 + g)
                            for c in range(4 * g, 4 * g + 4):
                                out = S4[g][:, (c % 4) // 2, 256 * (c % 2):256 * (c % 2) + 256]
                                for part in range(P):
                                    p.matmul(out, kb[:, w, part, 2 * c:2 * c + 2, :].rearrange("p h k -> p (h k)"),
                                             queries_r[:, w, part, c // 2, :], start=(part == 0), stop=False)
                                ins = p.matmul(out, sel_r[:, c, :], nmaxT[:, w, :], start=False, stop=True)
                            ins.then_inc(s.s_done, 1)
                        if has(2) and g == 0:
                            p.wait_ge(s.on_done, 2 * (self.m0 + b) + 2)
                            if has(0):
                                p.wait_ge(s.raw_done, 2 * (self.m0 + i) + 2)
                            wait(p, self.ln.x_done, b)
                            if has(3):
                                p.wait_ge(self.ln.xT_done, i - 2)
                        if has(2) and g < P:
                            wait(p, s.oT_done, self.m0 + P * b + g)
                            for k in range(2):
                                ins = p.transpose(ps[:, 7, 128 * k:128 * k + 128], on[:, k, g, :], ident)
                            ins.then_inc(s.oT_raw, 1)
                    if has(2):
                        p.wait_ge(s.oT_done, self.m0 + P * b + P)
                        for k in range(2):
                            out = ps[:, 7, 256 + 128 * k:256 + 128 * k + 128]
                            for part in range(P):
                                p.matmul(out, oT[:, part, 128 * k:128 * k + 128], self.wo[part], start=(part == 0), stop=False)
                            ins = p.matmul(out, ones_row, self.bo, start=False, stop=True)
                        ins.then_inc(s.y_done, 1)
                pipelined(p, body, 3)

            def act(self, a):
                s, P = self.s, self.parts

                def body(i, u, has):
                    w = 1 - u
                    if has(0):
                        wait(a, s.q_split, self.m0 + i)
                        for r in range(2):
                            a.wait_ge(s.q_raw, 2 * (self.m0 + i) + r + 1)
                            if P == 1:
                                for k in range(2):
                                    ins = a.activation(q_raw[:, 512 * r + 256 * k:512 * r + 256 * k + 256], ps[:, 7, 256 * k:256 * k + 256],
                                                       ACT.Identity, bias=K(f"bq{self.L}")[:, 2 * r + k:2 * r + k + 1])
                            else:
                                a.activation(q_raw[:, 512 * r:512 * r + 512], ps[:, 7, :], ACT.Exp, bias=K("fmb"))
                                ins = a.activation(q_raw[:, 1024 + 512 * r:1536 + 512 * r], ps[:, 7, :], ACT.Exp, bias=nfmb[:, 0:1], scale=-1.0)
                            ins.then_inc(s.raw_done, 1)
                    if has(2):
                        b = i - 2
                        wait(a, s.o_done, 2 * (self.m0 + b))
                        for r in range(P):
                            a.wait_ge(s.pv_done, self.m0 + P * b + r + 1)
                            a.activation(acc[:, 512 * r:512 * r + 512], ps[0:72, 6, :], ACT.Copy).then_inc(s.acc_out, 1)
                    if has(1):
                        n = self.n0 + i - 1
                        a.wait_ge(s.mT_raw, n + 1)
                        a.activation(nmaxT[:, w, :], MT_RAW, ACT.Copy).then_inc(s.mT_done, 1)
                    if has(3):
                        self.ln.act_xT(a, i - 3, w, ps[:, 7, 0:256])
                    for g in range(2):
                        if has(1):
                            a.wait_ge(s.s_done, 2 * n + g + 1)
                            wait(a, s.pv_done, self.m0 + P * (i - 2))
                            a.activation(pT[:, w, 4 * g:4 * g + 4, :].rearrange("p c q -> p (c q)"),
                                         S4[g].rearrange("p a n -> p (a n)"), ACT.Exp, scale=self.scale).then_inc(s.p_done, 1)
                        if has(2) and g < P:
                            wait(a, s.y_done, self.n0 + b)
                            a.wait_ge(s.oT_raw, self.m0 + P * b + g + 1)
                            a.activation(oT[:, g, :], ps[:, 7, 0:256], ACT.Copy).then_inc(s.oT_done, 1)
                pipelined(a, body, 3)

            def dve(self, v):
                s, P, CG = self.s, self.parts, self.CG

                def body(i, u, has):
                    w = 1 - u
                    if has(3):
                        self.ln.dve_apply(v, i - 3, w)
                    if has(1):
                        n = self.n0 + i - 1
                        for k in range(2):
                            v.wait_ge(s.nat_done, 2 * n + k + 1)
                            v.tensor_reduce(nmax[:, w, k, 0:H], ps[:, 2 * k:2 * k + 2, :].rearrange("p a (h k) -> p (a h) k", k=TK),
                                            X_AXIS, ALU.max, negate=True).then_inc(s.max_done, 1)
                    if has(0):
                        m = self.m0 + i
                        v.wait_ge(s.raw_done, 2 * m + 2)
                        wait(v, s.q_split, m)
                        v.tensor_scalar(q_upper[:, 0:1024 * P].bitcast(I32), q_raw[:, 0:1024 * P].bitcast(I32), -4096,
                                        K("split_sign")[:, 0:1].bitcast(I32), ALU.bitwise_and, ALU.bitwise_xor).then_inc(s.q_upper, 1)
                        v.wait_ge(s.q_upper, m + 1)
                        wait(v, s.s_done, 2 * (self.n0 + i - 1))
                        v.scalar_tensor_tensor(queries_r[:, u, 0:P, :, :].rearrange("p a t q -> p (a t q)"), q_raw[:, 0:1024 * P],
                                               K("split_all")[:, 0:1], q_upper[:, 0:1024 * P], ALU.mult, ALU.add).then_inc(s.q_split, 1)
                    if has(2):
                        b = i - 2
                        m = self.m0 + b
                        for k in range(2):
                            v.wait_ge(s.o_done, 2 * m + k + 1)
                            wait(v, s.oT_raw, self.m0 + P * b)
                            o = ps[:, (6, 1)[k], 0:144 * P].rearrange("p (g n) -> p g n", n=72)
                            v.reciprocal(rsum[:, k, :].rearrange("p (g e) -> p g e", e=2 * CG), o[:, :, 64:64 + 2 * CG]).then_inc(s.rsum_done, 1)
                            v.wait_ge(s.rsum_done, 2 * m + k + 1)
                            for part in range(P):
                                for cc in range(CG):
                                    at = 16 * P * cc + 16 * part
                                    ins = v.tensor_tensor(
                                        on[:, k, part, :].rearrange("p (g c n) -> p g c n", c=CG, n=16)[:, :, cc, :].rearrange("p g (j d) -> p g j d", j=2),
                                        o[:, :, at:at + 16].rearrange("p g (j d) -> p g j d", j=2),
                                        rsum[:, k, :].rearrange("p (g c j) -> p g c j", c=CG, j=2)[:, :, cc, :].unsqueeze(3).to_broadcast([128, 2 * P, 2, HD]),
                                        ALU.mult)
                            ins.then_inc(s.on_done, 1)
                        v.wait_ge(s.y_done, self.n0 + b + 1)
                        tiles = x[:, bass.ds(2 * b, 2), :]
                        v.tensor_tensor(tiles, tiles, ps[:, 7, 256:512].rearrange("p (a d) -> p a d", a=2), ALU.add).then_inc(self.ln.x_done, 1)
                        v.wait_ge(self.ln.x_done, b + 1)
                        self.ln.dve_stats(v, b, u)
                pipelined(v, body, 3)

            def pool(self, g):
                s, P = self.s, self.parts

                def body(i, u, has):
                    if has(0):
                        if isinstance(i, int) and i == 0:
                            g.wait_ge(s.k_split, self.q0 + P)
                            g.wait_ge(s.v_done, self.q0 + 1)
                        wait(g, s.s_done, 2 * (self.n0 + i) - 2)
                        for part in range(P):
                            g.tensor_tensor(kb[:, u, part, :, :].rearrange("p (t h) k -> p t h k", t=4),
                                            k_split[:, part, :, bass.ds(i * TK, TK)].unsqueeze(2).to_broadcast([128, 4, 4, TK]),
                                            K("quad_mask").unsqueeze(1).unsqueeze(3).to_broadcast([128, 4, 4, TK]), ALU.mult).then_inc(s.kb_done, 1)
                    if has(1):
                        wait(g, s.pv_done, self.m0 + P * (i - 2))
                        g.tensor_copy(v_now[:, 1 - u, :, :], v_all[:, bass.ds(i - 1, 1), :, :].rearrange("p a c n -> p (a c) n")).then_inc(s.v_now_done, 1)
                    if has(2):
                        self.ln.pool_rstd(g, i - 2, u)
                    if has(3) and self.ln.keep is not None:
                        self.ln.pool_save(g, i - 3, 1 - u)
                pipelined(g, body, 3)

        nfmb = sb("nfmb", [128, 1])
        sel_r = sb("sel_r", [128, C, 128], F32R)
        identr = sb("identr", [128, 128], F32R)
        nf_done, identr_done = sem("nf_done"), sem("identr_done")
        beta_dram = nc.dram_tensor("beta_rows", (B, C, 128), F32).ap()
        parts_dram = nc.dram_tensor("beta_part_rows", (2, B, C * 128), F32).ap()

        kflat = kblk[:, :, :, :, :].rearrange("p u s h k -> p (u s h k)")
        vflat = big[:, 8192:10368]

        G = N // 512
        w1 = sb("w1", [128, 2, F + FC])
        w2 = sb("w2", [128, 2, FC, D])
        hT = big[:, 0:2 * F * FC].rearrange("p (u c n) -> p u c n", u=2, c=FC)
        gates = sb("gates", [128, NT, E])
        gatesT = sb("gatesT", [128, 128])
        b2blk = pT[:, 0, :, :].rearrange("p c q -> p (c q)").rearrange("p (t d) -> p t d", t=NT)
        res = kflat[:, 0:NT * D].rearrange("p (t d) -> p t d", t=NT)

        def tiles8(ap):
            return ap.rearrange("p (t e) -> p t e", e=E)

        def scratch(k, n=1):
            return vflat[:, 128 * k:128 * (k + n)]

        rt = {n: tiles8(scratch(k)) for k, n in enumerate(("val", "eq", "cand", "sel1", "sel2", "tmp"))}
        tot, scan = scratch(6, 2), scratch(8, 2)
        scT, gtm, eqm, cmp = (scratch(10 + k) for k in range(4))
        rc = {n: sb(f"rc_{n}", [128, NT]) for n in ("m1", "m2", "idx", "e2", "den", "p1", "p2")}
        thr, bit, cand_thr, okm = (sb(n, [128, 1], I32) for n in ("thr", "bit", "cand_thr", "okm"))
        cnt = sb("cnt", [128, 2])

        def bc(per_tile):
            return per_tile[:, :].unsqueeze(2).to_broadcast([128, NT, E])


        links = [0]

        class Moe:
            def __init__(self, layer, norm_before, gelu, dst):
                self.L, self.before, self.gelu, self.dst = layer, norm_before, gelu, dst
                self.s = moe_signals
                self.st0, self.r0 = layer * G * E, [0, 1, 3][layer]

            def pe_logits(self, p):
                p.wait_ge(self.before.xT_done, B)
                for t_ in range(NT):
                    ins = p.matmul(ps[:, 0, E * t_:E * t_ + E], xnT[:, 128 * t_:128 * t_ + 128], K(f"gate{self.L}"), start=True, stop=True)
                ins.then_inc(self.s.logits, 1)

            def link(self, ins):
                links[0] += 1
                ins.then_inc(self.s.chain, 1)
                return links[0]

            def probs(self, v):
                s = self.s
                after = lambda ins: v.wait_ge(s.chain, self.link(ins))
                v.wait_ge(s.logits, self.L + 1)
                lg = tiles8(ps[:, 0, 0:128])
                after(v.tensor_reduce(rc["m1"][:, :], lg, X_AXIS, ALU.max))
                v.tensor_tensor(rt["val"][:, :, :], lg, bc(rc["m1"]), ALU.subtract).then_inc(s.logits_read, 1)
                v.wait_ge(s.exp_out, self.r0 + 1)
                after(v.tensor_reduce(rc["den"][:, :], rt["tmp"][:, :, :], X_AXIS, ALU.add))
                after(v.reciprocal(rc["den"][:, :], rc["den"][:, :]))
                v.tensor_tensor(rt["val"][:, :, :], rt["tmp"][:, :, :], bc(rc["den"]), ALU.mult).then_inc(s.probs_done, 1)
                v.wait_ge(s.probs_done, self.L)

            def act_probs(self, a):
                a.wait_ge(self.s.logits_read, self.r0 + 1)
                a.activation(rt["tmp"][:, :, :], rt["val"][:, :, :], ACT.Exp).then_inc(self.s.exp_out, 1)

            def top2(self, v):
                s = self.s
                after = lambda ins: v.wait_ge(s.chain, self.link(ins))
                desc = K("descending").unsqueeze(1).to_broadcast([128, NT, E])
                for m, sel in (("m1", "sel1"), ("m2", "sel2")):
                    after(v.tensor_reduce(rc[m][:, :], rt["val"][:, :, :], X_AXIS, ALU.max))
                    after(v.tensor_tensor(rt["eq"][:, :, :], rt["val"][:, :, :], bc(rc[m]), ALU.is_equal))
                    after(v.tensor_tensor(rt["cand"][:, :, :], rt["eq"][:, :, :], desc, ALU.mult))
                    after(v.tensor_reduce(rc["idx"][:, :], rt["cand"][:, :, :], X_AXIS, ALU.max))
                    v.tensor_tensor(rt[sel][:, :, :], bc(rc["idx"]), desc, ALU.is_equal).then_inc(s.picked, 1)
                    v.wait_ge(s.picked, 2 * self.L + (1 if m == "m1" else 2))
                    if m == "m1":
                        after(v.scalar_tensor_tensor(rt["val"][:, :, :], rt[sel][:, :, :], -1e30, rt["val"][:, :, :], ALU.mult, ALU.add))
                v.tensor_tensor(rc["p2"][:, :], rc["m2"][:, :], rc["m1"][:, :], ALU.subtract).then_inc(s.logits_read, 1)

            def dve_logits(self, v):
                v.wait_ge(self.s.logits, self.L + 1)
                v.tensor_copy(rt["val"][:, :, :], tiles8(ps[:, 0, 0:128])).then_inc(self.s.chain, 1)
                links[0] += 1
                v.wait_ge(self.s.chain, links[0])

            def act_pair(self, a, n):
                a.wait_ge(self.s.logits_read, self.r0 + n)
                a.activation(rc["e2"][:, :], rc["p2"][:, :], ACT.Exp).then_inc(self.s.exp_out, 1)

            def pair_probs(self, v, n):
                after = lambda ins: v.wait_ge(self.s.chain, self.link(ins))
                v.wait_ge(self.s.exp_out, self.r0 + n)
                after(v.tensor_scalar(rc["den"][:, :], rc["e2"][:, :], 1.0, None, ALU.add))
                after(v.reciprocal(rc["p1"][:, :], rc["den"][:, :]))
                after(v.tensor_tensor(rc["p2"][:, :], rc["p1"][:, :], rc["e2"][:, :], ALU.mult))

            def combine(self, v):
                after = lambda ins: v.wait_ge(self.s.chain, self.link(ins))
                after(v.tensor_tensor(rt["eq"][:, :, :], rt["sel1"][:, :, :], bc(rc["p1"]), ALU.mult))
                after(v.tensor_tensor(rt["cand"][:, :, :], rt["sel2"][:, :, :], bc(rc["p2"]), ALU.mult))
                v.tensor_tensor(gates[:, :, :], rt["eq"][:, :, :], rt["cand"][:, :, :], ALU.add).then_inc(self.s.gates_done, 1)

            def pe_prefix(self, p):
                s = self.s
                p.wait_ge(s.picked, 2)
                for k, sel in enumerate(("sel1", "sel2")):
                    p.matmul(ps[:, 1, 128 * k:128 * k + 128], K("before"), rt[sel][:, :, :].rearrange("p t e -> p (t e)"), start=True, stop=True)
                    ins = p.matmul(ps[:, 2, 128 * k:128 * k + 128], K("all_ones"), rt[sel][:, :, :].rearrange("p t e -> p (t e)"), start=True, stop=True)
                ins.then_inc(s.prefix, 1)

            def capacity(self, v):
                s = self.s
                after = lambda ins: v.wait_ge(s.chain, self.link(ins))
                v.wait_ge(s.prefix, 1)
                after(v.tensor_copy(tot[:, :], ps[:, 2, 0:256]))
                for e in range(E):
                    ins = v.tensor_tensor_scan(scan[:, :].rearrange("p (k e) -> p k e", e=E)[:, :, e],
                                               K("all_ones")[:, 0:2 * NT],
                                               tot[:, :].rearrange("p (k e) -> p k e", e=E)[:, :, e],
                                               0.0, ALU.mult, ALU.add)
                    self.link(ins)
                v.wait_ge(s.chain, links[0])
                after(v.tensor_tensor(scan[:, :], scan[:, :], tot[:, :], ALU.subtract))
                after(v.tensor_tensor(scan[:, :], scan[:, :], ps[:, 1, 0:256], ALU.add))
                after(v.tensor_scalar(scan[:, :], scan[:, :], float(CAP0), None, ALU.is_lt))
                for k, sel in enumerate(("sel1", "sel2")):
                    after(v.tensor_tensor(rt[sel][:, :, :], rt[sel][:, :, :], tiles8(scan[:, 128 * k:128 * k + 128]), ALU.mult))

            def dve_threshold(self, v):
                s = self.s
                after = lambda ins: v.wait_ge(s.chain, self.link(ins))
                v.wait_ge(s.gT_raw, 3)
                after(v.tensor_copy(scT[:, :], ps[:, 3, 0:128]))
                after(v.memset(thr[:, :], 0))
                after(v.memset(bit[:, :], 1 << 29))
                with v.Fori(0, 30) as i:
                    v.tensor_tensor(cand_thr[:, :], thr[:, :], bit[:, :], ALU.bitwise_or).then_inc(s.cand_done, 1)
                    v.wait_ge(s.cand_done, i + 1)
                    v.tensor_scalar(cmp[:, :], scT[:, :], cand_thr[:, 0:1].bitcast(F32), None, ALU.is_ge, ALU.add, accum_out=cnt[:, 0:1]).then_inc(s.counted, 1)
                    v.wait_ge(s.summed, i + 1)
                    v.tensor_scalar(okm[:, :], ps[:, 4, 0:1], float(TOP2), -1.0, ALU.is_ge, ALU.mult).then_inc(s.ok_done, 1)
                    v.wait_ge(s.ok_done, i + 1)
                    v.scalar_tensor_tensor(thr[:, :], bit[:, :], okm[:, 0:1], thr[:, :], ALU.bitwise_and, ALU.bitwise_or).then_inc(s.thr_done, 1)
                    v.wait_ge(s.thr_done, i + 1)
                    v.tensor_scalar(bit[:, :], bit[:, :], 1, None, ALU.logical_shift_right).then_inc(s.bit_done, 1)
                    v.wait_ge(s.bit_done, i + 1)
                t_f = thr[:, 0:1].bitcast(F32)
                after(v.tensor_scalar(gtm[:, :], scT[:, :], t_f, None, ALU.is_gt, ALU.add, accum_out=cnt[:, 0:1]))
                v.tensor_scalar(eqm[:, :], scT[:, :], t_f, None, ALU.is_equal, ALU.add, accum_out=cnt[:, 1:2]).then_inc(s.ties_counted, 1)
                v.wait_ge(s.ties_counted, 1)
                after(v.tensor_tensor_scan(cmp[:, :], K("all_ones"), eqm[:, :], 0.0, ALU.mult, ALU.add))
                after(v.tensor_tensor(cmp[:, :], cmp[:, :], eqm[:, :], ALU.subtract))
                v.wait_ge(s.prefix, 2)
                after(v.tensor_copy(cnt[:, 0:2], ps[:, 4, 1:3]))
                after(v.tensor_tensor(cnt[:, 0:1], cnt[:, 0:1], cnt[:, 1:2], ALU.add))
                after(v.tensor_scalar(cnt[:, 0:1], cnt[:, 0:1], -1.0, float(TOP2), ALU.mult, ALU.add))
                after(v.tensor_scalar(cmp[:, :], cmp[:, :], cnt[:, 0:1], None, ALU.is_lt))
                after(v.tensor_tensor(cmp[:, :], cmp[:, :], eqm[:, :], ALU.mult))
                after(v.tensor_tensor(cmp[:, :], cmp[:, :], gtm[:, :], ALU.add))
                v.tensor_tensor(gatesT[:, :], cmp[:, :], scT[:, :], ALU.mult).then_inc(s.gT_done, 1)

            def pe_threshold(self, p):
                s = self.s
                p.wait_ge(s.probs_done, self.L)
                p.transpose(ps[:, 3, 0:128], rt["val"][:, :, :].rearrange("p t e -> p (t e)"), ident).then_inc(s.gT_raw, 1)
                with p.Fori(0, 30) as i:
                    p.wait_ge(s.counted, i + 1)
                    p.matmul(ps[:, 4, 0:1], K("same_expert"), cnt[:, 0:1], start=True, stop=True).then_inc(s.summed, 1)
                p.wait_ge(s.ties_counted, 1)
                p.matmul(ps[:, 4, 1:2], K("same_expert"), cnt[:, 0:1], start=True, stop=True)
                p.matmul(ps[:, 4, 2:3], K("earlier_tile"), cnt[:, 1:2], start=True, stop=True).then_inc(s.prefix, 1)

            def pool_b2(self, g):
                g.tensor_tensor(b2blk[:, :, :], K(f"b2_{self.L}").unsqueeze(1).to_broadcast([128, NT, D]),
                                K("tile_mask").unsqueeze(2).to_broadcast([128, NT, D]), ALU.mult).then_inc(self.s.b2_done, 1)

            def pe_init(self, p):
                s = self.s
                if self.L != 2:
                    p.wait_ge(s.gates_done, self.L + 1)
                    p.transpose(ps[:, 3, 0:128], gates[:, :, :].rearrange("p t e -> p (t e)"), ident).then_inc(s.gT_raw, 1)
                p.wait_ge(s.gT_done, self.L + 1)
                if self.L == 2:
                    p.transpose(ps[:, 3, 0:128], gatesT[:, :], ident).then_inc(s.gT_raw, 1)
                p.wait_ge(s.b2_done, self.L + 1)
                for k in range(4):
                    p.matmul(ps[:, 4 + k, :], gatesT[:, :], b2blk[:, 4 * k:4 * k + 4, :].rearrange("p t d -> p (t d)"), start=True, stop=True).then_inc(s.b2_raw, 1)

            def dve_init(self, v):
                s = self.s
                if self.L != 2:
                    v.wait_ge(s.gT_raw, self.L + 1)
                    v.tensor_copy(gatesT[:, :], ps[:, 3, 0:128]).then_inc(s.gT_done, 1)
                else:
                    v.wait_ge(s.gT_raw, 4)
                    v.tensor_copy(gates[:, :, :].rearrange("p t e -> p (t e)"), ps[:, 3, 0:128]).then_inc(s.gates_done, 1)
                if self.before.keep is not None:
                    v.wait_ge(self.before.saved, B)
                for k in range(4):
                    v.wait_ge(s.b2_raw, 4 * self.L + k + 1)
                    tiles = self.dst[:, 4 * k:4 * k + 4, :].rearrange("p t d -> p (t d)")
                    v.tensor_tensor(tiles, tiles, ps[:, 4 + k, :], ALU.add).then_inc(s.init_done, 1)
                if self.L == 2:
                    v.wait_ge(s.init_done, 4 * self.L + 4)
                    v.tensor_tensor(x[:, :, :], x[:, :, :], xn[:, :, :], ALU.add).then_inc(s.init_done, 1)
                v.wait_ge(s.init_done, 4 * self.L + (5 if self.L == 2 else 4))
                v.wait_ge(s.gates_done, self.L + 1)

            def experts(self, eng, body):
                for e in range(2):
                    body(e, e, 0)
                with eng.Fori(1, E // 2) as pair:
                    body(2 * pair, 0, pair)
                    body(2 * pair + 1, 1, pair)

            def sync(self, sp):
                s = self.s

                def body(e, u, pair):
                    for ww, src, landed in ((w1, t[f"w1_{self.L}"], (s.w1_in0, s.w1_in1)), (w2, t[f"w2_{self.L}"], (s.w2_in0, s.w2_in1))):
                        wait(sp, s.fc2_done, self.st0 + G * (e - 1))
                        dst = ww[:, u, :] if ww is w1 else ww[:, u, :, :].rearrange("p c d -> p (c d)")
                        sp.dma_start(dst, src[bass.ds(e, 1), :, :].rearrange("a p n -> (a p) n")).then_inc(landed[u], 16)
                self.experts(sp, body)

            def fc2(self, p, step, u, parity):
                s = self.s
                p.wait_ge(s.gelu_done, FC * step + FC)
                wait(p, s.acc_done, 4 * (step - 1))
                for k in range(4):
                    for c in range(FC):
                        ins = p.matmul(ps[:, 4 + parity, 128 * k:128 * k + 128], hT[:, parity, c, 128 * k:128 * k + 128],
                                       w2[:, u, c, :], start=(c == 0), stop=(c == FC - 1))
                ins.then_inc(s.fc2_done, 1)

            def pe(self, p):
                s = self.s
                p.wait_ge(s.init_done, 4 * self.L + 4)
                if self.L == 2:
                    p.wait_ge(ln_g.xT_done, B)

                def body(e, u, pair):
                    for g in range(G):
                        step = self.st0 + G * e + g
                        if g == 0:
                            p.wait_ge((s.w1_in0, s.w1_in1)[u], 16 * (self.L * (E // 2) + pair) + 16)
                        for c in range(FC):
                            wait(p, s.gelu_done, FC * (step - 1) + c + 1)
                            p.matmul(ps[:, c, :], w1[:, u, 128 * c:128 * c + 128], xnT[:, 512 * g:512 * g + 512], start=True, stop=True).then_inc(
                                s.fc1_chunk, 1)
                        if g == 0:
                            if not (isinstance(e, int) and e == 0):
                                self.fc2(p, step - 1, 1 - u, 1)
                            p.wait_ge((s.w2_in0, s.w2_in1)[u], 16 * (self.L * (E // 2) + pair) + 16)
                        else:
                            self.fc2(p, step - 1, u, (g - 1) % 2)
                self.experts(p, body)
                self.fc2(p, self.st0 + G * E - 1, 1, 1)

            def act(self, a):
                s = self.s

                def body(e, u, pair):
                    for g in range(G):
                        step = self.st0 + G * e + g
                        wait(a, s.fc2_done, step - 1)
                        for c in range(FC):
                            a.wait_ge(s.fc1_chunk, FC * step + c + 1)
                            a.activation(hT[:, g % 2, c, :], ps[:, c, :], self.gelu, bias=w1[:, u, F + c:F + c + 1]).then_inc(s.gelu_done, 1)
                self.experts(a, body)

            def dve(self, v):
                s = self.s

                def body(e, u, pair):
                    for g in range(G):
                        step = self.st0 + G * e + g
                        v.wait_ge(s.fc2_done, step + 1)
                        for k in range(4):
                            tile = self.dst[:, 4 * g + k, :]
                            v.scalar_tensor_tensor(tile, ps[:, 4 + g % 2, 128 * k:128 * k + 128],
                                                   gates[:, 4 * g + k, bass.ds(e, 1)], tile, ALU.mult, ALU.add).then_inc(s.acc_done, 1)
                self.experts(v, body)

        class NormPhase:

            def __init__(self, norm, add_to=None, pe_after=(), act_after=(), dve_after=()):
                self.n, self.add_to = norm, add_to
                self.pe_after, self.act_after, self.dve_after = pe_after, act_after, dve_after

            def pe(self, p):
                for sm, value in self.pe_after:
                    p.wait_ge(sm, value)

                def body(i, u, has):
                    if has(2):
                        wait(p, self.n.xT_done, i - 2)
                        self.n.pe_transpose(p, i - 2, u, XT_RAW)
                if self.add_to is None:
                    pipelined(p, body, 3)

            def act(self, a):
                for sm, value in self.act_after:
                    a.wait_ge(sm, value)

                def body(i, u, has):
                    if has(2):
                        self.n.act_xT(a, i - 2, u, XT_RAW)
                if self.add_to is None:
                    pipelined(a, body)

            def dve(self, v):
                for sm, value in self.dve_after:
                    v.wait_ge(sm, value)

                def body(i, u, has):
                    if has(0):
                        self.n.dve_stats(v, i, u)
                    if has(1):
                        b = i - 1
                        self.n.dve_apply(v, b, 1 - u)
                        if self.add_to is not None:
                            v.wait_ge(xn_done, self.n.n0 + b + 1)
                            tiles = self.add_to[:, bass.ds(2 * b, 2), :]
                            v.tensor_tensor(tiles, tiles, xs[:, 1 - u, :, :], ALU.add).then_inc(xT_raw, 1)
                pipelined(v, body)

            def pool(self, g):
                def body(i, u, has):
                    if has(0):
                        self.n.pool_rstd(g, i, u)
                pipelined(g, body)

        A1 = big[:, 0:B * C * 128].rearrange("p (b c n) -> p b c n", b=B, c=C)
        VW = big[:, B * C * 128:2 * B * C * 128].rearrange("p (b c n) -> p b c n", b=B, c=C)
        wide_w = pT[:, :, :, :].rearrange("p u c q -> p (u c q)").rearrange("p (w n) -> p w n", w=4)
        khead = kflat[:, 0:4 * B * TK].rearrange("p (v b j k) -> p v b j k", v=2, b=B, j=2)
        keep = on[:, :, :, :].rearrange("p k a d -> p (k a d)")
        mask8 = sb("mask8", [128, B * TK], mybir.dt.uint8)
        drop = kflat[0:1, 3072:4096].rearrange("p (b j k) -> p b j k", b=B, j=2)
        beta = kflat[0:1, 2048:3072].rearrange("p (b n) -> p b n", b=B)
        beta_in = kblk[0:2, :, 1, :, :].rearrange("p u h k -> p u (h k)")
        beta_r = keys_r[:, 0:8, :].rearrange("p h k -> p (h k)").rearrange("p (u n) -> p u n", u=2)
        ones_r = queries_r[:, 0, 0, 0, :]
        beta_flat, beta_parts = kT[:, 1, 0:64], kT[:, 1, 64:192].rearrange("p (a n) -> p a n", a=2)
        xb = kT[:, 0, :].rearrange("p (u q) -> p u q", u=2)
        rec, rec_upper = kT[0:48, 1, 0:256], kT[0:48, 1, 256:512]
        rsT = sb("rsT", [128, TQ], F32R)

        class Wide:
            def __init__(self, before, ln):
                self.before, self.ln = before, ln
                self.s = WideSignals()
                self.n0 = B

            def sync_prepare(self, sp):
                s = self.s
                sp.dma_start(wide_w[:, :, :], t["wide_w"]).then_inc(s.w_in, 16)
                sp.dma_start(mask8[:, :], t["mask"].partition_broadcast(128).rearrange("a b n -> a (b n)")).then_inc(s.mask_in, 16)
                for c in range(C):
                    sp.wait_ge(s.beta_done, c + 1)
                    sp.dma_start(beta_dram[:, c, :], beta[:, :, :]).then_inc(s.beta_out, 16)

            def pe_prepare(self, p):
                s = self.s
                p.wait_ge(s.w_in, 16)
                for c in range(C):
                    col = slice(128 * c, 128 * c + 128)
                    if c >= 1:
                        p.wait_ge(s.kv_done, 2 * c)
                    p.matmul(ps[:, 2, :], wide_w[:, 1, col], K("ctxT2")[:, :, 0, :], start=True, stop=True)
                    p.matmul(ps[:, 3, :], wide_w[:, 2, col], K("ctxT2")[:, :, 0, :], start=True, stop=True).then_inc(s.kv_raw, 1)
                    p.wait_ge(s.kv_masked, c + 1)
                    p.wait_ge(s.kv_done, 2 * c + 2)
                    if c >= 1:
                        p.wait_ge(s.A_done, 2 * c)
                        p.wait_ge(s.beta_done, c)
                        p.wait_ge(s.VW_done, 2 * c)
                    for n in range(2):
                        keys = khead[:, 0, 4 * n:4 * n + 4, :, :].rearrange("p b j k -> p (b j k)")
                        p.matmul(ps[:, 4 + n, :], wide_w[:, 0, col], keys, start=True, stop=True).then_inc(s.A_raw, 1)
                    for n in range(2):
                        keys = khead[:, 0, 4 * n:4 * n + 4, :, :].rearrange("p b j k -> p (b j k)")
                        ins = p.matmul(ps[0:1, n, :], K("bq1")[:, c:c + 1], keys, start=True, stop=True)
                    ins.then_inc(s.beta_raw, 1)
                    for b in range(B):
                        ins = p.matmul(ps[:, 6 + b // 4, 128 * (b % 4):128 * (b % 4) + 128], khead[:, 1, b, :, :].rearrange("p j k -> p (j k)"),
                                       wide_w[:, 3, col], start=True, stop=True)
                    ins.then_inc(s.VW_raw, 1)

            def act_prepare(self, a):
                s = self.s
                a.wait_ge(s.zero, 1)
                for c in range(C):
                    a.wait_ge(s.kv_raw, c + 1)
                    if c >= 1:
                        a.wait_ge(s.VW_raw, c)
                    for kind in range(2):
                        bias = K("bk1" if kind == 0 else "bv1")
                        for j in range(2):
                            rows = slice(64 * j, 64 * j + 64)
                            ins = a.activation(khead[rows, kind, :, j, :], ps[rows, 2 + kind, :].rearrange("p (b k) -> p b k", b=B),
                                               ACT.Identity, bias=bias[rows, c:c + 1])
                        ins.then_inc(s.kv_done, 1)
                    for n in range(2):
                        a.wait_ge(s.A_raw, 2 * c + n + 1)
                        a.activation(A1[:, 4 * n:4 * n + 4, c, :], ps[:, 4 + n, :].rearrange("p (b n) -> p b n", b=4), ACT.Copy).then_inc(s.A_done, 1)

            def dve_prepare(self, v):
                s = self.s
                v.wait_ge(m0.s.fc2_done, 1 * G * E)
                v.memset(khead[:, :, :, :, :], 0.0).then_inc(s.zero, 1)
                v.tensor_scalar(rsT[:, :], K("row0_ones"), 0.0, None, ALU.mult).then_inc(s.keep_done, 1)
                v.tensor_copy(ones_r, K("rows01_ones")).then_inc(s.keep_done, 1)
                v.tensor_scalar(beta_r, K("row0_ones")[:, 0:1].unsqueeze(2).to_broadcast([128, 2, C * 128]), 0.0, None, ALU.mult).then_inc(s.keep_done, 1)
                v.wait_ge(s.mask_in, 16)
                v.tensor_copy(keep[:, :], mask8[:, :]).then_inc(s.keep_done, 1)
                v.wait_ge(s.keep_done, 4)
                for j in range(2):
                    v.tensor_scalar(drop[:, :, j, :], keep[0:1, :].rearrange("p (b k) -> p b k", b=B), -1e9, None, ALU.mult).then_inc(s.keep_done, 1)
                v.wait_ge(s.keep_done, 6)
                v.tensor_scalar(keep[:, :], keep[:, :], -(HD1 ** -0.5), HD1 ** -0.5, ALU.mult, ALU.add).then_inc(s.keep_done, 1)
                v.wait_ge(s.keep_done, 7)
                for c in range(C):
                    v.wait_ge(s.kv_done, 2 * c + 1)
                    for j in range(2):
                        rows = slice(64 * j, 64 * j + 64)
                        ins = v.tensor_tensor(khead[rows, 0, :, j, :], khead[rows, 0, :, j, :], keep[rows, :].rearrange("p (b k) -> p b k", b=B), ALU.mult)
                    ins.then_inc(s.kv_masked, 1)
                    v.wait_ge(s.beta_raw, c + 1)
                    if c >= 1:
                        v.wait_ge(s.beta_out, 16 * c)
                    v.tensor_tensor(beta[:, :, :].rearrange("p (n b) k -> p n (b k)", n=2), ps[0:1, 0:2, :],
                                    drop[:, :, :, :].rearrange("p (n b) j k -> p n (b j k)", n=2), ALU.add).then_inc(s.beta_done, 1)
                    v.wait_ge(s.VW_raw, c + 1)
                    for n in range(2):
                        v.tensor_copy(VW[:, 4 * n:4 * n + 4, c, :], ps[:, 6 + n, :].rearrange("p (b n) -> p b n", b=4)).then_inc(s.VW_done, 1)
                v.wait_ge(s.beta_back, 16)
                v.tensor_scalar(beta_parts[:, 0, :].bitcast(I32), beta_flat.bitcast(I32), -4096, None, ALU.bitwise_and).then_inc(s.part_done, 1)
                v.wait_ge(s.part_done, 1)
                v.tensor_tensor(beta_parts[:, 1, :], beta_flat, beta_parts[:, 0, :], ALU.subtract).then_inc(s.part_done, 1)

            def sync(self, sp):
                s = self.s
                sp.wait_ge(s.beta_out, 16 * C)
                sp.dma_start(beta_flat, beta_dram.rearrange("b c n -> (b c n)").rearrange("(p n) -> p n", p=128)).then_inc(s.beta_back, 16)
                sp.wait_ge(s.part_done, 2)
                sp.dma_start(parts_dram.rearrange("a b n -> a (b n)").rearrange("a (p n) -> p a n", p=128), beta_parts).then_inc(s.parts_out, 16)
                sp.wait_ge(s.parts_out, 16)

                def body(b, u):
                    wait(sp, s.beta_r_done, b - 1)
                    sp.dma_start(beta_in[:, u, :], parts_dram[:, bass.ds(b, 1), :].rearrange("p a n -> p (a n)")).then_inc((s.beta_in0, s.beta_in1)[u], 16)
                for b in range(2):
                    body(b, b)
                with sp.Fori(1, B // 2) as pair:
                    body(2 * pair, 0)
                    body(2 * pair + 1, 1)

            def pe(self, p):
                s = self.s
                p.wait_ge(s.VW_done, 2 * C)
                p.wait_ge(self.before.xT_done, B)
                p.wait_ge(s.A_done, 2 * C)

                def body(i, u, has):
                    w = 1 - u
                    n = self.n0 + i
                    if has(0):
                        p.wait_ge(s.xb_done, i + 1)
                        wait(p, s.mT_done, n)
                        wait(p, self.ln.x_done, i - 2)
                        wait(p, self.ln.xT_done, i - 3)
                        for k in range(2):
                            if k == 1:
                                wait(p, s.p_done, 2 * n - 1)
                            for half in range(2):
                                out = ps[:, 2 * k + half, :]
                                p.matmul(out, xb[:, u, 128 * k:128 * k + 128],
                                         A1[:, bass.ds(i, 1), 4 * half:4 * half + 4, :].rearrange("p a c n -> p (a c n)"), start=True, stop=False)
                                ins = p.matmul(out, ones_r[:, 0:128], beta_r[:, u, 512 * half:512 * half + 512], start=False, stop=True)
                            ins.then_inc(s.nat_done, 1)
                    if has(2):
                        b = i - 2
                        if has(0):
                            p.wait_ge(s.max_done, 2 * n + 1)
                        else:
                            p.wait_ge(self.ln.x_done, i - 2)
                            p.wait_ge(self.ln.xT_done, i - 3)
                        p.wait_ge(s.pn_done, 4 * b + 4)
                        for k in range(2):
                            out = Y[:, 128 * k:128 * k + 128]
                            for c in range(C):
                                p.matmul(out, pT[:, u, c, 128 * k:128 * k + 128],
                                         VW[:, bass.ds(b, 1), c, :].rearrange("p a n -> p (a n)"), start=(c == 0), stop=False)
                            ins = p.matmul(out, ones_row, K("bo1"), start=False, stop=True)
                        ins.then_inc(s.y_done, 1)
                    if has(1):
                        b = i - 1
                        p.wait_ge(s.p_done, 2 * (self.n0 + b) + 2)
                        wait(p, s.pn_done, 4 * b)
                        for c in range(C):
                            ins = p.matmul(ps[0:48, 6, 0:256], K("pair_rows")[:, 14 - 2 * c:62 - 2 * c], pT[:, w, c, :],
                                           start=(c == 0), stop=(c == C - 1))
                        ins.then_inc(s.sum_done, 1)
                    if has(0):
                        p.wait_ge(s.max_done, 2 * n + 2)
                        for k in range(2):
                            ins = p.transpose(MT_RAW[:, 128 * k:128 * k + 128], nmax[:, u, k, :], ident)
                        ins.then_inc(s.mT_raw, 1)
                    if has(3):
                        wait(p, self.ln.x_done, i - 1 if has(2) else i - 2)
                        wait(p, self.ln.xT_done, i - 3)
                        self.ln.pe_transpose(p, i - 3, w, XT_RAW)
                    if has(0):
                        for g in range(2):
                            wait(p, s.p_done, 2 * n - 1 + g)
                            p.wait_ge(s.mT_done, n + 1)
                            for c in range(4 * g, 4 * g + 4):
                                out = S4[g][:, (c % 4) // 2, 256 * (c % 2):256 * (c % 2) + 256]
                                p.matmul(out, Ab[:, u, c, :], xb[:, u, :], start=True, stop=False)
                                p.matmul(out, beta_r[:, u, 128 * c:128 * c + 128], ones_r, start=False, stop=False)
                                ins = p.matmul(out, sel_r[:, c, :], nmaxT[:, u, :], start=False, stop=True)
                            ins.then_inc(s.s_done, 1)
                    if has(1):
                        b = i - 1
                        p.wait_ge(s.rs_done, b + 1)
                        for r in range(4):
                            if r >= 2:
                                p.wait_ge(s.pn_done, 4 * b + r - 1)
                            for c in (2 * r, 2 * r + 1):
                                ins = p.matmul(ps[:, 6 + r % 2, 256 * (c % 2):256 * (c % 2) + 256], sel_r[:, c, :], rsT[:, :], start=True, stop=True)
                            ins.then_inc(s.r_raw, 1)
                pipelined(p, body, 3)

            def act(self, a):
                s = self.s

                def body(i, u, has):
                    n = self.n0 + i
                    if has(0):
                        a.wait_ge(s.mT_raw, n + 1)
                        a.activation(nmaxT[:, u, :], MT_RAW, ACT.Copy).then_inc(s.mT_done, 1)
                    if has(3):
                        self.ln.act_xT(a, i - 3, 1 - u, XT_RAW)
                    if has(0):
                        for g in range(2):
                            a.wait_ge(s.s_done, 2 * n + g + 1)
                            wait(a, s.y_done, n - 1)
                            a.activation(pT[:, u, 4 * g:4 * g + 4, :].rearrange("p c q -> p (c q)"),
                                         S4[g].rearrange("p a n -> p (a n)"), ACT.Exp).then_inc(s.p_done, 1)
                pipelined(a, body, 3)

            def dve(self, v):
                s = self.s

                def body(i, u, has):
                    n = self.n0 + i
                    if has(3):
                        self.ln.dve_apply(v, i - 3, 1 - u)
                    if has(0):
                        for k in range(2):
                            v.wait_ge(s.nat_done, 2 * n + k + 1)
                            v.tensor_reduce(nmax[:, u, k, 0:H], ps[:, 2 * k:2 * k + 2, :].rearrange("p a (h k) -> p (a h) k", k=TK),
                                            X_AXIS, ALU.max, negate=True).then_inc(s.max_done, 1)
                    if has(2):
                        b = i - 2
                        v.wait_ge(s.y_done, self.n0 + b + 1)
                        tiles = x[:, bass.ds(2 * b, 2), :]
                        v.tensor_tensor(tiles, tiles, Y.rearrange("p (a d) -> p a d", a=2), ALU.add).then_inc(self.ln.x_done, 1)
                        v.wait_ge(self.ln.x_done, b + 1)
                        self.ln.dve_stats(v, b, u)
                    if has(1):
                        b = i - 1
                        v.wait_ge(s.sum_done, b + 1)
                        wait(v, s.rs_done, b)
                        v.reciprocal(rec, ps[0:48, 6, 0:256]).then_inc(s.rec_done, 1)
                        v.wait_ge(s.rec_done, b + 1)
                        v.tensor_scalar(rec_upper.bitcast(I32), rec.bitcast(I32), -4096, K("rec_sign")[0:48, :].bitcast(I32),
                                        ALU.bitwise_and, ALU.bitwise_xor).then_inc(s.upper_done, 1)
                        v.wait_ge(s.upper_done, b + 1)
                        v.scalar_tensor_tensor(rsT[0:48, :], rec, K("rec_all")[0:48, :], rec_upper, ALU.mult, ALU.add).then_inc(s.rs_done, 1)
                        for r in range(4):
                            v.wait_ge(s.r_raw, 4 * b + r + 1)
                            part = pT[:, 1 - u, 2 * r:2 * r + 2, :].rearrange("p c q -> p (c q)")
                            v.tensor_tensor(part, part, ps[:, 6 + r % 2, :], ALU.mult).then_inc(s.pn_done, 1)
                pipelined(v, body, 3)

            def pool(self, g):
                s = self.s

                def body(i, u, has, pair):
                    n = self.n0 + i
                    if has(0):
                        g.wait_ge(self.before.xT_done, i + 1)
                        wait(g, s.s_done, 2 * n - 2)
                        if isinstance(i, int) and i == 0:
                            g.wait_ge(s.A_done, 2 * C)
                            g.wait_ge(s.VW_done, 2 * C)
                            g.wait_ge(s.VW_raw, C)
                            g.wait_ge(s.beta_out, 16 * C)
                        g.tensor_copy(Ab[:, u, :, :], A1[:, bass.ds(i, 1), :, :].rearrange("p a c n -> p (a c) n"))
                        g.tensor_copy(xb[:, u, :], xnT[:, bass.ds(i * TQ, TQ)])
                        g.wait_ge((s.beta_in0, s.beta_in1)[u], 16 * pair + 16)
                        g.sem_inc(passed_pool, 1)
                        g.tensor_copy(beta_r[0:2, u, :], beta_in[:, u, :]).then_inc(s.beta_r_done, 1)
                        g.wait_ge(s.beta_r_done, i + 1)
                        g.sem_inc(s.xb_done, 1)
                    if has(2):
                        self.ln.pool_rstd(g, i - 2, u)
                    if has(3):
                        self.ln.pool_save(g, i - 3, 1 - u)
                for i in range(4):
                    body(i, i % 2, lambda lag, i=i: 0 <= i - lag < B, i // 2)
                with g.Fori(2, B // 2) as pair:
                    body(2 * pair, 0, lambda lag: True, pair)
                    body(2 * pair + 1, 1, lambda lag: True, pair)
                for i in range(B, B + 3):
                    body(i, i % 2, lambda lag, i=i: 0 <= i - lag < B, 0)

        Ab = kblk[:, :, 0, :, :].rearrange("p u h k -> p u (h k)").rearrange("p u (c n) -> p u c n", c=C)

        SK = TQ
        NG = H // 2
        skblk = keys_r
        spT = [big[:, at:at + 1024].rearrange("p (h c q) -> p h c q", h=2, c=2) for at in (0, 1024, 12800, 13824)]
        raw = big[:, 2048:4096]
        kp = big[:, 4096:5120]
        upper = big[:, 5120:6144]
        sq = queries_r[:, :, 0, :, :]
        values = big[:, 6144:6144 + 8 * 720].rearrange("p (u c e n) -> p u c e n", u=2, c=2, e=2)
        self_acc = big[0:72, 12288:12800]

        class SelfAttn:
            def __init__(self, before, ln):
                self.before, self.ln = before, ln
                self.s = SelfSignals()

            def pe(self, p):
                s = self.s

                def pv(b, w, g):
                    p.wait_ge(s.p_done, NG * b + g + 1)
                    for j in range(2):
                        h = 2 * g + j
                        for c in range(2):
                            ins = p.matmul(ps[0:72, 6, 256 * (h // 8):256 * (h // 8) + 256],
                                           values[:, w, c, h // 8, 72 * (h % 8):72 * (h % 8) + 72], spT[g % 4][:, j, c, :],
                                           start=(h % 8 == 0 and c == 0), stop=(h % 8 == 7 and c == 1))
                    ins.then_inc(s.pv_done, 1)

                def bank7(i, u, has, slot):
                    if slot < 4 and has(0):
                        if slot == 0:
                            p.wait_ge(s.xb_done, i + 1)
                            wait(p, s.v_done, i)
                            wait(p, self.ln.x_done, i - 2)
                        else:
                            p.wait_ge(s.raw_done, 4 * i + slot)
                        w = K("sqp" if slot < 2 else "skp")
                        for n in range(2):
                            ins = p.matmul(ps[:, 7, 256 * n:256 * n + 256], w[:, 2 * (slot % 2) + n, :], xb[:, u, :], start=True, stop=True)
                        ins.then_inc(s.qk_raw, 1)
                    if slot == 4 and has(0):
                        p.wait_ge(s.raw_done, 4 * i + 4)
                        for k in range(2):
                            ins = p.matmul(ps[:, 7, 128 * k:128 * k + 128], xb[:, u, 128 * k:128 * k + 128], K("swv"), start=True, stop=True)
                        ins.then_inc(s.v_raw, 1)
                    if slot == 5 and has(3):
                        if has(0):
                            p.wait_ge(s.v_done, i + 1)
                        else:
                            p.wait_ge(s.v_done, B)
                            p.wait_ge(self.ln.x_done, i - 2)
                        self.ln.pe_transpose(p, i - 3, 1 - u, ps[:, 7, 0:256])
                    if slot == 6 and has(2):
                        if has(3):
                            p.wait_ge(self.ln.xT_done, i - 2)
                        else:
                            p.wait_ge(s.v_done, i + 1)
                        p.wait_ge(s.on_done, 2 * (i - 1))
                        for k in range(2):
                            ins = p.transpose(ps[:, 7, 128 * k:128 * k + 128], on[:, k, 0, :], ident)
                        ins.then_inc(s.oT_raw, 1)
                    if slot == 7 and has(2):
                        p.wait_ge(s.oT_done, i - 1)
                        for k in range(2):
                            out = ps[:, 7, 256 + 128 * k:256 + 128 * k + 128]
                            p.matmul(out, oT[:, 0, 128 * k:128 * k + 128], K("swo"), start=True, stop=False)
                            ins = p.matmul(out, ones_row, K("sbo"), start=False, stop=True)
                        ins.then_inc(s.y_done, 1)

                def body(i, u, has):
                    b, w = i - 1, 1 - u
                    if has(1):
                        wait(p, s.mT_done, b)
                    for g in range(NG):
                        if has(1):
                            p.wait_ge(s.kblk_done, 4 * b + g // 2 + 1)
                            for k in range(2):
                                wait(p, s.max_done, 2 * (NG * b + g) + k - 1)
                                p.matmul(ps[:, k, :], sq[:, w, g // 2, 128 * k:128 * k + 128],
                                         skblk[:, 2 * g:2 * g + 2, :].rearrange("p h k -> p (h k)"),
                                         start=True, stop=True).then_inc(s.nat_done, 1)
                        bank7(i, u, has, g)
                        if g < 3 and has(2):
                            pv(i - 2, u, NG - 3 + g)
                        if g == 4 and has(2):
                            p.wait_ge(s.acc_out, i - 1)
                            for k in range(2):
                                for e in range(2):
                                    ins = p.transpose(ps[:, 6, 144 * k + 72 * e:144 * k + 72 * e + 72],
                                                      self_acc[:, 256 * e + 128 * k:256 * e + 128 * k + 128], ident[0:72, 0:72])
                            ins.then_inc(s.o_done, 1)
                    if has(1):
                        p.wait_ge(s.max_done, 2 * NG * b + 2 * NG)
                        for k in range(2):
                            ins = p.transpose(MT_RAW[:, 128 * k:128 * k + 128], nmax[:, w, k, :], ident)
                        ins.then_inc(s.mT_raw, 1)
                        for g in range(NG):
                            wait(p, s.p_done, NG * b + g - 1)
                            if g == 0:
                                p.wait_ge(s.mT_done, b + 1)
                            for j in range(2):
                                h = 2 * g + j
                                bank = ps[:, 2 + 2 * (g % 2) + j, :]
                                p.matmul(bank.rearrange("p (c q) -> p c q", c=2), identr[:, h:h + 1].to_broadcast([128, 128]),
                                         nmaxT[:, w, :].unsqueeze(1).to_broadcast([128, 2, TQ]), start=True, stop=False)
                                for c in range(2):
                                    ins = p.matmul(bank[:, 256 * c:256 * c + 256], skblk[:, h, 128 * c:128 * c + 128],
                                                   sq[:, w, h // 4, :], start=False, stop=(c == 1))
                            ins.then_inc(s.s_done, 1)
                            if g == 3:
                                wait(p, s.on_done, 2 * b)
                            if g >= 3:
                                pv(b, w, g - 3)
                pipelined(p, body, 3)

            def act(self, a):
                s = self.s

                def body(i, u, has):
                    if has(0):
                        for r in range(4):
                            a.wait_ge(s.qk_raw, 4 * i + r + 1)
                            wait(a, s.split_done, 2 * (i - 1) + 1 + r // 2)
                            a.activation(raw[:, 512 * r:512 * r + 512], ps[:, 7, :], ACT.Copy).then_inc(s.raw_done, 1)
                        a.wait_ge(s.v_raw, i + 1)
                        a.wait_ge(s.ones, 2)
                        wait(a, s.pv_done, NG * (i - 1))
                        for c in range(2):
                            ins = a.activation(values[:, u, c, :, 0:640].rearrange("p e (j n) -> p e j n", j=8)[:, :, :, 0:8],
                                               ps[:, 7, 128 * c:128 * c + 128].rearrange("p (e j d) -> p e j d", e=2, j=8), ACT.Copy)
                        ins.then_inc(s.v_done, 1)
                    if has(2):
                        a.wait_ge(s.pv_done, NG * (i - 1))
                        wait(a, s.o_done, i - 2)
                        a.activation(self_acc, ps[0:72, 6, :], ACT.Copy).then_inc(s.acc_out, 1)
                    if has(3):
                        self.ln.act_xT(a, i - 3, 1 - u, ps[:, 7, 0:256])
                    if has(2):
                        a.wait_ge(s.oT_raw, i - 1)
                        wait(a, s.y_done, i - 2)
                        a.activation(oT[:, 0, :], ps[:, 7, 0:256], ACT.Copy).then_inc(s.oT_done, 1)
                    if has(1):
                        b = i - 1
                        a.wait_ge(s.mT_raw, b + 1)
                        a.activation(nmaxT[:, 1 - u, :], MT_RAW, ACT.Copy).then_inc(s.mT_done, 1)
                        for g in range(NG):
                            a.wait_ge(s.s_done, NG * b + g + 1)
                            wait(a, s.pv_done, NG * b + g - 3)
                            a.activation(spT[g % 4].rearrange("p h c q -> p (h c q)"),
                                         ps[:, 2 + 2 * (g % 2):4 + 2 * (g % 2), :].rearrange("p a n -> p (a n)"), ACT.Exp,
                                         scale=HD ** -0.5).then_inc(s.p_done, 1)
                pipelined(a, body, 3)

            def dve_split(self, v, i, half, out):
                s = self.s
                both = raw[:, 1024 * half:1024 * half + 1024]
                v.wait_ge(s.raw_done, 4 * i + 2 * half + 2)
                wait(v, s.split_done, 2 * i + half)
                v.tensor_scalar(upper.bitcast(I32), both.bitcast(I32), -4096, K("split_sign")[:, half:half + 1].bitcast(I32),
                                ALU.bitwise_and, ALU.bitwise_xor).then_inc(s.upper_done, 1)
                v.wait_ge(s.upper_done, 2 * i + half + 1)
                v.scalar_tensor_tensor(out, both, K("split_all")[:, half:half + 1], upper, ALU.mult, ALU.add).then_inc(s.split_done, 1)

            def dve(self, v):
                s = self.s
                v.memset(values, 0.0).then_inc(s.ones, 1)
                v.wait_ge(s.ones, 1)
                v.memset(values[:, :, :, :, 64:648].rearrange("p u c e (j n) -> p (u c e) j n", j=8)[:, :, :, 0:1], 1.0).then_inc(s.ones, 1)

                def body(i, u, has):
                    if has(3):
                        self.ln.dve_apply(v, i - 3, 1 - u)
                    for g in range(NG):
                        if has(1):
                            for k in range(2):
                                v.wait_ge(s.nat_done, 2 * (NG * (i - 1) + g) + k + 1)
                                v.tensor_reduce(nmax[:, 1 - u, k, 2 * g:2 * g + 2], ps[:, k, :].rearrange("p (h k) -> p h k", h=2),
                                                X_AXIS, ALU.max, negate=True).then_inc(s.max_done, 1)
                        if g == 1 and has(0):
                            wait(v, s.s_done, NG * (i - 1))
                            self.dve_split(v, i, 0, sq[:, u, :, :].rearrange("p t q -> p (t q)"))
                        if g == 3 and has(0):
                            wait(v, s.kblk_done, 4 * i)
                            self.dve_split(v, i, 1, kp)
                        if g == 6 and has(2):
                            b = i - 2
                            v.wait_ge(s.o_done, b + 1)
                            wait(v, s.oT_raw, b)
                            for k in range(2):
                                o = ps[:, 6, 144 * k:144 * k + 144].rearrange("p (e n) -> p e n", e=2)
                                v.reciprocal(rsum[:, k, :].rearrange("p (e j) -> p e j", e=2), o[:, :, 64:72]).then_inc(s.rsum_done, 1)
                                v.wait_ge(s.rsum_done, 2 * b + k + 1)
                                v.tensor_tensor(on[:, k, 0, :].rearrange("p (e j d) -> p e j d", e=2, j=8),
                                                o[:, :, 0:64].rearrange("p e (j d) -> p e j d", j=8),
                                                rsum[:, k, :].rearrange("p (e j) -> p e j", e=2).unsqueeze(3).to_broadcast([128, 2, 8, HD]),
                                                ALU.mult).then_inc(s.on_done, 1)
                    if has(2):
                        b = i - 2
                        v.wait_ge(s.y_done, b + 1)
                        v.tensor_tensor(res[:, bass.ds(2 * b, 2), :], xn[:, bass.ds(2 * b, 2), :],
                                        ps[:, 7, 256:512].rearrange("p (a d) -> p a d", a=2), ALU.add).then_inc(self.ln.x_done, 1)
                        v.wait_ge(self.ln.x_done, b + 1)
                        self.ln.dve_stats(v, b, u)
                pipelined(v, body, 3)

            def pool(self, g):
                s = self.s

                def body(i, u, has):
                    if has(0):
                        g.wait_ge(self.before.xT_done, i + 1)
                        wait(g, s.v_raw, i - 1)
                        g.tensor_copy(xb[:, u, :], xnT[:, bass.ds(i * TQ, TQ)]).then_inc(s.xb_done, 1)
                        g.wait_ge(s.split_done, 2 * i + 2)
                        for t_ in range(4):
                            wait(g, s.s_done, NG * (i - 1) + 2 * t_ + 2)
                            g.tensor_tensor(skblk[:, 4 * t_:4 * t_ + 4, :], kp[:, SK * t_:SK * t_ + SK].unsqueeze(1).to_broadcast([128, 4, SK]),
                                            K("quad_mask").unsqueeze(2).to_broadcast([128, 4, SK]), ALU.mult).then_inc(s.kblk_done, 1)
                    if has(2):
                        self.ln.pool_rstd(g, i - 2, u)
                    if has(3):
                        self.ln.pool_save(g, i - 3, 1 - u)
                pipelined(g, body, 3)

        wq3 = sb("wq3", [128, D])
        tern = sb("tern", [128, 4])
        yT3 = big[:, 0:2 * TQ].rearrange("p (u q) -> p u q", u=2)

        class Ternary:
            def __init__(self, before):
                self.before = before
                self.s = TernarySignals()

            def dve_prepare(self, v):
                s = self.s
                v.tensor_reduce(tern[:, 0:1], K("w3"), X_AXIS, ALU.add, apply_absolute_value=True).then_inc(s.abs_done, 1)
                v.wait_ge(s.sum_done, 1)
                v.tensor_scalar(tern[:, 1:2], ps[:, 3, 0:1], 1.0 / (D * D), 0.7, ALU.mult, ALU.mult).then_inc(s.chain, 1)
                v.wait_ge(s.chain, 1)
                v.tensor_scalar(tern[:, 2:3], tern[:, 1:2], -1.0, None, ALU.mult).then_inc(s.chain, 1)
                v.tensor_scalar(wq3[:, :], K("w3"), tern[:, 1:2], None, ALU.is_gt).then_inc(s.chain, 1)
                v.wait_ge(s.chain, 3)
                v.tensor_scalar(b2blk[:, 0, :], K("w3"), tern[:, 2:3], None, ALU.is_lt).then_inc(s.chain, 1)
                v.wait_ge(s.chain, 4)
                v.tensor_tensor(wq3[:, :], wq3[:, :], b2blk[:, 0, :], ALU.subtract).then_inc(s.chain, 1)
                v.wait_ge(s.chain, 5)
                v.tensor_scalar(wq3[:, :], wq3[:, :], K("alpha"), None, ALU.mult).then_inc(s.w_done, 1)

            def pe_prepare(self, p):
                s = self.s
                p.wait_ge(s.abs_done, 1)
                p.matmul(ps[:, 3, 0:1], K("all_ones"), tern[:, 0:1], start=True, stop=True).then_inc(s.sum_done, 1)

            def pe(self, p):
                s = self.s
                p.wait_ge(s.w_done, 1)

                def body(i, u, has):
                    if has(0):
                        p.wait_ge(self.before.xT_done, i + 1)
                        wait(p, s.o_done, i - 1)
                        p.matmul(ps[:, 2 + u, 0:256], wq3[:, :], xnT[:, bass.ds(i * TQ, TQ)], start=True, stop=True).then_inc(s.o_raw, 1)
                    if has(1):
                        p.wait_ge(s.o_done, i)
                        wait(p, s.x_done, i - 1)
                        for k in range(2):
                            ins = p.transpose(ps[:, 4, 128 * k:128 * k + 128], yT3[:, 1 - u, 128 * k:128 * k + 128], ident)
                        ins.then_inc(s.t_done, 1)
                pipelined(p, body)

            def act(self, a):
                s = self.s

                def body(i, u, has):
                    if has(0):
                        a.wait_ge(s.o_raw, i + 1)
                        wait(a, s.t_done, i - 1)
                        a.activation(yT3[:, u, :], ps[:, 2 + u, 0:256], ACT.Identity, bias=K("b3")).then_inc(s.o_done, 1)
                pipelined(a, body)

            def dve(self, v):
                s = self.s

                def body(i, u, has):
                    if has(1):
                        v.wait_ge(s.t_done, i)
                        tiles = x[:, bass.ds(2 * (i - 1), 2), :]
                        v.tensor_tensor(tiles, tiles, ps[:, 4, 0:256].rearrange("p (a d) -> p a d", a=2), ALU.add).then_inc(s.x_done, 1)
                pipelined(v, body)

            def sync(self, sp):
                s = self.s
                for b in range(B):
                    sp.wait_ge(s.x_done, b + 1)
                    sp.dma_start(t["out"][:, 2 * b:2 * b + 2, :], x[:, 2 * b:2 * b + 2, :]).then_inc(s.out_done, 16)
                sp.wait_ge(s.out_done, 16 * B)

        ln0 = Norm("ln0", x, 1e-5, residual=False)
        first = NormPhase(ln0)
        ln_a = Norm("ln_after_x0", x, 1e-5)
        a0 = XAttn(0, 0, ln0, ln_a)
        m0 = Moe(0, ln_a, ACT.Gelu, x)
        ln_b = Norm("ln_after_m0", x, 1e-5, residual=False)
        nb = NormPhase(ln_b, dve_after=[(m0.s.acc_done, 1 * 4 * G * E)], pe_after=[(m0.s.gelu_done, 1 * FC * G * E)])
        ln_c = Norm("ln_after_wide", x, 1e-5, keep=xn)
        wide = Wide(ln_b, ln_c)
        ln_d = Norm("ln1", res, 1e-6, affine=("ln1_g", "ln1_b"), keep=res)
        selfa = SelfAttn(ln_c, ln_d)
        m1 = Moe(1, ln_d, ACT.Gelu, res)
        ln_e = Norm("ln2", res, 1e-6, affine=("ln2_g", "ln2_b"), residual=False)
        ne = NormPhase(ln_e, add_to=x, dve_after=[(m1.s.acc_done, 2 * 4 * G * E)])
        ln_f = Norm("ln_after_m1", x, 1e-5, residual=False)
        nf = NormPhase(ln_f, dve_after=[(xT_raw, ln_e.n0 + B)], pe_after=[(m1.s.gelu_done, 2 * FC * G * E)])
        a2 = XAttn(2, 1, ln_f, Norm("ln_after_x2", x, 1e-5, keep=xn), [(m1.s.gelu_done, 2 * FC * G * E), (m1.s.acc_done, 2 * 4 * G * E)])
        ln_g = Norm("ln_inner", xn, 1e-5, affine=("lnw", "lnb"), residual=False)
        m2 = Moe(2, a2.ln, ACT.Gelu_apprx_tanh, x)
        ng = NormPhase(ln_g, pe_after=[(a2.ln.xT_done, B)], act_after=[(m2.s.logits, 3)], dve_after=[(a2.ln.saved, B)])
        ln_h = Norm("ln_after_m2", x, 1e-5, residual=False)
        nh = NormPhase(ln_h, dve_after=[(m2.s.acc_done, 3 * 4 * G * E)], pe_after=[(m2.s.gelu_done, 3 * FC * G * E)])
        a3 = XAttn(3, 2, ln_h, Norm("ln_after_x3", x, 1e-5), [(m2.s.gelu_done, 3 * FC * G * E), (m2.s.acc_done, 3 * 4 * G * E)])
        fin = Ternary(a3.ln)

        block = ctx.enter_context(nc.Block())

        @block.sync
        def _(sp):
            a0.sync_prepare(sp)
            sp.dma_start(cw[:, 0:cols.first], t["cols"][:, 0:cols.first]).then_inc(in_cw, 16)
            sp.dma_start(x[:, :, :], t["x"]).then_inc(in_x, 16)
            sp.dma_start(pT[:, 0, 0:4, :].rearrange("p c q -> p (c q)"), t["head_sel"]).then_inc(in_sel, 16)
            sp.dma_start(cw[:, cols.first:cols.width], t["cols"][:, cols.first:cols.width]).then_inc(in_rest, 16)
            m0.sync(sp)
            sp.wait_ge(m0.s.b2_raw, 4)
            sp.wait_ge(m0.s.acc_done, 1 * 4 * G * E)
            wide.sync_prepare(sp)
            wide.sync(sp)
            sp.wait_ge(m0.s.fc2_done, 1 * G * E)
            m1.sync(sp)
            a2.sync_prepare(sp)
            m2.sync(sp)
            a3.sync_prepare(sp)
            fin.sync(sp)

        @block.vector
        def _(v):
            v.wait_ge(in_cw, 16)
            v.memset(nmax[:, :, :, :], 0.0).then_inc(nf_done, 1)
            v.wait_ge(nf_done, 1)
            v.tensor_scalar(nfmb[:, 0:1], K("fmb"), -1.0, None, ALU.mult).then_inc(nf_done, 1)
            v.wait_ge(in_x, 16)
            a0.dve_prepare(v)
            first.dve(v)
            a0.dve(v)
            v.wait_ge(in_rest, 16)
            m0.dve_logits(v)
            m0.top2(v)
            m0.capacity(v)
            m0.pair_probs(v, 1)
            m0.combine(v)
            m0.dve_init(v)
            m0.dve(v)
            wide.dve_prepare(v)
            nb.dve(v)
            wide.dve(v)
            selfa.dve(v)
            m1.probs(v)
            m1.top2(v)
            m1.pair_probs(v, 2)
            m1.combine(v)
            m1.dve_init(v)
            m1.dve(v)
            ne.dve(v)
            a2.dve_prepare(v)
            nf.dve(v)
            a2.dve(v)
            m2.probs(v)
            ng.dve(v)
            m2.dve_threshold(v)
            m2.dve_init(v)
            m2.dve(v)
            a3.dve_prepare(v)
            nh.dve(v)
            a3.dve(v)
            fin.dve_prepare(v)
            fin.dve(v)

        @block.tensor
        def _(p):
            p.wait_ge(in_cw, 16)
            a0.pe_prepare(p)
            p.wait_ge(identr_done, 2)
            first.pe(p)
            a0.pe(p)
            p.wait_ge(in_rest, 16)
            m0.pe_logits(p)
            m0.pe_prefix(p)
            m0.pe_init(p)
            m0.pe(p)
            wide.pe_prepare(p)
            nb.pe(p)
            wide.pe(p)
            selfa.pe(p)
            m1.pe_logits(p)
            m1.pe_init(p)
            m1.pe(p)
            a2.pe_prepare(p)
            nf.pe(p)
            a2.pe(p)
            m2.pe_logits(p)
            ng.pe(p)
            m2.pe_threshold(p)
            m2.pe_init(p)
            m2.pe(p)
            a3.pe_prepare(p)
            nh.pe(p)
            a3.pe(p)
            fin.pe_prepare(p)
            fin.pe(p)

        @block.scalar
        def _(a):
            a.wait_ge(in_cw, 16)
            a.activation(identr[:, :], ident, ACT.Copy).then_inc(identr_done, 1)
            a.wait_ge(in_sel, 16)
            a.activation(sel_r[:, :, :].rearrange("p c n -> p (c n)"), pT[:, 0, 0:4, :].rearrange("p c q -> p (c q)"), ACT.Copy).then_inc(identr_done, 1)
            a0.act_prepare(a)
            first.act(a)
            a0.act(a)
            a.wait_ge(in_rest, 16)
            m0.act_pair(a, 1)
            m0.act(a)
            wide.act_prepare(a)
            nb.act(a)
            wide.act(a)
            selfa.act(a)
            m1.act_probs(a)
            m1.act_pair(a, 2)
            m1.act(a)
            a2.act_prepare(a)
            nf.act(a)
            a2.act(a)
            m2.act_probs(a)
            ng.act(a)
            m2.act(a)
            a3.act_prepare(a)
            nh.act(a)
            a3.act(a)
            fin.act(a)

        @block.gpsimd
        def _(g):
            a0.pool_prepare(g)
            g.wait_ge(in_cw, 16)
            first.pool(g)
            a0.pool(g)
            g.wait_ge(a0.s.y_done, B)
            g.wait_ge(in_rest, 16)
            m0.pool_b2(g)
            nb.pool(g)
            wide.pool(g)
            g.wait_ge(wide.s.y_done, 2 * B)
            m1.pool_b2(g)
            selfa.pool(g)
            a2.pool_prepare(g)
            ne.pool(g)
            nf.pool(g)
            a2.pool(g)
            g.wait_ge(a2.s.y_done, 3 * B)
            m2.pool_b2(g)
            ng.pool(g)
            a3.pool_prepare(g)
            nh.pool(g)
            a3.pool(g)


def kernel(**inputs):
    import concourse.bacc as bacc
    from concourse.bass_utils import run_bass_kernel_spmd as run

    a = {k: np.ascontiguousarray(v) for k, v in inputs.items()}
    cols = packs()
    cp = np.zeros((128, cols.width), np.float32)

    def put(pack, arr, name, value):
        off, shape = pack.at[name]
        n = int(np.prod(shape))
        v = np.asarray(value).reshape(value.shape[0], n)
        arr[0:v.shape[0], off:off + n] = v

    d = np.arange(128)
    put(cols, cp, "ident", np.eye(128, dtype=np.float32))
    row = d[:, None, None]
    head_sel = ((row < 48) & (row // 16 != 1) & (row % 16 == 2 * np.arange(C)[None, :, None] + (d // TK)[None, None, :])).astype(np.float32)
    put(cols, cp, "minus_half", np.full((128, 2), -0.5, np.float32))
    ctxT = a["ctx_1024"].transpose(2, 0, 1)
    put(cols, cp, "ctxT2", np.stack([ctxT, ctxT], axis=2))
    def four_times(w):
        return np.tile(w.reshape(-1, 4, 32), (1, 1, 4))

    for L, w in ((0, "L0_xattn"), (2, "L2_xattn")):
        put(cols, cp, f"bq{L}", four_times(a[f"{w}_bq"][None])[0].T)
    put(cols, cp, "bk0", four_times(a["L0_xattn_bk"][None])[0].T)
    put(cols, cp, "bk2", four_times(a["L2_xattn_bkv"][0::2][None])[0].T)
    fm = np.zeros((128, 128), np.float32)
    for h in range(H):
        fm[HD * h:HD * h + HD, HD * h:HD * h + HD] = a["L3_xattn_fm_w"].T
    put(cols, cp, "fmb", np.tile(a["L3_xattn_fm_b"], H)[:, None])

    def x_weights(wq, wk, wv, wo):
        packed = np.concatenate([four_times(wq).reshape(D, 512), four_times(wk).reshape(D, 512), wv, wo], axis=1)
        return np.pad(packed, ((0, 0), (0, 1408 - packed.shape[1])))

    fcw = a["L3_xattn_fc_w"].reshape(D, H, 2, HD).transpose(1, 3, 2, 0).reshape(128, 2 * D)
    put(cols, cp, "row0_ones", np.ones((1, TQ), np.float32))
    put(cols, cp, "rows01_ones", np.ones((2, TQ), np.float32))
    put(cols, cp, "bv0", a["L0_xattn_bv"][None])
    put(cols, cp, "bo0", a["L0_xattn_bo"][None])
    put(cols, cp, "bv2", a["L2_xattn_bkv"][1::2][None])
    put(cols, cp, "bo2", a["L2_xattn_bout"][None])
    put(cols, cp, "fmb_row", np.tile(a["L3_xattn_fm_b"], H)[None])
    put(cols, cp, "fcb", a["L3_xattn_fc_b"][None])
    put(cols, cp, "gate0", a["L0_ffn_gate_w"])
    put(cols, cp, "gate1", a["L1_ffn_Wr"])
    put(cols, cp, "gate2", a["L2_ffn_gate_w"].T)
    b2 = [a["L0_ffn_proj_bias"].reshape(E, D), a["L1_ffn_be2"], a["L2_ffn_b2s"]]
    for L in range(3):
        put(cols, cp, f"b2_{L}", np.tile(b2[L], (NT, 1)))
    put(cols, cp, "tile_mask", (d[:, None] // E == np.arange(NT)[None]).astype(np.float32))
    put(cols, cp, "descending", np.tile(np.arange(E, 0, -1, dtype=np.float32), (128, 1)))
    put(cols, cp, "before", (d[:, None] < d[None]).astype(np.float32))
    put(cols, cp, "all_ones", np.ones((128, 128), np.float32))
    put(cols, cp, "same_expert", (d[:, None] % E == d[None] % E).astype(np.float32))
    put(cols, cp, "earlier_tile", ((d[:, None] % E == d[None] % E) & (d[:, None] // E < d[None] // E)).astype(np.float32))
    put(cols, cp, "sqp", four_times(a["L1_ffn_Wq"]))
    put(cols, cp, "skp", four_times(a["L1_ffn_Wk"]))
    put(cols, cp, "swv", a["L1_ffn_Wv"])
    put(cols, cp, "swo", a["L1_ffn_Wo"])
    lower = np.stack([d // 64 == 1, d // 32 % 2 == 1], axis=1)
    put(cols, cp, "split_sign", np.where(lower, np.float32(-0.0), np.float32(0.0)))
    put(cols, cp, "split_all", lower.astype(np.float32))
    put(cols, cp, "quad_mask", (d[:, None] % 32 // HD == np.arange(4)[None]).astype(np.float32))
    put(cols, cp, "sbo", a["L1_ffn_bo"][None])
    for n in ("ln1_g", "ln1_b", "ln2_g", "ln2_b"):
        put(cols, cp, n, np.tile(a[f"L1_ffn_{n}"][None], (128, 1)))
    put(cols, cp, "lnw", np.tile(a["L2_ffn_ln_w"][None], (128, 1)))
    put(cols, cp, "lnb", np.tile(a["L2_ffn_ln_b"][None], (128, 1)))
    for n in ("bq", "bk", "bv"):
        put(cols, cp, n + "1", a[f"L1_xattn_{n}"].reshape(C, 128).T)
    put(cols, cp, "bo1", a["L1_xattn_bo"][None])
    at = np.arange(62)
    put(cols, cp, "pair_rows", ((at % 16 >= 14)[None] & (d[:, None] // TK == (at % 16 - 14)[None])).astype(np.float32))
    third = (d[:, None] // 16 == 2)
    put(cols, cp, "rec_sign", np.where(third, np.float32(-0.0), np.float32(0.0)))
    put(cols, cp, "rec_all", third.astype(np.float32))
    put(cols, cp, "w3", a["L3_ffn_weight"].T)
    put(cols, cp, "alpha", np.tile(a["L3_ffn_alpha"][None], (128, 1)))
    put(cols, cp, "b3", a["L3_ffn_bias"][:, None])
    by_rows = lambda w: w.reshape(C, 128, D).transpose(1, 0, 2).reshape(128, C * D)
    wide_w = np.stack([by_rows(a["L1_xattn_Wq"]), a["L1_xattn_Wk"].T, a["L1_xattn_Wv"].T, by_rows(a["L1_xattn_Wo"].T)], axis=1)

    def first_weights(w, b):
        return np.concatenate([w, b.reshape(E, FC, 128).transpose(0, 2, 1)], axis=2)

    def second_weights(w):
        return w.reshape(E, FC, 128, D).transpose(0, 2, 1, 3).reshape(E, 128, F)

    arrays = {"wide_w": wide_w, "head_sel": head_sel.reshape(128, C * 128),
              "xw_0": x_weights(a["L0_xattn_Wq"].T, a["L0_xattn_Wk"].T, a["L0_xattn_Wv"].T, a["L0_xattn_Wo"].T),
              "xw_2": x_weights(a["L2_xattn_Wq"], a["L2_xattn_Wkv"][:, 0::2], a["L2_xattn_Wkv"][:, 1::2], a["L2_xattn_Wout"]),
              "xw_3": x_weights(fm, fm, fm, fcw),
              "mask": a["mask_BxS2_bk0"].reshape(1, B * TK),
              "w1_0": first_weights(a["L0_ffn_c_fc"], a["L0_ffn_fc_bias"].reshape(E, F)), "w2_0": second_weights(a["L0_ffn_c_proj"]),
              "w1_1": first_weights(a["L1_ffn_We1"], a["L1_ffn_be1"]), "w2_1": second_weights(a["L1_ffn_We2"]),
              "w1_2": first_weights(a["L2_ffn_fc1s"].transpose(0, 2, 1), a["L2_ffn_b1s"]),
              "w2_2": second_weights(a["L2_ffn_fc2s"].transpose(0, 2, 1)),
              "cols": cp, "x": np.ascontiguousarray(a["x"].reshape(NT, 128, D).transpose(1, 0, 2))}

    arrays = {k: np.ascontiguousarray(v) for k, v in arrays.items()}
    nc = bacc.Bacc("TRN2", target_bir_lowering=False, num_devices=1)
    t = {k: nc.dram_tensor(f"in_{k}", v.shape, mybir.dt.from_np(v.dtype), kind="ExternalInput").ap() for k, v in arrays.items()}
    t["out"] = nc.dram_tensor("out_x", (128, NT, D), F32, kind="ExternalOutput").ap()
    build(nc, t)
    got = run(nc, [{f"in_{k}": v for k, v in arrays.items()}], core_ids=[0]).results[0]["out_x"]
    return np.ascontiguousarray(got.transpose(1, 0, 2)).reshape(B, TQ, D)
```
